# Optimizing a Trainium2 kernel written in Bass

```python
import numpy as np
import jax
import jax.numpy as jnp

def _softmax(x, axis=-1):
    return jax.nn.softmax(x, axis=axis)

def _gelu(x):
    return jax.nn.gelu(x, approximate=True)

def _silu(x):
    return jax.nn.silu(x)

def _sigmoid(x):
    return jax.nn.sigmoid(x)

def _layernorm(x, axis=-1, eps=1e-05):
    m = jnp.mean(x, axis=axis, keepdims=True)
    v = jnp.var(x, axis=axis, keepdims=True)
    return (x - m) / jnp.sqrt(v + eps)

def _scatter_add(tgt, idx, src, axis=0):
    return tgt.at[idx].add(src)

def _segment_sum(src, seg, n):
    return jax.ops.segment_sum(src, seg, n)
kernel_name = 'mk_conv_seq_d2_conv_nchw96_r2_b770cd'

def setup_inputs(seed: int=0):
    np.random.seed(seed)
    _w = jnp.asarray

    def _rec_inputs():
        import jax
        import jax.numpy as jnp
        _gk = jax.random.key(seed)
        x = -0.0002221 + 1 * jax.random.normal(jax.random.fold_in(_gk, 1), (4, 48, 128, 128), jnp.float32)
        return x
    x = _rec_inputs()

    def _L0_conv_setup():
        import jax, jax.numpy as jnp
        import numpy as np
        WS = 8
        NH = 4
        DIM = 48
        HID = 4 * DIM
        EPS = 1e-05

        def _rel_pos_index(ws):
            coords = np.stack(np.meshgrid(np.arange(ws), np.arange(ws), indexing='ij'))
            cf = coords.reshape(2, -1)
            rel = cf[:, :, None] - cf[:, None, :]
            rel = rel.transpose(1, 2, 0).astype(np.int64)
            rel[:, :, 0] += ws - 1
            rel[:, :, 1] += ws - 1
            rel[:, :, 0] *= 2 * ws - 1
            return jnp.asarray(rel.sum(-1), dtype=jnp.int32)

        def _layernorm(x, g, b):
            m = x.mean(-1, keepdims=True)
            v = ((x - m) ** 2).mean(-1, keepdims=True)
            return (x - m) * jax.lax.rsqrt(v + EPS) * g + b
        key = jax.random.key(seed)
        ks = jax.random.split(key, 12)
        B, C, H, W = (4, DIM, 128, 128)
        s = lambda fan_in: 1.0 / np.sqrt(fan_in)
        inp = {'x': jax.random.normal(ks[0], (B, C, H, W), jnp.float32), 'norm1_g': jnp.ones((C,), jnp.float32), 'norm1_b': jnp.zeros((C,), jnp.float32), 'qkv_w': jax.random.normal(ks[1], (3 * C, C), jnp.float32) * s(C), 'qkv_b': jnp.zeros((3 * C,), jnp.float32), 'rpb_table': jax.random.normal(ks[2], ((2 * WS - 1) ** 2, NH), jnp.float32) * 0.02, 'proj_w': jax.random.normal(ks[3], (C, C), jnp.float32) * s(C), 'proj_b': jnp.zeros((C,), jnp.float32), 'norm2_g': jnp.ones((C,), jnp.float32), 'norm2_b': jnp.zeros((C,), jnp.float32), 'fc1_w': jax.random.normal(ks[4], (HID, C), jnp.float32) * s(C), 'fc1_b': jnp.zeros((HID,), jnp.float32), 'fc2_w': jax.random.normal(ks[5], (C, HID), jnp.float32) * s(HID), 'fc2_b': jnp.zeros((C,), jnp.float32), 'rel_idx': _rel_pos_index(WS)}
        return inp
    _L0_conv_all = _L0_conv_setup()
    _L0_conv_in = {k: v for k, v in _L0_conv_all.items() if k in ('norm1_g', 'norm1_b', 'qkv_w', 'qkv_b', 'rpb_table', 'proj_w', 'proj_b', 'norm2_g', 'norm2_b', 'fc1_w', 'fc1_b', 'fc2_w', 'fc2_b', 'rel_idx')}
    del _L0_conv_all

    def _L1_conv_setup():
        import jax, jax.numpy as jnp
        import numpy as np
        B, C, H, W = (32, 48, 56, 56)
        HID, OUP = (288, 48)
        EPS = 1e-05

        def _bn(x, g, b, m, v):
            scale = (g * jax.lax.rsqrt(v + EPS)).reshape(1, -1, 1, 1)
            shift = (b - m * g * jax.lax.rsqrt(v + EPS)).reshape(1, -1, 1, 1)
            return x * scale + shift
        key = jax.random.key(seed)
        ks = jax.random.split(key, 16)
        n = lambda k, s, sc=1.0: jax.random.normal(k, s, dtype=jnp.float32) * sc
        u = lambda k, s: jax.random.uniform(k, s, dtype=jnp.float32, minval=0.5, maxval=1.5)
        return {'x': n(ks[0], (B, C, H, W)), 'w1': n(ks[1], (HID, C), 0.05), 'g1': u(ks[2], (HID,)), 'b1': n(ks[3], (HID,), 0.1), 'm1': n(ks[4], (HID,), 0.1), 'v1': u(ks[5], (HID,)), 'wd': n(ks[6], (HID, 1, 3, 3), 0.05), 'gd': u(ks[7], (HID,)), 'bd': n(ks[8], (HID,), 0.1), 'md': n(ks[9], (HID,), 0.1), 'vd': u(ks[10], (HID,)), 'w2': n(ks[11], (OUP, HID), 0.05), 'g2': u(ks[12], (OUP,)), 'b2': n(ks[13], (OUP,), 0.1), 'm2': n(ks[14], (OUP,), 0.1), 'v2': u(ks[15], (OUP,))}
    _L1_conv_all = _L1_conv_setup()
    _L1_conv_in = {k: v for k, v in _L1_conv_all.items() if k in ('w1', 'g1', 'b1', 'm1', 'v1', 'wd', 'gd', 'bd', 'md', 'vd', 'w2', 'g2', 'b2', 'm2', 'v2')}
    del _L1_conv_all
    return {'x': x, 'L0_conv_norm1_g': _L0_conv_in['norm1_g'], 'L0_conv_norm1_b': _L0_conv_in['norm1_b'], 'L0_conv_qkv_w': _L0_conv_in['qkv_w'], 'L0_conv_qkv_b': _L0_conv_in['qkv_b'], 'L0_conv_rpb_table': _L0_conv_in['rpb_table'], 'L0_conv_proj_w': _L0_conv_in['proj_w'], 'L0_conv_proj_b': _L0_conv_in['proj_b'], 'L0_conv_norm2_g': _L0_conv_in['norm2_g'], 'L0_conv_norm2_b': _L0_conv_in['norm2_b'], 'L0_conv_fc1_w': _L0_conv_in['fc1_w'], 'L0_conv_fc1_b': _L0_conv_in['fc1_b'], 'L0_conv_fc2_w': _L0_conv_in['fc2_w'], 'L0_conv_fc2_b': _L0_conv_in['fc2_b'], 'L0_conv_rel_idx': _L0_conv_in['rel_idx'], 'L1_conv_w1': _L1_conv_in['w1'], 'L1_conv_g1': _L1_conv_in['g1'], 'L1_conv_b1': _L1_conv_in['b1'], 'L1_conv_m1': _L1_conv_in['m1'], 'L1_conv_v1': _L1_conv_in['v1'], 'L1_conv_wd': _L1_conv_in['wd'], 'L1_conv_gd': _L1_conv_in['gd'], 'L1_conv_bd': _L1_conv_in['bd'], 'L1_conv_md': _L1_conv_in['md'], 'L1_conv_vd': _L1_conv_in['vd'], 'L1_conv_w2': _L1_conv_in['w2'], 'L1_conv_g2': _L1_conv_in['g2'], 'L1_conv_b2': _L1_conv_in['b2'], 'L1_conv_m2': _L1_conv_in['m2'], 'L1_conv_v2': _L1_conv_in['v2']}

def reference(x, L0_conv_norm1_g, L0_conv_norm1_b, L0_conv_qkv_w, L0_conv_qkv_b, L0_conv_rpb_table, L0_conv_proj_w, L0_conv_proj_b, L0_conv_norm2_g, L0_conv_norm2_b, L0_conv_fc1_w, L0_conv_fc1_b, L0_conv_fc2_w, L0_conv_fc2_b, L0_conv_rel_idx, L1_conv_w1, L1_conv_g1, L1_conv_b1, L1_conv_m1, L1_conv_v1, L1_conv_wd, L1_conv_gd, L1_conv_bd, L1_conv_md, L1_conv_vd, L1_conv_w2, L1_conv_g2, L1_conv_b2, L1_conv_m2, L1_conv_v2):
    import jax
    import jax.numpy as jnp

    def _L0_conv_ref(x, norm1_g, norm1_b, qkv_w, qkv_b, rpb_table, proj_w, proj_b, norm2_g, norm2_b, fc1_w, fc1_b, fc2_w, fc2_b, rel_idx):
        import jax, jax.numpy as jnp
        import numpy as np
        WS = 8
        NH = 4
        DIM = 48
        HID = 4 * DIM
        EPS = 1e-05

        def _rel_pos_index(ws):
            coords = np.stack(np.meshgrid(np.arange(ws), np.arange(ws), indexing='ij'))
            cf = coords.reshape(2, -1)
            rel = cf[:, :, None] - cf[:, None, :]
            rel = rel.transpose(1, 2, 0).astype(np.int64)
            rel[:, :, 0] += ws - 1
            rel[:, :, 1] += ws - 1
            rel[:, :, 0] *= 2 * ws - 1
            return jnp.asarray(rel.sum(-1), dtype=jnp.int32)

        def _layernorm(x, g, b):
            m = x.mean(-1, keepdims=True)
            v = ((x - m) ** 2).mean(-1, keepdims=True)
            return (x - m) * jax.lax.rsqrt(v + EPS) * g + b
        B, C, H, W = x.shape
        ws, nh = (WS, NH)
        hd = C // nh
        scale = hd ** (-0.5)
        N = ws * ws
        xf = x.reshape(B, C, H * W).transpose(0, 2, 1)
        shortcut = xf
        h = _layernorm(xf, norm1_g, norm1_b).reshape(B, H, W, C)
        h = h.reshape(B, H // ws, ws, W // ws, ws, C)
        h = h.transpose(0, 1, 3, 2, 4, 5).reshape(-1, N, C)
        B_ = h.shape[0]
        qkv = h @ qkv_w.T + qkv_b
        qkv = qkv.reshape(B_, N, 3, nh, hd).transpose(2, 0, 3, 1, 4)
        q, k, v = (qkv[0] * scale, qkv[1], qkv[2])
        attn = jnp.einsum('whnd,whmd->whnm', q, k)
        bias = rpb_table[rel_idx]
        attn = attn + bias.transpose(2, 0, 1)[None]
        attn = jax.nn.softmax(attn, axis=-1)
        o = jnp.einsum('whnm,whmd->whnd', attn, v)
        o = o.transpose(0, 2, 1, 3).reshape(B_, N, C)
        o = o @ proj_w.T + proj_b
        o = o.reshape(B, H // ws, W // ws, ws, ws, C)
        o = o.transpose(0, 1, 3, 2, 4, 5).reshape(B, H * W, C)
        xf = shortcut + o
        m = _layernorm(xf, norm2_g, norm2_b)
        m = jax.nn.gelu(m @ fc1_w.T + fc1_b, approximate=False)
        m = m @ fc2_w.T + fc2_b
        xf = xf + m
        return xf.reshape(B, H, W, C).transpose(0, 3, 1, 2)

    def _L1_conv_ref(x, w1, g1, b1, m1, v1, wd, gd, bd, md, vd, w2, g2, b2, m2, v2):
        import jax, jax.numpy as jnp
        import numpy as np
        B, C, H, W = (32, 48, 56, 56)
        HID, OUP = (288, 48)
        EPS = 1e-05

        def _bn(x, g, b, m, v):
            scale = (g * jax.lax.rsqrt(v + EPS)).reshape(1, -1, 1, 1)
            shift = (b - m * g * jax.lax.rsqrt(v + EPS)).reshape(1, -1, 1, 1)
            return x * scale + shift
        h = jnp.einsum('oc,bchw->bohw', w1, x)
        h = jax.nn.relu(_bn(h, g1, b1, m1, v1))
        h = jax.lax.conv_general_dilated(h, wd, window_strides=(1, 1), padding=((1, 1), (1, 1)), feature_group_count=HID, dimension_numbers=('NCHW', 'OIHW', 'NCHW'))
        h = jax.nn.relu(_bn(h, gd, bd, md, vd))
        h = jnp.einsum('oc,bchw->bohw', w2, h)
        h = _bn(h, g2, b2, m2, v2)
        return x + h

    def _gn(v, G=32, eps=1e-05):
        B_, C_, H_, W_ = v.shape
        g = v.reshape(B_, G, C_ // G, H_, W_)
        m = jnp.mean(g, axis=(2, 3, 4), keepdims=True)
        s = jnp.var(g, axis=(2, 3, 4), keepdims=True)
        return ((g - m) / jnp.sqrt(s + eps)).reshape(v.shape)

    def _ln_c(v, eps=1e-06):
        m = jnp.mean(v, axis=1, keepdims=True)
        s = jnp.var(v, axis=1, keepdims=True)
        return (v - m) / jnp.sqrt(s + eps)

    def _ln_t(v, eps=1e-05):
        m = jnp.mean(v, axis=-1, keepdims=True)
        s = jnp.var(v, axis=-1, keepdims=True)
        return (v - m) / jnp.sqrt(s + eps)

    def _to_tokens(v):
        B_, C_, H_, W_ = v.shape
        return v.reshape(B_, C_, H_ * W_).transpose(0, 2, 1)

    def _from_tokens(t, like):
        B_, C_, H_, W_ = like.shape
        return t.transpose(0, 2, 1).reshape(B_, C_, H_, W_)
    x = _L0_conv_ref(x, L0_conv_norm1_g, L0_conv_norm1_b, L0_conv_qkv_w, L0_conv_qkv_b, L0_conv_rpb_table, L0_conv_proj_w, L0_conv_proj_b, L0_conv_norm2_g, L0_conv_norm2_b, L0_conv_fc1_w, L0_conv_fc1_b, L0_conv_fc2_w, L0_conv_fc2_b, L0_conv_rel_idx)
    x = _L1_conv_ref(x, L1_conv_w1, L1_conv_g1, L1_conv_b1, L1_conv_m1, L1_conv_v1, L1_conv_wd, L1_conv_gd, L1_conv_bd, L1_conv_md, L1_conv_vd, L1_conv_w2, L1_conv_g2, L1_conv_b2, L1_conv_m2, L1_conv_v2)
    return x

_drawn_inputs = setup_inputs


def setup_inputs(seed=0):
    import zlib

    import numpy as np

    out = dict(_drawn_inputs(seed))
    spreads = {'L0_conv_norm1_g': (1.0, 0.2),
     'L0_conv_norm1_b': (0.0, 0.1),
     'L0_conv_qkv_b': (0.0, 0.1),
     'L0_conv_proj_b': (0.0, 0.1),
     'L0_conv_norm2_g': (1.0, 0.2),
     'L0_conv_norm2_b': (0.0, 0.1),
     'L0_conv_fc1_b': (0.0, 0.1),
     'L0_conv_fc2_b': (0.0, 0.1)}
    factors = {'L0_conv_rpb_table': 8.0,
     'L1_conv_g1': 40.462,
     'L1_conv_b1': 8.0,
     'L1_conv_m1': 8.0,
     'L1_conv_v1': 200.0,
     'L1_conv_gd': 60.295,
     'L1_conv_vd': 200.0,
     'L1_conv_v2': 96.692,
     'L1_conv_w1': 4.249,
     'L1_conv_bd': 4.38,
     'L1_conv_g2': 5.236}
    for name, (base, spread) in spreads.items():
        noise = np.random.default_rng([zlib.crc32(name.encode()), seed]).standard_normal(out[name].shape)
        drawn = base * np.exp(spread * noise) if base else spread * noise
        out[name] = jnp.asarray(drawn.astype(out[name].dtype))
    for name, factor in factors.items():
        out[name] = (out[name] * factor).astype(out[name].dtype)
    return out
```

```python
from contextlib import ExitStack

import numpy as np

import concourse.bass as bass
from concourse import mybir

F32 = mybir.dt.float32
I32 = mybir.dt.int32
ALU = mybir.AluOpType
ACT = mybir.ActivationFunctionType
AX_X = mybir.AxisListType.X

P = 128
B, C, H, W = 4, 48, 128, 128
WS, NH = 8, 4
HD = C // NH
NT = WS * WS
EPS = 1e-5
ONE = 64

GW = 64
PAIRS = GW // (2 * WS)
TOK = PAIRS * 2 * NT
GROUPS = B * (H // WS) * (W // GW)
VB = 2 * 2 * (HD + 1)
NB = 96
MID = 112
HID0 = 4 * C

HID1 = 288
PH, PW = 10, 8
PIN, POUT = (PH + 2) * (PW + 2), PH * PW
PC, PR = 8, 13
PATCHES = PC * PR
HALF = PC * PW
SC = HALF + 2
CH = 96
CHUNKS = HID1 // CH
TCH = 32
LOADS = CH // TCH
TAPROW = 32
HALVES = B * 2
UNITS = 24


def wait(eng, sem, n):
    if not isinstance(n, int) or n >= 1:
        eng.wait_ge(sem, n)


def bc(ap, axis, n):
    a = ap.unsqueeze(axis)
    shape = list(a.shape)
    shape[axis] = n
    return a.broadcast_to(shape)


def prepare_conv(nc, d):
    half = POUT // 2
    with ExitStack() as ctx:
        sb = lambda n, s: ctx.enter_context(nc.sbuf_tensor(n, s, F32))
        sem = lambda n: ctx.enter_context(nc.semaphore(n))
        places = sb("places", [P, 2, half, P])
        taps = sb("taps", [P, HID1])
        gd, vd, md, bd = (sb(n, [P, HID1]) for n in ("gd", "vd", "md", "bd"))
        sd, shift = sb("sd", [P, HID1]), sb("shift", [P, HID1])
        eps = sb("eps_d", [P, 1])
        mats = sb("mats", [P, HID1, POUT])
        banks = [ctx.enter_context(nc.psum_tensor(f"pm{j}", [P, 512], F32)) for j in range(4)]
        loaded, cleared, eps_set = sem("d_loaded"), sem("d_cleared"), sem("d_eps")
        root, scaled = sem("d_root"), sem("d_scaled")
        mat_ready, copied_v, copied_a, stored = sem("mat_ready"), sem("mat_cv"), sem("mat_ca"), sem("mat_stored")
        K = TAPROW + 1
        block = ctx.enter_context(nc.Block(name="prepare_conv"))

        @block.sync
        def _(sp):
            sp.wait_ge(cleared, 1)
            sp.dma_start(taps[0:9, :], d["wd"]).then_inc(loaded, 16)
            sp.dma_start(places[0:K, :, :, :], d["places"].rearrange("k (a o) i -> k a o i", a=2)).then_inc(loaded, 16)
            for t, n in ((gd, "gd"), (vd, "vd"), (md, "md"), (bd, "bd")):
                sp.dma_start(t[0:K, :], d[n].partition_broadcast(K)).then_inc(loaded, 16)
            sp.wait_ge(copied_v, half)
            sp.wait_ge(copied_a, half)
            for u in range(HID1 // TCH):
                sp.dma_start(d["conv_mats"][u], mats[0:PIN + 1, u * TCH:(u + 1) * TCH, :]).then_inc(stored, 16)
            sp.wait_ge(stored, 16 * (HID1 // TCH))

        @block.vector
        def _(dve):
            nc.vector.memset(taps[:, :], 0.0).then_inc(cleared, 1)
            nc.vector.memset(eps[:, :], EPS).then_inc(eps_set, 1)
            dve.wait_ge(root, 1)
            nc.vector.reciprocal(vd[0:K, :], sd[0:K, :]).then_inc(scaled, 1)
            dve.wait_ge(scaled, 1)
            nc.vector.tensor_tensor(sd[0:K, :], vd[0:K, :], gd[0:K, :], ALU.mult).then_inc(scaled, 1)
            dve.wait_ge(scaled, 2)
            nc.vector.tensor_tensor(md[0:K, :], md[0:K, :], sd[0:K, :], ALU.mult).then_inc(scaled, 1)
            nc.vector.tensor_tensor(taps[0:9, :], taps[0:9, :], sd[0:9, :], ALU.mult).then_inc(scaled, 1)
            dve.wait_ge(scaled, 4)
            nc.vector.tensor_tensor(shift[0:K, :], bd[0:K, :], md[0:K, :], ALU.subtract).then_inc(scaled, 1)
            dve.wait_ge(scaled, 5)
            nc.vector.tensor_copy(taps[TAPROW:K, :], shift[0:1, :]).then_inc(scaled, 1)
            for j in range(0, POUT, 2):
                dve.wait_ge(mat_ready, j + 1)
                nc.vector.tensor_copy(mats[:, :, j], banks[j % 4][:, 0:HID1]).then_inc(copied_v, 1)

        @block.scalar
        def _(act):
            act.wait_ge(loaded, 96)
            act.wait_ge(eps_set, 1)
            nc.scalar.activation(sd[0:K, :], vd[0:K, :], ACT.Sqrt, bias=eps[0:K, :]).then_inc(root, 1)
            for j in range(1, POUT, 2):
                act.wait_ge(mat_ready, j + 1)
                nc.scalar.activation(mats[:, :, j], banks[j % 4][:, 0:HID1], ACT.Copy).then_inc(copied_a, 1)

        @block.tensor
        def _(pe):
            pe.wait_ge(loaded, 96)
            pe.wait_ge(scaled, 6)
            for j in range(POUT):
                if j >= 4:
                    pe.wait_ge(copied_a if j % 2 else copied_v, (j - 4) // 2 + 1)
                nc.tensor.matmul(banks[j % 4][:, 0:HID1], places[0:K, j // half, j % half, :], taps[0:K, :],
                                 start=True, stop=True).then_inc(mat_ready, 1)


def prepare_bias(nc, d):
    rows = d["table"].shape[0]
    with ExitStack() as ctx:
        sb = lambda n, s, t=F32: ctx.enter_context(nc.sbuf_tensor(n, s, t))
        sem = lambda n: ctx.enter_context(nc.semaphore(n))
        ids, idsf = sb("ids", [P, NT, NT], I32), sb("idsf", [P, NT, NT])
        table, number = sb("table", [P, 2, NH]), sb("number", [P, 2])
        onehot = sb("onehot", [P, 2, NT, NT])
        bias = sb("bias", [NT, NH, NT])
        ps = ctx.enter_context(nc.psum_tensor("ps_bias", [P, 512], F32))
        cleared, loaded, cast = sem("t_cleared"), sem("t_loaded"), sem("ids_cast")
        hot, looked_up, copied, stored = sem("hot"), sem("looked_up"), sem("b_copied"), sem("b_stored")
        block = ctx.enter_context(nc.Block(name="prepare_bias"))

        @block.sync
        def _(sp):
            sp.wait_ge(cleared, 1)
            for dst, src in ((number[:, :], d["number"]), (table[:, 0, :], d["table"][0:P, :]),
                             (table[0:rows - P, 1, :], d["table"][P:rows, :]),
                             (ids[:, :, :], d["rel_idx"].partition_broadcast(P))):
                sp.dma_start(dst, src).then_inc(loaded, 16)
            sp.wait_ge(copied, 1)
            sp.dma_start(d["rel_bias"], bias[:, :, :].rearrange("n h m -> n (h m)")).then_inc(stored, 16)
            sp.wait_ge(stored, 16)

        @block.vector
        def _(dve):
            nc.vector.memset(table[:, :, :], 0.0).then_inc(cleared, 1)
            dve.wait_ge(loaded, 64)
            nc.vector.tensor_copy(idsf[:, :, :], ids[:, :, :]).then_inc(cast, 1)
            dve.wait_ge(cast, 1)
            for t in range(2):
                nc.vector.tensor_scalar(onehot[:, t, :, :], idsf[:, :, :], number[:, t:t + 1], None, ALU.is_equal)\
                    .then_inc(hot, 1)
            dve.wait_ge(looked_up, 1)
            nc.vector.tensor_copy(bias[:, :, :], ps[0:NT, 0:NT * NH].rearrange("n (m h) -> n h m", h=NH))\
                .then_inc(copied, 1)

        @block.tensor
        def _(pe):
            pe.wait_ge(hot, 2)
            for m in range(NT):
                for t in range(2):
                    mm = nc.tensor.matmul(ps[0:NT, m * NH:(m + 1) * NH], onehot[:, t, :, m], table[:, t, :],
                                          start=(t == 0), stop=(t == 1))
            mm.then_inc(looked_up, 1)


def attention(nc, d):
    with ExitStack() as ctx:
        sb = lambda n, s, t=F32: ctx.enter_context(nc.sbuf_tensor(n, s, t))
        sem = lambda n: ctx.enter_context(nc.semaphore(n))
        ident = sb("ident", [P, P])
        headmask = sb("headmask", [P, NH])
        eps = sb("eps", [P, 1])
        w_qk = sb("w_qk", [P, 112])
        w_v, w_o = sb("w_v", [P, NB]), sb("w_o", [P, NB])
        qkv_w, qkv_b = sb("qkv_w", [C, 3 * C]), sb("qkv_b", [1, 3 * C])
        lnrow = sb("lnrow", [1, 3 * C])
        ln_g, ln_b = sb("ln_g", [C, 1]), sb("ln_b", [C, 1])
        xs = [sb(f"xs{s}", [C, TOK]) for s in range(2)]
        xtok = sb("xtok", [P, GROUPS, PAIRS, C])
        sums, sq_sums, lnv, rstd = ([sb(f"{n}{s}", [P, PAIRS]) for s in range(2)] for n in ("sum", "sqs", "lnv", "rstd"))
        sums2, sq_sums2, lnv2, rstd2 = ([sb(f"{n}{s}", [P, PAIRS]) for s in range(2)] for n in ("sumb", "sqsb", "lnvb", "rstdb"))
        cen = [sb(f"cen{s}", [P, PAIRS, C]) for s in range(2)]
        cen2 = [sb(f"cenb{s}", [P, PAIRS, C]) for s in range(2)]
        sq, sq2 = sb("sq", [P, PAIRS, C]), sb("sqb", [P, PAIRS, C])
        xn = [sb(f"xn{s}", [P, PAIRS, C]) for s in range(2)]
        xnT = [sb(f"xnT{s}", [P, TOK]) for s in range(2)]
        qa = [sb(f"qa{s}", [P, TOK]) for s in range(2)]
        ks = sb("ks", [P, TOK])
        kb = [sb(f"kb{s}", [P, 2 * PAIRS, NH, NT]) for s in range(2)]
        vb = [sb(f"vb{s}", [P, 2 * PAIRS * VB + NB - VB]) for s in range(2)]
        top = [sb(f"top{s}", [P, PAIRS * NH]) for s in range(2)]
        prob = [sb(f"prob{s}", [P, PAIRS * NH, NT]) for s in range(2)]
        probT = sb("probT", [P, PAIRS, 2, P])
        rden = sb("rden", [P, 2 * PAIRS, 2])
        o = sb("o", [P, PAIRS, C])
        oT = sb("oT", [P, TOK])
        mid = [sb(f"mid{s}", [P, PAIRS, MID]) for s in range(2)]

        ps_s = ctx.enter_context(nc.psum_tensor("ps_s", [P, 2, 512], F32))
        ps_p = ctx.enter_context(nc.psum_tensor("ps_p", [P, 2, 512], F32))
        ps_x = ctx.enter_context(nc.psum_tensor("ps_x", [P, 512], F32))
        ps_t = ctx.enter_context(nc.psum_tensor("ps_t", [P, 512], F32))
        ps_k = ctx.enter_context(nc.psum_tensor("ps_k", [P, 512], F32))
        ps_v = ctx.enter_context(nc.psum_tensor("ps_v", [P, 512], F32))

        w_loaded, fixed, w_bias, w_ready = sem("w_loaded"), sem("fixed"), sem("w_bias"), sem("w_ready")
        ident_put = sem("ident_put")
        x_loaded = [sem(f"x_loaded{s}") for s in range(2)]
        stored = [sem(f"mid_stored{s}") for s in range(2)]
        x_turned, x_copied, sum_done, cen_done, sq_done, var_done, ln_done, rstd_done, xn_done = (
            sem(n) for n in ("x_turned", "x_copied", "sum_done", "cen_done", "sq_done", "var_done", "ln_done",
                             "rstd_done", "xn_done"))
        xnT_ready, xnT_copied, qk_ready, k_copied, q_copied, kb_done = (
            sem(n) for n in ("xnT_ready", "xnT_copied", "qk_ready", "k_copied", "q_copied", "kb_done"))
        v_ready, v_copied, s_ready, top_done, sub_done, exp_done = (
            sem(n) for n in ("v_ready", "v_copied", "s_ready", "top_done", "sub_done", "exp_done"))
        pT_ready, pT_copied, o_ready, rden_done, o_done, oT_ready, oT_copied, y_ready, res_done = (
            sem(n) for n in ("pT_ready", "pT_copied", "o_ready", "rden_done", "o_done", "oT_ready", "oT_copied",
                             "y_ready", "res_done"))
        sum2_done, cen2_done, sq2_done, var2_done, ln2_done, rstd2_done, mid_done = (
            sem(n) for n in ("sum2_done", "cen2_done", "sq2_done", "var2_done", "ln2_done", "rstd2_done", "mid_done"))

        W_LOADS = 10
        def has(g):
            return not isinstance(g, int) or 0 <= g < GROUPS

        def schedule(eng, step):
            for i in range(-2, 6):
                step(i, i % 2)
            with eng.Fori(6, GROUPS - 5, 2) as i:
                step(i, 0)
                step(i + 1, 1)
            for i in range(GROUPS - 4, GROUPS + 3):
                step(i, i % 2)

        block = ctx.enter_context(nc.Block(name="attention"))

        @block.sync
        def _(sp):
            sp.wait_ge(fixed, 1)
            for dst, src in ((ident[:, :], d["ident"]), (headmask[:, :], d["headmask"]), (qkv_w[:, :], d["qkv_wT"]),
                             (qkv_b[:, :], d["qkv_b"]), (ln_g[:, :], d["n1_g"]), (ln_b[:, :], d["n1_b"]),
                             (w_o[0:C, 0:C], d["proj_wT"]), (w_o[ONE:ONE + 1, 0:C], d["proj_b"]),
                             (kb[0][0:NT, :, :, :], bc(d["rel_bias"], 1, 2 * PAIRS)),
                             (kb[1][0:NT, :, :, :], bc(d["rel_bias"], 1, 2 * PAIRS))):
                sp.dma_start(dst, src).then_inc(w_loaded, 16)

            def load(g, s):
                if has(g):
                    wait(sp, x_turned, g - 1)
                    sp.dma_start(xs[s][:, :], d["x_groups"][g]).then_inc(x_loaded[s], 16)

            def step(i, s):
                load(i + 4, s)
                if has(i - 3):
                    sp.wait_ge(mid_done, i - 2)
                    sp.dma_start(d["tok_mid"][i - 3], mid[1 - s][:, :, :]).then_inc(stored[1 - s], 16)

            load(0, 0)
            load(1, 1)
            schedule(sp, step)
            for s in range(2):
                sp.wait_ge(stored[s], 16 * (GROUPS // 2))

        @block.tensor
        def _(pe):
            pe.wait_ge(w_loaded, 16 * W_LOADS)
            nc.tensor.matmul(ps_x[0:1, 0:3 * C], ln_b[:, :], qkv_w[:, :], start=True, stop=True).then_inc(w_bias, 1)
            pe.wait_ge(w_ready, 6)
            pe.wait_ge(ident_put, 1)

            def step(i, s):
                if isinstance(i, int):
                    for sem, g in ((v_copied, i - 1), (oT_copied, i - 3), (xnT_copied, i), (res_done, i - 3),
                                   (x_copied, i + 1), (pT_copied, i - 2), (o_done, i - 2), (q_copied, i)):
                        if has(g):
                            pe.wait_ge(sem, g + 1)
                if has(i):
                    pe.wait_ge(q_copied, i + 1)
                    pe.wait_ge(kb_done, i + 1)
                    wait(pe, sub_done, i)
                    for n in range(2 * PAIRS):
                        if n == 2 * PAIRS - 2 and has(i + 1):
                            pe.wait_ge(xn_done, i + 2)
                            if has(i - 3):
                                pe.wait_ge(oT_copied, i - 2)
                        p, w = divmod(n, 2)
                        mm = nc.tensor.matmul(ps_s[NT * w:NT * w + NT, p // 2, 256 * (p % 2):256 * (p % 2) + 256],
                                              qa[s][:, NT * n:NT * n + NT], kb[s][:, n, :, :], start=True, stop=True)
                    mm.then_inc(s_ready, 1)
                elif has(i + 1):
                    pe.wait_ge(xn_done, i + 2)
                if has(i + 1):
                    for p in range(PAIRS):
                        mm = nc.tensor.transpose(ps_t[0:C, P * p:P * p + P], xn[1 - s][:, p, :], ident[:, :])
                    mm.then_inc(xnT_ready, 1)
                if has(i - 1):
                    pe.wait_ge(exp_done, i)
                    wait(pe, pT_copied, i - 1)
                    for p in range(PAIRS):
                        for h in range(2):
                            src = prob[1 - s][:, NH * p + 2 * h:NH * p + 2 * h + 2, :]
                            at = 256 * (p % 2) + P * h
                            mm = nc.tensor.transpose(ps_p[:, p // 2, at:at + P], src, ident[:, :])
                    mm.then_inc(pT_ready, 1)
                if has(i):
                    wait(pe, o_done, i - 1)
                if has(i + 2):
                    pe.wait_ge(x_loaded[s], 8 * (i + 2 - s) + 16)
                    wait(pe, res_done, i - 2)
                if has(i):
                    for p in range(PAIRS):
                        mm = nc.tensor.matmul(ps_v[:, C * p:C * p + NB], xnT[s][:, P * p:P * p + P], w_v[:, :],
                                              start=True, stop=True)
                    mm.then_inc(v_ready, 1)
                if has(i + 2):
                    for p in range(PAIRS):
                        mm = nc.tensor.transpose(ps_x[:, C * p:C * p + C], xs[s][:, P * p:P * p + P], ident[0:C, 0:C])
                    mm.then_inc(x_turned, 1)
                if has(i + 1):
                    pe.wait_ge(xnT_copied, i + 2)
                    wait(pe, q_copied, i + 1)
                if has(i - 2):
                    pe.wait_ge(o_done, i - 1)
                if has(i + 1):
                    nc.tensor.matmul(ps_k[0:112, :], w_qk[:, :], xnT[1 - s][:, :], start=True, stop=True)\
                        .then_inc(qk_ready, 1)
                if has(i - 2):
                    for p in range(PAIRS):
                        mm = nc.tensor.transpose(ps_t[0:C, P * p:P * p + P], o[:, p, :], ident[:, :])
                    mm.then_inc(oT_ready, 1)
                if has(i - 1):
                    pe.wait_ge(pT_copied, i)
                    if has(i):
                        pe.wait_ge(v_copied, i + 1)
                    for p in range(PAIRS):
                        for h in range(2):
                            at = VB * (2 * p + h)
                            mm = nc.tensor.matmul(ps_v[:, at:at + NB], probT[:, p, h, :], vb[1 - s][:, at:at + NB],
                                                  start=True, stop=True)
                    mm.then_inc(o_ready, 1)
                if has(i - 2):
                    pe.wait_ge(oT_copied, i - 1)
                    if has(i + 2):
                        pe.wait_ge(x_copied, i + 3)
                    for p in range(PAIRS):
                        mm = nc.tensor.matmul(ps_x[:, C * p:C * p + NB], oT[:, P * p:P * p + P], w_o[:, :],
                                              start=True, stop=True)
                    mm.then_inc(y_ready, 1)

            schedule(pe, step)

        @block.vector
        def _(dve):
            for t in (w_qk, w_v, w_o, xnT[0], xnT[1], oT, qa[0], qa[1], vb[0], vb[1], kb[0], kb[1], mid[0], mid[1]):
                nc.vector.memset(t[...], 0.0)
            nc.vector.memset(eps[:, :], EPS).then_inc(fixed, 1)
            dve.wait_ge(fixed, 1)
            for t in (xnT[0], xnT[1], oT):
                nc.vector.memset(t[ONE:ONE + 1, :], 1.0)
            for s in range(2):
                v5 = vb[s][:, 0:2 * PAIRS * VB].rearrange("q (b w h e) -> q b w h e", w=2, h=2, e=HD + 1)
                for h in range(2):
                    for w in range(2):
                        last = nc.vector.memset(v5[NT * h:NT * h + NT, :, w, h, HD:HD + 1], 1.0)
            last.then_inc(fixed, 1)
            dve.wait_ge(w_loaded, 16 * W_LOADS)
            for s in range(2):
                last = nc.vector.tensor_copy(qa[s][0:NT, :].rearrange("q (n t) -> q n t", n=2 * PAIRS),
                                             bc(ident[0:NT, 0:NT], 1, 2 * PAIRS))
            last.then_inc(ident_put, 1)
            nc.vector.tensor_scalar(w_qk[0:C, 0:C], qkv_w[:, 0:C], ln_g[:, 0:1], HD ** -0.5, ALU.mult, ALU.mult)\
                .then_inc(w_ready, 1)
            nc.vector.tensor_scalar(w_qk[0:C, ONE:ONE + C], qkv_w[:, C:2 * C], ln_g[:, 0:1], None, ALU.mult)\
                .then_inc(w_ready, 1)
            nc.vector.tensor_scalar(w_v[0:C, 0:C], qkv_w[:, 2 * C:3 * C], ln_g[:, 0:1], None, ALU.mult)\
                .then_inc(w_ready, 1)
            dve.wait_ge(w_bias, 1)
            nc.vector.tensor_tensor(lnrow[:, :], ps_x[0:1, 0:3 * C], qkv_b[:, :], ALU.add).then_inc(fixed, 1)
            dve.wait_ge(fixed, 3)
            one = slice(ONE, ONE + 1)
            nc.vector.tensor_scalar(w_qk[one, 0:C], lnrow[:, 0:C], HD ** -0.5, None, ALU.mult).then_inc(w_ready, 1)
            nc.vector.tensor_copy(w_qk[one, ONE:ONE + C], lnrow[:, C:2 * C]).then_inc(w_ready, 1)
            nc.vector.tensor_copy(w_v[one, 0:C], lnrow[:, 2 * C:3 * C]).then_inc(w_ready, 1)

            def step(i, s):
                if has(i - 2):
                    dve.wait_ge(o_ready, i - 1)
                    wait(dve, oT_ready, i - 2)
                    for w in range(2):
                        t = slice(NT * w, NT * w + NT)
                        v5 = ps_v[t, 0:2 * PAIRS * VB].rearrange("q (b w h e) -> q b w h e", w=2, h=2, e=HD + 1)
                        nc.vector.reciprocal(rden[t, :, :], v5[:, :, w, :, HD]).then_inc(rden_done, 1)
                    dve.wait_ge(rden_done, 2 * i - 2)
                    for w in range(2):
                        t = slice(NT * w, NT * w + NT)
                        v5 = ps_v[t, 0:2 * PAIRS * VB].rearrange("q (b w h e) -> q b w h e", w=2, h=2, e=HD + 1)
                        last = nc.vector.tensor_tensor(
                            o[t, :, :].rearrange("q p (a h e) -> q (p a) h e", a=2, h=2), v5[:, :, w, :, 0:HD],
                            bc(rden[t, :, :], 3, HD), ALU.mult)
                    last.then_inc(o_done, 1)
                if has(i - 3):
                    dve.wait_ge(y_ready, i - 2)
                    wait(dve, stored[1 - s], 8 * (i - 3 - (1 - s)))
                    x = xtok[:, bass.ds(i - 3, 1), :, :].rearrange("q g p c -> q (g p) c")
                    m = mid[1 - s][:, :, ONE:ONE + C]
                    nc.vector.tensor_tensor(m, ps_x[:, 0:PAIRS * C].rearrange("q (p c) -> q p c", c=C), x, ALU.add)\
                        .then_inc(res_done, 1)
                    dve.wait_ge(res_done, i - 2)
                    nc.vector.tensor_reduce(sums2[1 - s][:, :], m, AX_X, ALU.add).then_inc(sum2_done, 1)
                    dve.wait_ge(sum2_done, i - 2)
                    nc.vector.scalar_tensor_tensor(cen2[1 - s][:, :, :], bc(sums2[1 - s][:, :], 2, C), -1.0 / C, m,
                                                   ALU.mult, ALU.add).then_inc(cen2_done, 1)
                if has(i):
                    dve.wait_ge(s_ready, i + 1)
                    sc = ps_s[:, :, :].rearrange("q b (h m) -> q (b h) m", m=NT)
                    nc.vector.tensor_reduce(top[s][:, :], sc, AX_X, ALU.max).then_inc(top_done, 1)
                    dve.wait_ge(top_done, i + 1)
                    nc.vector.tensor_tensor(prob[s][:, :, :], sc, bc(top[s][:, :], 2, NT), ALU.subtract)\
                        .then_inc(sub_done, 1)
                if has(i + 2):
                    dve.wait_ge(x_copied, i + 3)
                    x = xtok[:, bass.ds(i + 2, 1), :, :].rearrange("q g p c -> q (g p) c")
                    nc.vector.tensor_reduce(sums[s][:, :], x, AX_X, ALU.add).then_inc(sum_done, 1)
                    dve.wait_ge(sum_done, i + 3)
                    nc.vector.scalar_tensor_tensor(cen[s][:, :, :], bc(sums[s][:, :], 2, C), -1.0 / C, x,
                                                   ALU.mult, ALU.add).then_inc(cen_done, 1)
                if has(i + 1):
                    dve.wait_ge(k_copied, i + 2)
                    for h in range(NH):
                        last = nc.vector.tensor_scalar(
                            kb[1 - s][ONE:ONE + C, :, h, :], ks[ONE:ONE + C, :].rearrange("q (n m) -> q n m", m=NT),
                            headmask[ONE:ONE + C, h:h + 1], None, ALU.mult)
                    last.then_inc(kb_done, 1)
                if has(i + 2):
                    dve.wait_ge(sq_done, i + 3)
                    nc.vector.tensor_reduce(sq_sums[s][:, :], sq[:, :, :], AX_X, ALU.add).then_inc(var_done, 1)
                if has(i - 3):
                    dve.wait_ge(sq2_done, i - 2)
                    nc.vector.tensor_reduce(sq_sums2[1 - s][:, :], sq2[:, :, :], AX_X, ALU.add).then_inc(var2_done, 1)

            schedule(dve, step)

        @block.scalar
        def _(act):
            nc.scalar.preload_act_table_set("natural_log_exp_and_others")
            act.wait_ge(fixed, 2)

            def step(i, s):
                if has(i + 1):
                    act.wait_ge(xnT_ready, i + 2)
                    nc.scalar.activation(xnT[1 - s][0:C, :], ps_t[0:C, :], ACT.Copy).then_inc(xnT_copied, 1)
                if has(i - 1):
                    act.wait_ge(pT_ready, i)
                    nc.scalar.activation(probT[:, :, :, :].rearrange("q p h n -> q (p h n)"),
                                         ps_p[:, :, :].rearrange("q b n -> q (b n)"), ACT.Copy).then_inc(pT_copied, 1)
                if has(i):
                    act.wait_ge(v_ready, i + 1)
                    for h in range(2):
                        for w in range(2):
                            dst = vb[s][NT * h:NT * h + NT, 0:2 * PAIRS * VB].rearrange(
                                "q (b w h e) -> q b w h e", w=2, h=2, e=HD + 1)[:, :, w, h, 0:HD]
                            src = ps_v[NT * w:NT * w + NT, 0:PAIRS * C].rearrange("q (b h e) -> q b h e", h=2, e=HD)
                            last = nc.scalar.activation(dst, src[:, :, h, :], ACT.Copy)
                    last.then_inc(v_copied, 1)
                if has(i + 2):
                    act.wait_ge(x_turned, i + 3)
                    x = xtok[:, bass.ds(i + 2, 1), :, :].rearrange("q g p c -> q (g p c)")
                    nc.scalar.activation(x, ps_x[:, 0:PAIRS * C], ACT.Copy).then_inc(x_copied, 1)
                if has(i + 1):
                    act.wait_ge(qk_ready, i + 2)
                    wait(act, kb_done, i + 1)
                    nc.scalar.activation(ks[ONE:ONE + C, :], ps_k[ONE:ONE + C, :], ACT.Copy).then_inc(k_copied, 1)
                    nc.scalar.activation(qa[1 - s][ONE:ONE + C, :], ps_k[0:C, :], ACT.Copy).then_inc(q_copied, 1)
                if has(i - 2):
                    act.wait_ge(oT_ready, i - 1)
                    nc.scalar.activation(oT[0:C, :], ps_t[0:C, :], ACT.Copy).then_inc(oT_copied, 1)
                if has(i):
                    act.wait_ge(sub_done, i + 1)
                    nc.scalar.activation(prob[s][:, :, :], prob[s][:, :, :], ACT.Exp).then_inc(exp_done, 1)
                if has(i + 2):
                    act.wait_ge(var_done, i + 3)
                    nc.scalar.activation(lnv[s][:, :], sq_sums[s][:, :], ACT.Ln, bias=eps[:, :], scale=1.0 / C)\
                        .then_inc(ln_done, 1)
                    act.wait_ge(ln_done, i + 3)
                    nc.scalar.activation(rstd[s][:, :], lnv[s][:, :], ACT.Exp, scale=-0.5).then_inc(rstd_done, 1)
                if has(i - 3):
                    act.wait_ge(var2_done, i - 2)
                    nc.scalar.activation(lnv2[1 - s][:, :], sq_sums2[1 - s][:, :], ACT.Ln, bias=eps[:, :], scale=1.0 / C)\
                        .then_inc(ln2_done, 1)
                    act.wait_ge(ln2_done, i - 2)
                    nc.scalar.activation(rstd2[1 - s][:, :], lnv2[1 - s][:, :], ACT.Exp, scale=-0.5)\
                        .then_inc(rstd2_done, 1)

            schedule(act, step)

        @block.gpsimd
        def _(pool):
            def step(i, s):
                if has(i - 3):
                    pool.wait_ge(cen2_done, i - 2)
                    nc.gpsimd.tensor_tensor(sq2[:, :, :], cen2[1 - s][:, :, :], cen2[1 - s][:, :, :], ALU.mult)\
                        .then_inc(sq2_done, 1)
                if has(i + 2):
                    pool.wait_ge(cen_done, i + 3)
                    nc.gpsimd.tensor_tensor(sq[:, :, :], cen[s][:, :, :], cen[s][:, :, :], ALU.mult).then_inc(sq_done, 1)
                    pool.wait_ge(rstd_done, i + 3)
                    nc.gpsimd.tensor_tensor(xn[s][:, :, :], cen[s][:, :, :], bc(rstd[s][:, :], 2, C), ALU.mult)\
                        .then_inc(xn_done, 1)
                if has(i - 3):
                    pool.wait_ge(rstd2_done, i - 2)
                    nc.gpsimd.tensor_tensor(mid[1 - s][:, :, 0:C], cen2[1 - s][:, :, :], bc(rstd2[1 - s][:, :], 2, C),
                                            ALU.mult).then_inc(mid_done, 1)

            schedule(pool, step)



def mlp(nc, d):
    STRIPS = GROUPS // 2
    REST = HID0 - P
    with ExitStack() as ctx:
        sb = lambda n, s: ctx.enter_context(nc.sbuf_tensor(n, s, F32))
        sem = lambda n: ctx.enter_context(nc.semaphore(n))
        ident = sb("ident2", [P, P])
        fc1, bias_row = sb("fc1", [C, HID0]), sb("bias_row", [1, HID0])
        g, b = sb("g2", [C, 1]), sb("b2", [C, 1])
        w1 = sb("w1", [P, HID0])
        w2 = sb("w2", [P, NT])
        w2r = [sb(f"w2r{k}", [P, NT]) for k in range(2)]
        b1, b1r = sb("b1", [P, 1]), sb("b1r", [P, 1])
        b2c = sb("b2c", [P, 1])
        mid = [sb(f"midb{s}", [P, 2, PAIRS, MID]) for s in range(2)]
        lnT = [sb(f"lnT{s}", [P, 2, TOK]) for s in range(2)]
        xT = [sb(f"xT{s}", [P, TOK]) for s in range(2)]
        hid = [sb(f"hid{s}", [P, 3, TOK]) for s in range(2)]
        y = [sb(f"y{s}", [P, WS, GW + 2]) for s in range(2)]
        ps_t = ctx.enter_context(nc.psum_tensor("ps_t2", [P, 2, 512], F32))
        ps_h = ctx.enter_context(nc.psum_tensor("ps_h", [P, 3, 512], F32))
        ps_y = ctx.enter_context(nc.psum_tensor("ps_y", [P, 2, 512], F32))
        fixed, w_loaded, w_bias, w_ready = sem("m_fixed"), sem("m_loaded"), sem("m_bias"), sem("m_ready")
        loaded = [sem(f"mid_loaded{s}") for s in range(2)]
        stored = [sem(f"img_stored{s}") for s in range(2)]
        turned, ln_copied, x_copied, hid_ready, gelu_done, y_ready, y_done = (
            sem(n) for n in ("m_turned", "m_ln_copied", "m_x_copied", "m_hid_ready", "gelu_done", "m_y_ready", "m_y_done"))

        def has(j):
            return not isinstance(j, int) or 0 <= j < STRIPS

        def schedule(eng, step):
            for j in range(-1, 4):
                step(j, j % 2)
            with eng.Fori(4, STRIPS - 5, 2) as j:
                step(j, 0)
                step(j + 1, 1)
            for j in range(STRIPS - 4, STRIPS + 1):
                step(j, j % 2)

        block = ctx.enter_context(nc.Block(name="mlp"))

        @block.sync
        def _(sp):
            sp.wait_ge(fixed, 1)
            for dst, src in ((ident[:, :], d["ident"]), (fc1[:, :], d["fc1_wT"]), (g[:, :], d["n2_g"]), (b[:, :], d["n2_b"]),
                             (w2[:, 0:C], d["fc2_wT"][0:P, :]), (w2r[0][0:REST, 0:C], d["fc2_wT"][P:HID0, :]),
                             (w2r[1][REST:P, 0:C], d["fc2_wT"][P:HID0, :]), (b1[:, :], d["fc1_b"][0:P, :]),
                             (b1r[0:REST, :], d["fc1_b"][P:HID0, :]), (b1r[REST:P, :], d["fc1_b"][P:HID0, :]),
                             (b2c[0:C, :], d["fc2_b"]), (b2c[ONE:ONE + C, :], d["fc2_b"])):
                sp.dma_start(dst, src).then_inc(w_loaded, 16)

            def load(j, s):
                if has(j):
                    wait(sp, turned, j - 1)
                    sp.dma_start(mid[s][:, :, :, :].rearrange("q k p e -> q k (p e)"),
                                 d["mid_strips"][j]).then_inc(loaded[s], 16)

            def step(j, s):
                load(j + 3, 1 - s)
                if has(j - 1):
                    sp.wait_ge(y_done, j)
                    for k in range(2):
                        x0 = (GW + 1) * k
                        sp.dma_start(d["img_strips"][:, j - 1, :, x0:x0 + GW + 1], y[1 - s][64 * k:64 * k + C, :, k:k + GW + 1])\
                            .then_inc(stored[1 - s], 16)

            load(0, 0)
            load(1, 1)
            schedule(sp, step)
            for s in range(2):
                sp.wait_ge(stored[s], 32 * (STRIPS // 2))

        @block.tensor
        def _(pe):
            pe.wait_ge(w_loaded, 16 * 12)
            nc.tensor.matmul(ps_y[0:1, 0, 0:HID0], b[:, :], fc1[:, :], start=True, stop=True).then_inc(w_bias, 1)
            pe.wait_ge(w_ready, 2)

            def step(j, s):
                if has(j + 1):
                    pe.wait_ge(loaded[1 - s], 8 * (j + 1 - (1 - s)) + 16)
                    wait(pe, ln_copied, j + 1)
                    wait(pe, x_copied, j + 1)
                    for k in range(2):
                        for p in range(PAIRS):
                            mm = nc.tensor.transpose(ps_t[0:MID, k, P * p:P * p + P], mid[1 - s][:, k, p, :], ident[:, :])
                    mm.then_inc(turned, 1)
                if has(j - 1):
                    pe.wait_ge(gelu_done, 3 * j)
                    wait(pe, y_done, j - 2)
                    for half in range(2):
                        for k in range(2):
                            mm = nc.tensor.matmul(ps_y[64 * k:64 * k + 64, 1 - s, :], w2r[k][:, :] if half else w2[:, :],
                                                  hid[1 - s][:, 2 if half else k, :], start=(half == 0), stop=(half == 1))
                    mm.then_inc(y_ready, 1)
                if has(j):
                    pe.wait_ge(ln_copied, j + 1)
                    for k in range(2):
                        wait(pe, gelu_done, 3 * j - 2 + k)
                        nc.tensor.matmul(ps_h[:, k, :], w1[:, 0:P], lnT[s][:, k, :], start=True, stop=True)\
                            .then_inc(hid_ready, 1)
                    wait(pe, gelu_done, 3 * j)
                    for k in range(2):
                        mm = nc.tensor.matmul(ps_h[REST * k:REST * k + REST, 2, :], w1[:, P:HID0], lnT[s][:, k, :],
                                              start=True, stop=True)
                    mm.then_inc(hid_ready, 1)

            schedule(pe, step)

        @block.vector
        def _(dve):
            for t in (w1, w2, w2r[0], w2r[1], lnT[0], lnT[1], xT[0], xT[1], y[0], y[1]):
                nc.vector.memset(t[...], 0.0)
            nc.vector.memset(b2c[:, :], 0.0).then_inc(fixed, 1)
            dve.wait_ge(w_loaded, 16 * 12)
            dve.wait_ge(w_bias, 1)
            nc.vector.tensor_copy(bias_row[:, :], ps_y[0:1, 0, 0:HID0]).then_inc(w_ready, 1)
            nc.vector.tensor_scalar(w1[0:C, :], fc1[:, :], g[:, 0:1], None, ALU.mult)
            dve.wait_ge(w_ready, 1)
            nc.vector.tensor_copy(w1[ONE:ONE + 1, :], bias_row[:, :])
            for s in range(2):
                last = nc.vector.memset(lnT[s][ONE:ONE + 1, :, :], 1.0)
            last.then_inc(w_ready, 1)

            def step(j, s):
                if has(j - 1):
                    dve.wait_ge(x_copied, j)
                    dve.wait_ge(y_ready, j)
                    wait(dve, stored[1 - s], 16 * (j - 1 - (1 - s)))
                    px = lambda ap: ap.rearrange("q (n r c) -> q n r c", r=WS, c=WS)
                    nc.vector.tensor_tensor(y[1 - s][:, :, 1:GW + 1].rearrange("q r (n c) -> q n r c", c=WS),
                                            px(ps_y[:, 1 - s, :]), px(xT[1 - s][:, :]), ALU.add).then_inc(y_done, 1)
                if has(j + 1):
                    wait(dve, y_done, j)
                    dve.wait_ge(turned, j + 2)
                    for k in range(2):
                        r = slice(64 * k, 64 * k + C)
                        last = nc.vector.tensor_scalar(xT[1 - s][r, :], ps_t[ONE:ONE + C, k, :], b2c[r, 0:1], None, ALU.add)
                    last.then_inc(x_copied, 1)

            schedule(dve, step)

        @block.scalar
        def _(act):
            act.wait_ge(w_ready, 2)

            def step(j, s):
                if has(j + 1):
                    act.wait_ge(turned, j + 2)
                    nc.scalar.activation(lnT[1 - s][0:C, :, :].rearrange("q k t -> q (k t)"),
                                         ps_t[0:C, :, :].rearrange("q k t -> q (k t)"), ACT.Copy).then_inc(ln_copied, 1)
                if has(j):
                    for k in range(3):
                        act.wait_ge(hid_ready, 3 * j + k + 1)
                        nc.scalar.activation(hid[s][:, k, :], ps_h[:, k, :], ACT.Gelu,
                                             bias=(b1r if k == 2 else b1)[:, 0:1]).then_inc(gelu_done, 1)

            schedule(act, step)


def conv(nc, d):
    with ExitStack() as ctx:
        sb = lambda n, s: ctx.enter_context(nc.sbuf_tensor(n, s, F32))
        sem = lambda n: ctx.enter_context(nc.semaphore(n))
        ident = sb("ident3", [P, P])
        eps = sb("eps3", [P, 1])
        w1 = sb("ew", [P, CHUNKS, CH])
        w2 = sb("pw", [P, CHUNKS, NT])
        q = {n: sb(f"q_{n}", [CH, C]) for n in "gvt"}
        c2 = {n: sb(f"c_{n}", [P, 1]) for n in "gbmvt"}
        piece = [sb(f"piece{s}", [C, PH + 2, SC]) for s in range(4)]
        xp = sb("xp", [P, PATCHES, PIN])
        h1 = sb("h1", [P, CH, PATCHES])
        e = {n: h1[0:C, CHUNKS * j:CHUNKS * (j + 1), 0:CH] for j, n in enumerate("gbmvt")}
        h2 = sb("h2", [POUT, PATCHES, CH])
        mats = [sb(f"mats{s}", [PIN + 1, TCH, POUT]) for s in range(LOADS)]
        h2T = [[sb(f"h2T{s}{k}", [P, 5 * POUT]) for k in range(2)] for s in range(2)]
        y = sb("yc", [P, PR * PH, PC // 2 * PW])
        ring = [ctx.enter_context(nc.psum_tensor(f"ring{s}", [P, 512], F32)) for s in range(4)]
        ps_t = [ctx.enter_context(nc.psum_tensor(f"ps_t3{k}", [P, 512], F32)) for k in range(2)]
        ps_y = [ctx.enter_context(nc.psum_tensor(f"ps_yc{s}", [P, 512], F32)) for s in range(2)]
        fixed, w_loaded, root, w_ready = sem("c_fixed"), sem("c_loaded"), sem("c_root"), sem("c_ready")
        piece_loaded, cut, ones_set = [sem(f"piece_loaded{s}") for s in range(4)], sem("cut"), sem("ones_set")
        mats_loaded = [sem(f"mats_loaded{s}") for s in range(LOADS)]
        unit_ready, unit_act, unit_dve = sem("unit_ready"), sem("unit_act"), sem("unit_dve")
        turned, copied_act, copied_dve = sem("c_turned"), sem("c_copied_act"), sem("c_copied_dve")
        y_ready, y_done, y_stored = sem("c_y_ready"), sem("c_y_done"), sem("c_y_stored")

        fives = PATCHES - 4 * UNITS
        start = lambda j: 4 * j + min(j, fives)
        PARTS = ((0, 5), (5, 4), (9, 4))
        STEPS = [(pc, a, n) for pc in range(PC // 2) for a, n in PARTS]
        NSTEP = len(STEPS)

        def schedule(eng, first, chunk):
            first()
            with eng.Fori(0, HALVES // 2 - 1, 1) as b:
                for hx in range(2):
                    for c in range(CHUNKS):
                        chunk(b, hx, c, False)
            for hx in range(2):
                for c in range(CHUNKS):
                    chunk(HALVES // 2 - 1, hx, c, hx == 1 and c == CHUNKS - 1)

        def more(b, hx):
            return not (hx == 1 and isinstance(b, int))

        slot_of = [0] + [1 + j % 2 for j in range(1, PR - 1)] + [3]
        PER_HALF = [slot_of.count(s) for s in range(4)]

        def nth_in_slot(j):
            return slot_of[:j].count(slot_of[j])

        def place_of(j):
            s = slot_of[j]
            before = [i for i in range(j) if slot_of[i] == s]
            return s, before[-1] + 1 if before else max(i for i in range(PR) if slot_of[i] == s) + 1 - PR

        def number(b, hx, c):
            return 2 * CHUNKS * b + CHUNKS * hx + c

        def expand_at(j):
            return start(j), start(j + 1) - start(j)

        def evacuate(activation, j, expand):
            bank = ring[j % 4]
            if expand:
                a, n = expand_at(j)
                dst = h1[0:PIN, :, a:a + n].rearrange("q c p -> q p c")
                src = bank[0:PIN, 0:n * CH].rearrange("q (p c) -> q p c", c=CH)
            else:
                dst = h2[:, :, 4 * j:4 * j + 4].rearrange("q p c -> q c p")
                src = bank[0:POUT, 0:4 * PATCHES].rearrange("q (c p) -> q c p", c=4)
            if activation:
                return nc.scalar.activation(dst, src, ACT.Relu)
            return nc.vector.tensor_scalar(dst, src, 0.0, None, ALU.max)

        block = ctx.enter_context(nc.Block(name="conv"))

        @block.sync
        def _(sp):
            sp.wait_ge(fixed, 1)
            loads = [(ident[:, :], d["ident"]), (w1[0:C, :, :], d["w1T"])]
            loads += [(e[n], d[f"bn1_{n}"].partition_broadcast(C)) for n in "gbmv"]
            loads += [(w2[0:CH, k, 0:C], d["w2T"][CH * k:CH * k + CH, :]) for k in range(CHUNKS)]
            loads += [(q[n][:, :], d[f"bn2_{n}"].partition_broadcast(CH)) for n in "gv"]
            loads += [(c2[n][r:r + C, :], d[f"bn2_{n}"].rearrange("(c a) -> c a", a=1)) for n in "gbmv" for r in (0, ONE)]
            assert len(loads) == 19
            for dst, src in loads:
                sp.dma_start(dst, src).then_inc(w_loaded, 16)

            def load_half(b, hx, h):
                for j in range(PR):
                    slot, nth = place_of(j)
                    wait(sp, cut, PR * h + nth)
                    lo, hi = max(PH * j - 1, 0), min(PH * j + PH + 1, H)
                    off = lo - (PH * j - 1)
                    sp.dma_start(piece[slot][:, off:off + hi - lo, :],
                                 d["img_images"][:, b, lo:hi, HALF * hx:HALF * hx + SC]).then_inc(piece_loaded[slot], 16)

            def first():
                load_half(0, 0, 0)
                for s in range(LOADS):
                    sp.dma_start(mats[s][:, :, :], d["conv_mats"][s]).then_inc(mats_loaded[s], 16)

            def chunk(b, hx, c, last):
                k = number(b, hx, c)
                if not last:
                    for s in range(LOADS):
                        sp.wait_ge(unit_ready, UNITS * (2 * k + 1) + UNITS // LOADS * (s + 1))
                        sp.dma_start(mats[s][:, :, :], d["conv_mats"][LOADS * ((c + 1) % CHUNKS) + s])\
                            .then_inc(mats_loaded[s], 16)
                if c == 1 and more(b, hx):
                    load_half(b + hx, 1 - hx, 2 * b + hx + 1)
                if c == CHUNKS - 1:
                    sp.wait_ge(y_done, NSTEP * (k + 1))
                    for r in range(2):
                        sp.dma_start(d["out"][4 * b + 2 * hx + r], y[64 * r:64 * r + C, 0:H, :].rearrange("c y x -> c (y x)"))\
                            .then_inc(y_stored, 16)

            schedule(sp, first, chunk)
            sp.wait_ge(y_stored, 32 * HALVES + 32)

        @block.tensor
        def _(pe):
            pe.wait_ge(w_ready, 5)

            def bank_free(stage, j):
                wait(pe, unit_dve if j % 2 else unit_act, UNITS // 2 * stage + (j - 4) // 2 + 1)

            def emptied(stages):
                wait(pe, unit_act, UNITS // 2 * stages)
                wait(pe, unit_dve, UNITS // 2 * stages)

            def expand(stage, c):
                for j in range(UNITS):
                    bank_free(stage, j)
                    a, n = expand_at(j)
                    for p in range(a, a + n):
                        mm = nc.tensor.matmul(ring[j % 4][0:PIN, CH * (p - a):CH * (p - a) + CH],
                                              xp[:, p, :], w1[:, c, :], start=True, stop=True)
                    mm.then_inc(unit_ready, 1)

            def first():
                pe.wait_ge(ones_set, 2)
                expand(0, 0)

            def chunk(b, hx, c, last):
                k = number(b, hx, c)
                emptied(2 * k + 1)
                for j in range(UNITS):
                    if j % (UNITS // LOADS) == 0:
                        pe.wait_ge(mats_loaded[j // (UNITS // LOADS)], 16 * (k + 1))
                    bank_free(2 * k + 1, j)
                    for n in range(4):
                        ch = 4 * j + n
                        mm = nc.tensor.matmul(ring[j % 4][0:POUT, PATCHES * n:PATCHES * (n + 1)],
                                              mats[ch // TCH][:, ch % TCH, :], h1[0:PIN + 1, ch, :], start=True, stop=True)
                    mm.then_inc(unit_ready, 1)
                if not last:
                    if c == CHUNKS - 1:
                        pe.wait_ge(ones_set, 2 * (2 * b + hx + 2))
                    expand(2 * k + 2, (c + 1) % CHUNKS)
                emptied(2 * k + 2)
                for n in range(NSTEP + 1):
                    if n < NSTEP:
                        pc, a, m = STEPS[n]
                        for r in range(2):
                            if n >= 1:
                                pe.wait_ge(copied_dve if r else copied_act, NSTEP * k + n)
                            for p in range(m):
                                patch = PR * (pc + PC // 2 * r) + a + p
                                mm = nc.tensor.transpose(ps_t[r][0:CH, POUT * p:POUT * (p + 1)], h2[:, patch, :],
                                                         ident[0:POUT, 0:POUT])
                            mm.then_inc(turned, 1)
                    if n >= 1:
                        m = STEPS[n - 1][2]
                        pe.wait_ge(copied_act, NSTEP * k + n)
                        pe.wait_ge(copied_dve, NSTEP * k + n)
                        if n >= 3:
                            pe.wait_ge(y_done, NSTEP * k + n - 2)
                        for r in range(2):
                            mm = nc.tensor.matmul(ps_y[(n - 1) % 2][64 * r:64 * r + 64, 0:POUT * m], w2[:, c, :],
                                                  h2T[(n - 1) % 2][r][:, 0:POUT * m], start=True, stop=True)
                        mm.then_inc(y_ready, 1)

            schedule(pe, first, chunk)

        @block.scalar
        def _(act):
            act.wait_ge(fixed, 1)
            act.wait_ge(w_loaded, 16 * 19)
            nc.scalar.activation(e["t"], e["v"], ACT.Sqrt, bias=eps[0:C, :]).then_inc(root, 1)
            nc.scalar.activation(q["t"][:, :], q["v"][:, :], ACT.Sqrt, bias=eps[0:CH, :]).then_inc(root, 1)
            nc.scalar.activation(c2["t"][:, :], c2["v"][:, :], ACT.Sqrt, bias=eps[:, :]).then_inc(root, 1)

            def units(k2, expand):
                for j in range(0, UNITS, 2):
                    act.wait_ge(unit_ready, UNITS * k2 + j + 1)
                    evacuate(True, j, expand).then_inc(unit_act, 1)

            def chunk(b, hx, c, last):
                k = number(b, hx, c)
                units(2 * k + 1, False)
                if not last:
                    units(2 * k + 2, True)
                for n in range(NSTEP):
                    m = STEPS[n][2]
                    act.wait_ge(turned, 2 * (NSTEP * k + n) + 1)
                    nc.scalar.activation(h2T[n % 2][0][0:CH, 0:POUT * m], ps_t[0][0:CH, 0:POUT * m], ACT.Copy)\
                        .then_inc(copied_act, 1)

            schedule(act, lambda: units(0, True), chunk)

        @block.vector
        def _(dve):
            nc.vector.memset(y[:, :, :], 0.0).then_inc(y_stored, 32)
            for t in (w1, w2, xp, *piece, *c2.values(), *h2T[0], *h2T[1]):
                nc.vector.memset(t[...], 0.0)
            nc.vector.memset(h1[96:P, :, :], 1.0)
            nc.vector.memset(eps[:, :], EPS).then_inc(fixed, 1)
            dve.wait_ge(fixed, 1)
            nc.vector.memset(xp[ONE:ONE + 1, :, :], 1.0).then_inc(fixed, 1)
            dve.wait_ge(fixed, 2)
            dve.wait_ge(root, 3)
            for t, v in ((e, 1), (q, 1), (c2, 1)):
                last = nc.vector.reciprocal(t["v"][...], t["t"][...])
            last.then_inc(w_ready, 1)
            dve.wait_ge(w_ready, 1)
            for t in (e, q, c2):
                last = nc.vector.tensor_tensor(t["t"][...], t["v"][...], t["g"][...], ALU.mult)
            last.then_inc(w_ready, 1)
            dve.wait_ge(w_ready, 2)
            for t in (e, c2):
                nc.vector.tensor_tensor(t["m"][...], t["m"][...], t["t"][...], ALU.mult)
            nc.vector.tensor_tensor(w1[0:C, :, :], w1[0:C, :, :], e["t"], ALU.mult)
            nc.vector.tensor_tensor(w2[0:CH, :, 0:C], w2[0:CH, :, 0:C], bc(q["t"][:, :], 1, CHUNKS), ALU.mult)\
                .then_inc(w_ready, 1)
            dve.wait_ge(w_ready, 3)
            for t in (e, c2):
                last = nc.vector.tensor_tensor(t["b"][...], t["b"][...], t["m"][...], ALU.subtract)
            last.then_inc(w_ready, 1)
            dve.wait_ge(w_ready, 4)
            nc.vector.tensor_copy(w1[ONE:ONE + 1, :, :], h1[0:1, CHUNKS:2 * CHUNKS, 0:CH]).then_inc(w_ready, 1)

            def cut_piece(j, h):
                slot, _ = place_of(j)
                dve.wait_ge(piece_loaded[slot], 16 * (PER_HALF[slot] * h + nth_in_slot(j) + 1))
                src = piece[slot][:, :, :]
                src = bass.AP(src.tensor, src.offset, [list(src.ap[0]), [PW, PC], [SC, PH + 2], [1, PW + 2]])
                dst = xp[0:C, :, :].rearrange("k (c j) (r x) -> k j c r x", j=PR, x=PW + 2)[:, j]
                nc.vector.tensor_copy(dst, src).then_inc(cut, 1)

            def place_ones(hx, h):
                ones = xp[ONE:ONE + 1, :, :].rearrange("k (c j) (r x) -> k c j r x", j=PR, x=PW + 2)
                for pc, x, out in ((0, 0, hx == 0), (PC - 1, PW + 1, hx == 1)):
                    last = nc.vector.memset(ones[:, pc, :, :, x], 0.0 if out else 1.0)
                last.then_inc(ones_set, 1)
                dve.wait_ge(ones_set, 2 * h + 1)
                nc.vector.memset(ones[:, :, 0, 0, :], 0.0)
                nc.vector.memset(ones[:, :, PR - 1, H - PH * (PR - 1) + 1:, :], 0.0).then_inc(ones_set, 1)

            def units(k2, expand):
                for j in range(1, UNITS, 2):
                    dve.wait_ge(unit_ready, UNITS * k2 + j + 1)
                    evacuate(False, j, expand).then_inc(unit_dve, 1)

            def add(n, b, hx, c, k):
                pc, a, m = STEPS[n]
                dve.wait_ge(y_ready, NSTEP * k + n + 1)
                rows = slice(PH * a, PH * (a + m))
                cols = slice(PW * pc, PW * pc + PW)
                dst = y[:, rows, cols]
                src = ps_y[n % 2][:, 0:POUT * m].rearrange("q (r x) -> q r x", x=PW)
                if c == 0:
                    if n == 0:
                        dve.wait_ge(y_stored, 32 * (2 * b + hx) + 32)
                    for r in range(2):
                        t = slice(64 * r, 64 * r + C)
                        p0 = PR * (pc + PC // 2 * r) + a
                        x = xp[0:C, p0:p0 + m, :].rearrange("k j (r x) -> k j r x", x=PW + 2)[:, :, 1:PH + 1, 1:PW + 1]
                        last = nc.vector.tensor_tensor(
                            y[t, rows, cols].rearrange("q (j r) x -> q j r x", j=m),
                            ps_y[n % 2][t, 0:POUT * m].rearrange("q (j r x) -> q j r x", j=m, x=PW), x, ALU.add)
                    last.then_inc(y_done, 1)
                elif c == CHUNKS - 1:
                    nc.vector.scalar_tensor_tensor(dst, src, c2["b"][:, 0:1], dst, ALU.add, ALU.add).then_inc(y_done, 1)
                else:
                    nc.vector.tensor_tensor(dst, src, dst, ALU.add).then_inc(y_done, 1)

            def chunk(b, hx, c, last):
                k = number(b, hx, c)
                units(2 * k + 1, False)
                if not last:
                    units(2 * k + 2, True)
                for n in range(NSTEP + 1):
                    if n < NSTEP:
                        m = STEPS[n][2]
                        dve.wait_ge(turned, 2 * (NSTEP * k + n) + 2)
                        nc.vector.tensor_copy(h2T[n % 2][1][0:CH, 0:POUT * m], ps_t[1][0:CH, 0:POUT * m])\
                            .then_inc(copied_dve, 1)
                    if n >= 1:
                        add(n - 1, b, hx, c, k)
                    if c == 1 and more(b, hx):
                        cut_piece(n, 2 * b + hx + 1)
                if c == 1 and more(b, hx):
                    place_ones(1 - hx, 2 * b + hx + 1)

            def first():
                for j in range(PR):
                    cut_piece(j, 0)
                place_ones(0, 0)
                units(0, True)

            assert NSTEP + 1 == PR
            schedule(dve, first, chunk)


def block_program(nc, d):
    d["mid_strips"] = d["tok_mid"].rearrange("(j k) q e -> j q k e", k=2)
    d["tok_mid"] = d["tok_mid"].rearrange("g q (p e) -> g q p e", e=MID)
    d["img_strips"] = d["img_mid"].rearrange("c (j r) x -> c j r x", r=WS)
    d["img_images"] = d["img_mid"].rearrange("c (b y) x -> c b y x", b=B)
    prepare_conv(nc, d)
    prepare_bias(nc, d)
    attention(nc, d)
    mlp(nc, d)
    conv(nc, d)


def tap_places():
    places = np.zeros((TAPROW + 1, POUT, P), np.float32)
    for r in range(PH):
        for c in range(PW):
            for t in range(9):
                places[t, r * PW + c, (r + t // 3) * (PW + 2) + c + t % 3] = 1
    places[TAPROW, :, PIN] = 1
    return places


def head_mask():
    mask = np.zeros((P, NH), np.float32)
    for h in range(NH):
        mask[ONE + HD * h:ONE + HD * (h + 1), h] = 1
    return mask


def kernel(**inputs):
    from concourse.bacc import Bacc
    from concourse.bass_utils import run_bass_kernel_spmd

    L0 = lambda n: np.asarray(inputs["L0_conv_" + n])
    L1 = lambda n: np.asarray(inputs["L1_conv_" + n])
    x = np.asarray(inputs["x"])
    groups = x.reshape(B, C, H // WS, WS, W // GW, GW // WS, WS).transpose(0, 2, 4, 1, 5, 3, 6)
    arrays = {
        "x_groups": groups.reshape(GROUPS, C, TOK),
        "n1_g": L0("norm1_g").reshape(C, 1), "n1_b": L0("norm1_b").reshape(C, 1),
        "qkv_wT": L0("qkv_w").T, "qkv_b": L0("qkv_b").reshape(1, 3 * C),
        "table": L0("rpb_table"), "rel_idx": L0("rel_idx").reshape(NT * NT),
        "proj_wT": L0("proj_w").T, "proj_b": L0("proj_b").reshape(1, C),
        "n2_g": L0("norm2_g").reshape(C, 1), "n2_b": L0("norm2_b").reshape(C, 1),
        "fc1_wT": L0("fc1_w").T, "fc1_b": L0("fc1_b").reshape(HID0, 1),
        "fc2_wT": L0("fc2_w").T, "fc2_b": L0("fc2_b").reshape(C, 1),
        "w1T": L1("w1").T, "wd": L1("wd").reshape(HID1, 9).T, "w2T": L1("w2").T,
        "ident": np.eye(P, dtype=np.float32), "headmask": head_mask(), "places": tap_places(),
        "number": np.arange(2 * P, dtype=np.float32).reshape(2, P).T,
    }
    for k, bn in (("1", "bn1"), ("2", "bn2")):
        for n in "gbmv":
            arrays[f"{bn}_{n}"] = L1(n + k)
    for n in ("gd", "bd", "md", "vd"):
        arrays[n] = L1(n)
    arrays = {f"in_{n}": np.ascontiguousarray(a) for n, a in arrays.items()}

    nc = Bacc("TRN2", target_bir_lowering=False, num_devices=1)
    d = {n[3:]: nc.dram_tensor(n, a.shape, mybir.dt.from_np(a.dtype), kind="ExternalInput").ap() for n, a in arrays.items()}
    halves = (B, W // HALF, 2, C, H, HALF // 2)
    for n, shape in (("conv_mats", (HID1 // TCH, PIN + 1, TCH, POUT)), ("rel_bias", (NT, NH * NT)),
                     ("tok_mid", (GROUPS, P, PAIRS * MID)), ("img_mid", (C, B * H, W + 2))):
        d[n] = nc.dram_tensor(n, shape, F32, kind="Internal").ap()
    d["out"] = nc.dram_tensor("out", (B * 4, C, H * HALF // 2), F32, kind="ExternalOutput").ap()
    block_program(nc, d)
    got = run_bass_kernel_spmd(nc, [arrays], core_ids=[0]).results[0]["out"]
    return got.reshape(halves).transpose(0, 3, 4, 1, 2, 5).reshape(B, C, H, W)
```

```python
from contextlib import ExitStack

import numpy as np

import concourse.bass as bass
from concourse import mybir

F32 = mybir.dt.float32
I32 = mybir.dt.int32
ALU = mybir.AluOpType
ACT = mybir.ActivationFunctionType
AX_X = mybir.AxisListType.X

P = 128
B, C, H, W = 4, 48, 128, 128
WS, NH = 8, 4
HD = C // NH
NT = WS * WS
EPS = 1e-5
ONE = 64

GW = 64
PAIRS = GW // (2 * WS)
TOK = PAIRS * 2 * NT
GROUPS = B * (H // WS) * (W // GW)
VB = 2 * 2 * (HD + 1)
NB = 96
MID = 112
HID0 = 4 * C

HID1 = 288
PH, PW = 10, 8
PIN, POUT = (PH + 2) * (PW + 2), PH * PW
PC, PR = 8, 13
PATCHES = PC * PR
HALF = PC * PW
SC = HALF + 2
CH = 96
CHUNKS = HID1 // CH
TCH = 32
LOADS = CH // TCH
TAPROW = 32
HALVES = B * 2
STRIPS = GROUPS // 2
UNITS = 24


def wait(eng, sem, n):
    if not isinstance(n, int) or n >= 1:
        eng.wait_ge(sem, n)


def bc(ap, axis, n):
    a = ap.unsqueeze(axis)
    shape = list(a.shape)
    shape[axis] = n
    return a.broadcast_to(shape)


def prepare_tables(nc, d, block, scratch, psum, kb):
    rows = d["table"].shape[0]
    half = POUT // 2
    ctx = ExitStack()
    sb = lambda n, s, t=F32: ctx.enter_context(nc.sbuf_tensor(n, s, t))
    sem = lambda n: ctx.enter_context(nc.semaphore(n))
    ids = sb("ids", [P, NT * NT], I32)
    table, number = sb("table", [P, 2, NH]), sb("number", [P, 2])
    taps = sb("taps", [P, HID1])
    gd, vd, md, bd = (sb(n, [TAPROW + 1, HID1]) for n in ("gd", "vd", "md", "bd"))
    sd, shift = sb("sd", [TAPROW + 1, HID1]), sb("shift", [TAPROW + 1, HID1])
    eps = sb("eps_d", [P, 1])
    size = [POUT * P, CH * POUT]
    places = scratch[:, 0:size[0]].rearrange("q (o i) -> q o i", o=POUT)
    onehot = scratch[:, size[0]:size[0] + 2 * NT * NT].rearrange("q (t n) -> q t n", t=2)
    idsf = scratch[:, size[0] + 2 * NT * NT:size[0] + 3 * NT * NT]
    bias = idsf[0:NH, :]
    mats = [scratch[:, size[0] + size[1] * k:size[0] + size[1] * (k + 1)].rearrange("q (c o) -> q c o", o=POUT)
            for k in range(2)]
    cleared, loaded, ids_loaded, cast = sem("t_cleared"), sem("t_loaded"), sem("ids_loaded"), sem("ids_cast")
    hot, looked_up, copied, stored, kb_loaded = (
        sem(n) for n in ("hot", "looked_up", "b_copied", "b_stored", "kb_loaded"))
    root, scaled = sem("d_root"), sem("d_scaled")
    mat_ready, copied_v, copied_a = sem("mat_ready"), sem("mat_cv"), sem("mat_ca")
    mats_stored = [sem(f"mat_stored{k}") for k in range(2)]
    K = TAPROW + 1
    UNIT = 4
    NU = POUT // UNIT
    BLOCKS = NT * NT // 512
    T_LOADS = 6

    @block.gpsimd
    def _(pool):
        for n, (t, value) in enumerate(((eps[:, :], EPS), (taps[:, :], 0.0), (places, 0.0))):
            nc.gpsimd.memset(t, value).then_inc(cleared, 1)
            pool.wait_ge(cleared, n + 1)

    @block.sync
    def _(sp):
        for dst, src in ((ids[:, :], d["rel_idx"].partition_broadcast(P)), (number[:, :], d["number"]),
                         (table[:, 0, :], d["table"][0:P, :]), (table[0:rows - P, 1, :], d["table"][P:rows, :])):
            sp.dma_start(dst, src).then_inc(ids_loaded, 16)
        for t, n in ((gd, "gd"), (vd, "vd"), (md, "md"), (bd, "bd")):
            sp.dma_start(t[:, :], d[n].partition_broadcast(K)).then_inc(loaded, 16)
        sp.wait_ge(cleared, 3)
        sp.dma_start(taps[0:9, :], d["wd"]).then_inc(loaded, 16)
        sp.dma_start(places[0:K, :, :], d["places"]).then_inc(loaded, 16)
        sp.wait_ge(copied, BLOCKS)
        sp.dma_start(d["rel_bias"], bias).then_inc(stored, 16)
        sp.wait_ge(stored, 16)
        for s in range(2):
            for h in range(NH):
                src = d["rel_bias"][h].rearrange("(n m) -> n m", m=NT)
                sp.dma_start(kb[s][0:NT, :, h, :], bc(src, 1, 2 * PAIRS)).then_inc(kb_loaded, 16)
        for c in range(CHUNKS):
            sp.wait_ge(copied_v, NU // 2 * (c + 1))
            sp.wait_ge(copied_a, NU // 2 * (c + 1))
            for u in range(LOADS):
                sp.dma_start(d["conv_mats"][LOADS * c + u], mats[c % 2][0:PIN + 1, TCH * u:TCH * u + TCH, :])\
                    .then_inc(mats_stored[c % 2], 16)

    def mats_free(eng, c):
        if c == 1:
            eng.wait_ge(stored, 16)
        if c >= 2:
            eng.wait_ge(mats_stored[c % 2], 16 * LOADS * (c // 2))

    @block.vector
    def _(dve):
        dve.wait_ge(ids_loaded, 64)
        nc.vector.tensor_copy(idsf, ids[:, :]).then_inc(cast, 1)
        dve.wait_ge(cast, 1)
        for t in range(2):
            nc.vector.tensor_scalar(onehot[:, t, :], idsf, number[:, t:t + 1], None, ALU.is_equal).then_inc(hot, 1)
        dve.wait_ge(root, 1)
        nc.vector.reciprocal(vd[:, :], sd[:, :]).then_inc(scaled, 1)
        dve.wait_ge(scaled, 1)
        nc.vector.tensor_tensor(sd[:, :], vd[:, :], gd[:, :], ALU.mult).then_inc(scaled, 1)
        dve.wait_ge(scaled, 2)
        nc.vector.tensor_tensor(md[:, :], md[:, :], sd[:, :], ALU.mult).then_inc(scaled, 1)
        nc.vector.tensor_tensor(taps[0:9, :], taps[0:9, :], sd[0:9, :], ALU.mult).then_inc(scaled, 1)
        dve.wait_ge(scaled, 4)
        nc.vector.tensor_tensor(shift[:, :], bd[:, :], md[:, :], ALU.subtract).then_inc(scaled, 1)
        dve.wait_ge(scaled, 5)
        nc.vector.tensor_copy(taps[TAPROW:K, :], shift[0:1, :]).then_inc(scaled, 1)
        for j in range(0, BLOCKS, 2):
            dve.wait_ge(looked_up, j + 1)
            nc.vector.tensor_copy(bias[:, 512 * j:512 * j + 512], psum[0:NH, j, :]).then_inc(copied, 1)
        for c in range(CHUNKS):
            mats_free(dve, c)
            for u in range(NU * c, NU * (c + 1), 2):
                dve.wait_ge(mat_ready, u + 1)
                j = UNIT * (u % NU)
                nc.vector.tensor_copy(mats[c % 2][0:PIN + 1, :, j:j + UNIT].rearrange("q c o -> q o c"),
                                      psum[0:PIN + 1, u % 8, 0:UNIT * CH].rearrange("q (o c) -> q o c", c=CH)).then_inc(copied_v, 1)

    @block.scalar
    def _(act):
        act.wait_ge(loaded, 16 * T_LOADS)
        act.wait_ge(cleared, 1)
        nc.scalar.activation(sd[:, :], vd[:, :], ACT.Sqrt, bias=eps[0:K, :]).then_inc(root, 1)
        for j in range(1, BLOCKS, 2):
            act.wait_ge(looked_up, j + 1)
            nc.scalar.activation(bias[:, 512 * j:512 * j + 512], psum[0:NH, j, :], ACT.Copy).then_inc(copied, 1)
        for c in range(CHUNKS):
            mats_free(act, c)
            for u in range(NU * c + 1, NU * (c + 1), 2):
                act.wait_ge(mat_ready, u + 1)
                j = UNIT * (u % NU)
                nc.scalar.activation(mats[c % 2][0:PIN + 1, :, j:j + UNIT].rearrange("q c o -> q o c"),
                                     psum[0:PIN + 1, u % 8, 0:UNIT * CH].rearrange("q (o c) -> q o c", c=CH), ACT.Copy)\
                    .then_inc(copied_a, 1)

    @block.tensor
    def _(pe):
        pe.wait_ge(ids_loaded, 64)
        pe.wait_ge(hot, 2)
        for j in range(BLOCKS):
            for t, k in enumerate((P, rows - P)):
                mm = nc.tensor.matmul(psum[0:NH, j, :], table[0:k, t, :], onehot[0:k, t, 512 * j:512 * j + 512],
                                      start=(t == 0), stop=(t == 1))
            mm.then_inc(looked_up, 1)
        pe.wait_ge(loaded, 16 * T_LOADS)
        pe.wait_ge(scaled, 6)
        pe.wait_ge(copied, BLOCKS)
        for u in range(CHUNKS * NU):
            if u >= 8:
                pe.wait_ge(copied_a if u % 2 else copied_v, (u - 8) // 2 + 1)
            c, j = u // NU, UNIT * (u % NU)
            for k in range(UNIT):
                mm = nc.tensor.matmul(psum[0:PIN + 1, u % 8, CH * k:CH * k + CH], places[:, j + k, 0:PIN + 1],
                                      taps[:, CH * c:CH * c + CH], start=True, stop=True)
            mm.then_inc(mat_ready, 1)
        pe.wait_ge(copied_a, NU // 2 * CHUNKS)
        pe.wait_ge(copied_v, NU // 2 * CHUNKS)

    return ctx, kb_loaded, mats_stored


def attention(nc, d):
    with ExitStack() as ctx:
        sb = lambda n, s, t=F32: ctx.enter_context(nc.sbuf_tensor(n, s, t))
        sem = lambda n: ctx.enter_context(nc.semaphore(n))
        ident = sb("ident", [P, P])
        headmask = sb("headmask", [P, NH])
        eps = sb("eps", [P, 1])
        w_qk = sb("w_qk", [P, 112])
        w_v, w_o = sb("w_v", [P, NB]), sb("w_o", [P, NB])
        qkv_w, qkv_b = sb("qkv_w", [C, 3 * C]), sb("qkv_b", [1, 3 * C])
        lnrow = sb("lnrow", [1, 3 * C])
        ln_g, ln_b = sb("ln_g", [C, 1]), sb("ln_b", [C, 1])
        xs = [sb(f"xs{s}", [C, TOK]) for s in range(2)]
        scratch = sb("scratch", [P, POUT * P + 2 * CH * POUT])
        xtok = scratch[:, 0:GROUPS * PAIRS * C].rearrange("q (g p c) -> q g p c", g=GROUPS, p=PAIRS)
        sums, sq_sums, lnv, rstd = ([sb(f"{n}{s}", [P, PAIRS]) for s in range(2)] for n in ("sum", "sqs", "lnv", "rstd"))
        sums2, sq_sums2, lnv2, rstd2 = ([sb(f"{n}{s}", [P, PAIRS]) for s in range(2)] for n in ("sumb", "sqsb", "lnvb", "rstdb"))
        cen = [sb(f"cen{s}", [P, PAIRS, C]) for s in range(2)]
        cen2 = [sb(f"cenb{s}", [P, PAIRS, C]) for s in range(2)]
        sq, sq2 = sb("sq", [P, PAIRS, C]), sb("sqb", [P, PAIRS, C])
        xn = [sb(f"xn{s}", [P, PAIRS, C]) for s in range(2)]
        xnT = [sb(f"xnT{s}", [P, TOK]) for s in range(2)]
        qa = [sb(f"qa{s}", [P, TOK]) for s in range(2)]
        ks = sb("ks", [P, TOK])
        kb = [sb(f"kb{s}", [P, 2 * PAIRS, NH, NT]) for s in range(2)]
        vb = [sb(f"vb{s}", [P, 2 * PAIRS * VB + NB - VB]) for s in range(2)]
        top = [sb(f"top{s}", [P, PAIRS * NH]) for s in range(2)]
        prob = [sb(f"prob{s}", [P, PAIRS * NH, NT]) for s in range(2)]
        probT = sb("probT", [P, PAIRS, 2, P])
        rden = sb("rden", [P, 2 * PAIRS, 2])
        o = sb("o", [P, PAIRS, C])
        oT = sb("oT", [P, TOK])
        mid = [sb(f"mid{s}", [P, PAIRS, MID]) for s in range(2)]

        psum = ctx.enter_context(nc.psum_tensor("psum1", [P, 8, 512], F32))
        ps_s = psum[:, 0:2, :]
        ps_p = psum[:, 2:4, :]
        ps_x = psum[:, 4, :]
        ps_t = psum[:, 5, :]
        ps_k = psum[:, 6, :]
        ps_v = psum[:, 7, :]

        w_loaded, fixed, w_bias, w_ready = sem("w_loaded"), sem("fixed"), sem("w_bias"), sem("w_ready")
        ident_put = sem("ident_put")
        x_loaded = [sem(f"x_loaded{s}") for s in range(2)]
        stored = [sem(f"mid_stored{s}") for s in range(2)]
        x_turned, x_copied, sum_done, cen_done, sq_done, var_done, ln_done, rstd_done, xn_done = (
            sem(n) for n in ("x_turned", "x_copied", "sum_done", "cen_done", "sq_done", "var_done", "ln_done",
                             "rstd_done", "xn_done"))
        xnT_ready, xnT_copied, qk_ready, k_copied, q_copied, kb_done = (
            sem(n) for n in ("xnT_ready", "xnT_copied", "qk_ready", "k_copied", "q_copied", "kb_done"))
        v_ready, v_copied, s_ready, top_done, sub_done, exp_done = (
            sem(n) for n in ("v_ready", "v_copied", "s_ready", "top_done", "sub_done", "exp_done"))
        pT_ready, pT_copied, o_ready, rden_done, o_done, oT_ready, oT_copied, y_ready, res_done = (
            sem(n) for n in ("pT_ready", "pT_copied", "o_ready", "rden_done", "o_done", "oT_ready", "oT_copied",
                             "y_ready", "res_done"))
        sum2_done, cen2_done, sq2_done, var2_done, ln2_done, rstd2_done, mid_done = (
            sem(n) for n in ("sum2_done", "cen2_done", "sq2_done", "var2_done", "ln2_done", "rstd2_done", "mid_done"))

        W_LOADS = 8
        W_FIXED, FIXED = 3, 26
        def has(g):
            return not isinstance(g, int) or 0 <= g < GROUPS

        def schedule(eng, step):
            for i in range(-2, 6):
                step(i, i % 2)
            with eng.Fori(6, GROUPS - 5, 2) as i:
                step(i, 0)
                step(i + 1, 1)
            for i in range(GROUPS - 4, GROUPS + 3):
                step(i, i % 2)

        block = ctx.enter_context(nc.Block(name="attention"))

        @block.gpsimd
        def _(pool):
            constants = [(t[...], 0.0) for t in (w_qk, w_v, w_o)]
            LOADED_INTO = len(constants)
            constants += [(t[...], 0.0) for t in (xnT[0], xnT[1], oT, qa[0], qa[1], vb[0], vb[1], kb[0], kb[1], mid[0], mid[1])]
            constants += [(eps[:, :], EPS)] + [(t[ONE:ONE + 1, :], 1.0) for t in (xnT[0], xnT[1], oT)]
            for s in range(2):
                v5 = vb[s][:, 0:2 * PAIRS * VB].rearrange("q (b w h e) -> q b w h e", w=2, h=2, e=HD + 1)
                constants += [(v5[NT * h:NT * h + NT, :, w, h, HD:HD + 1], 1.0) for h in range(2) for w in range(2)]
            for n, (t, value) in enumerate(constants):
                nc.gpsimd.memset(t, value).then_inc(fixed, 1)
                pool.wait_ge(fixed, n + 1)
            assert (LOADED_INTO, len(constants)) == (W_FIXED, FIXED)

        @block.scalar
        def _(act):
            act.wait_ge(fixed, W_FIXED)
            for dst, src in ((ident[:, :], d["ident"]), (headmask[:, :], d["headmask"]), (qkv_w[:, :], d["qkv_wT"]),
                             (qkv_b[:, :], d["qkv_b"]), (ln_g[:, :], d["n1_g"]), (ln_b[:, :], d["n1_b"]),
                             (w_o[0:C, 0:C], d["proj_wT"]), (w_o[ONE:ONE + 1, 0:C], d["proj_b"])):
                act.dma_start(dst, src).then_inc(w_loaded, 16)
            for s in range(2):
                act.dma_start(xs[s][:, :], d["x_groups"][s]).then_inc(x_loaded[s], 16)

        @block.vector
        def _(dve):
            dve.wait_ge(fixed, FIXED)
            dve.wait_ge(w_loaded, 16 * W_LOADS)
            for s in range(2):
                last = nc.vector.tensor_copy(qa[s][0:NT, :].rearrange("q (n t) -> q n t", n=2 * PAIRS),
                                             bc(ident[0:NT, 0:NT], 1, 2 * PAIRS))
            last.then_inc(ident_put, 1)
            nc.vector.tensor_scalar(w_qk[0:C, 0:C], qkv_w[:, 0:C], ln_g[:, 0:1], HD ** -0.5, ALU.mult, ALU.mult)\
                .then_inc(w_ready, 1)
            nc.vector.tensor_scalar(w_qk[0:C, ONE:ONE + C], qkv_w[:, C:2 * C], ln_g[:, 0:1], None, ALU.mult)\
                .then_inc(w_ready, 1)
            nc.vector.tensor_scalar(w_v[0:C, 0:C], qkv_w[:, 2 * C:3 * C], ln_g[:, 0:1], None, ALU.mult)\
                .then_inc(w_ready, 1)
            dve.wait_ge(w_bias, 1)
            nc.vector.tensor_tensor(lnrow[:, :], ps_x[0:1, 0:3 * C], qkv_b[:, :], ALU.add).then_inc(fixed, 1)
            dve.wait_ge(fixed, FIXED + 1)
            one = slice(ONE, ONE + 1)
            nc.vector.tensor_scalar(w_qk[one, 0:C], lnrow[:, 0:C], HD ** -0.5, None, ALU.mult).then_inc(w_ready, 1)
            nc.vector.tensor_copy(w_qk[one, ONE:ONE + C], lnrow[:, C:2 * C]).then_inc(w_ready, 1)
            nc.vector.tensor_copy(w_v[one, 0:C], lnrow[:, 2 * C:3 * C]).then_inc(w_ready, 1)

        @block.tensor
        def _(pe):
            pe.wait_ge(w_loaded, 16 * W_LOADS)
            nc.tensor.matmul(ps_x[0:1, 0:3 * C], ln_b[:, :], qkv_w[:, :], start=True, stop=True).then_inc(w_bias, 1)

        tables, kb_loaded, mats_stored = prepare_tables(nc, d, block, scratch, psum, kb)
        ctx.enter_context(tables)

        @block.sync
        def _(sp):
            def load(g, s):
                if has(g):
                    wait(sp, x_turned, g - 1)
                    sp.dma_start(xs[s][:, :], d["x_groups"][g]).then_inc(x_loaded[s], 16)

            def step(i, s):
                load(i + 4, s)
                if has(i - 3):
                    sp.wait_ge(mid_done, i - 2)
                    sp.dma_start(d["tok_mid"][i - 3], mid[1 - s][:, :, :]).then_inc(stored[1 - s], 16)

            schedule(sp, step)
            for s in range(2):
                sp.wait_ge(stored[s], 16 * (GROUPS // 2))

        @block.tensor
        def _(pe):
            pe.wait_ge(w_ready, 6)
            pe.wait_ge(ident_put, 1)
            pe.wait_ge(fixed, FIXED)
            pe.wait_ge(kb_loaded, 16 * 2 * NH)

            def step(i, s):
                if isinstance(i, int):
                    for sem, g in ((v_copied, i - 1), (oT_copied, i - 3), (xnT_copied, i), (res_done, i - 3),
                                   (x_copied, i + 1), (pT_copied, i - 2), (o_done, i - 2), (q_copied, i)):
                        if has(g):
                            pe.wait_ge(sem, g + 1)
                if has(i):
                    pe.wait_ge(q_copied, i + 1)
                    pe.wait_ge(kb_done, i + 1)
                    wait(pe, sub_done, i)
                    for n in range(2 * PAIRS):
                        if n == 2 * PAIRS - 2 and has(i + 1):
                            pe.wait_ge(xn_done, i + 2)
                            if has(i - 3):
                                pe.wait_ge(oT_copied, i - 2)
                        p, w = divmod(n, 2)
                        mm = nc.tensor.matmul(ps_s[NT * w:NT * w + NT, p // 2, 256 * (p % 2):256 * (p % 2) + 256],
                                              qa[s][:, NT * n:NT * n + NT], kb[s][:, n, :, :], start=True, stop=True)
                    mm.then_inc(s_ready, 1)
                elif has(i + 1):
                    pe.wait_ge(xn_done, i + 2)
                if has(i + 1):
                    for p in range(PAIRS):
                        mm = nc.tensor.transpose(ps_t[0:C, P * p:P * p + P], xn[1 - s][:, p, :], ident[:, :])
                    mm.then_inc(xnT_ready, 1)
                if has(i - 1):
                    pe.wait_ge(exp_done, i)
                    wait(pe, pT_copied, i - 1)
                    for p in range(PAIRS):
                        for h in range(2):
                            src = prob[1 - s][:, NH * p + 2 * h:NH * p + 2 * h + 2, :]
                            at = 256 * (p % 2) + P * h
                            mm = nc.tensor.transpose(ps_p[:, p // 2, at:at + P], src, ident[:, :])
                    mm.then_inc(pT_ready, 1)
                if has(i):
                    wait(pe, o_done, i - 1)
                if has(i + 2):
                    pe.wait_ge(x_loaded[s], 8 * (i + 2 - s) + 16)
                    wait(pe, res_done, i - 2)
                if has(i):
                    for p in range(PAIRS):
                        mm = nc.tensor.matmul(ps_v[:, C * p:C * p + NB], xnT[s][:, P * p:P * p + P], w_v[:, :],
                                              start=True, stop=True)
                    mm.then_inc(v_ready, 1)
                if has(i + 2):
                    for p in range(PAIRS):
                        mm = nc.tensor.transpose(ps_x[:, C * p:C * p + C], xs[s][:, P * p:P * p + P], ident[0:C, 0:C])
                    mm.then_inc(x_turned, 1)
                if has(i + 1):
                    pe.wait_ge(xnT_copied, i + 2)
                    wait(pe, q_copied, i + 1)
                if has(i - 2):
                    pe.wait_ge(o_done, i - 1)
                if has(i + 1):
                    nc.tensor.matmul(ps_k[0:112, :], w_qk[:, :], xnT[1 - s][:, :], start=True, stop=True)\
                        .then_inc(qk_ready, 1)
                if has(i - 2):
                    for p in range(PAIRS):
                        mm = nc.tensor.transpose(ps_t[0:C, P * p:P * p + P], o[:, p, :], ident[:, :])
                    mm.then_inc(oT_ready, 1)
                if has(i - 1):
                    pe.wait_ge(pT_copied, i)
                    if has(i):
                        pe.wait_ge(v_copied, i + 1)
                    for p in range(PAIRS):
                        for h in range(2):
                            at = VB * (2 * p + h)
                            mm = nc.tensor.matmul(ps_v[:, at:at + NB], probT[:, p, h, :], vb[1 - s][:, at:at + NB],
                                                  start=True, stop=True)
                    mm.then_inc(o_ready, 1)
                if has(i - 2):
                    pe.wait_ge(oT_copied, i - 1)
                    if has(i + 2):
                        pe.wait_ge(x_copied, i + 3)
                    for p in range(PAIRS):
                        mm = nc.tensor.matmul(ps_x[:, C * p:C * p + NB], oT[:, P * p:P * p + P], w_o[:, :],
                                              start=True, stop=True)
                    mm.then_inc(y_ready, 1)

            schedule(pe, step)

        @block.vector
        def _(dve):
            def step(i, s):
                if has(i - 2):
                    dve.wait_ge(o_ready, i - 1)
                    wait(dve, oT_ready, i - 2)
                    for w in range(2):
                        t = slice(NT * w, NT * w + NT)
                        v5 = ps_v[t, 0:2 * PAIRS * VB].rearrange("q (b w h e) -> q b w h e", w=2, h=2, e=HD + 1)
                        nc.vector.reciprocal(rden[t, :, :], v5[:, :, w, :, HD]).then_inc(rden_done, 1)
                    dve.wait_ge(rden_done, 2 * i - 2)
                    for w in range(2):
                        t = slice(NT * w, NT * w + NT)
                        v5 = ps_v[t, 0:2 * PAIRS * VB].rearrange("q (b w h e) -> q b w h e", w=2, h=2, e=HD + 1)
                        last = nc.vector.tensor_tensor(
                            o[t, :, :].rearrange("q p (a h e) -> q (p a) h e", a=2, h=2), v5[:, :, w, :, 0:HD],
                            bc(rden[t, :, :], 3, HD), ALU.mult)
                    last.then_inc(o_done, 1)
                if has(i - 3):
                    dve.wait_ge(y_ready, i - 2)
                    wait(dve, stored[1 - s], 8 * (i - 3 - (1 - s)))
                    x = xtok[:, bass.ds(i - 3, 1), :, :].rearrange("q g p c -> q (g p) c")
                    m = mid[1 - s][:, :, ONE:ONE + C]
                    nc.vector.tensor_tensor(m, ps_x[:, 0:PAIRS * C].rearrange("q (p c) -> q p c", c=C), x, ALU.add)\
                        .then_inc(res_done, 1)
                    dve.wait_ge(res_done, i - 2)
                    nc.vector.tensor_reduce(sums2[1 - s][:, :], m, AX_X, ALU.add).then_inc(sum2_done, 1)
                    dve.wait_ge(sum2_done, i - 2)
                    nc.vector.scalar_tensor_tensor(cen2[1 - s][:, :, :], bc(sums2[1 - s][:, :], 2, C), -1.0 / C, m,
                                                   ALU.mult, ALU.add).then_inc(cen2_done, 1)
                if has(i):
                    dve.wait_ge(s_ready, i + 1)
                    sc = ps_s[:, :, :].rearrange("q b (h m) -> q (b h) m", m=NT)
                    nc.vector.tensor_reduce(top[s][:, :], sc, AX_X, ALU.max).then_inc(top_done, 1)
                    dve.wait_ge(top_done, i + 1)
                    nc.vector.tensor_tensor(prob[s][:, :, :], sc, bc(top[s][:, :], 2, NT), ALU.subtract)\
                        .then_inc(sub_done, 1)
                if has(i + 2):
                    dve.wait_ge(x_copied, i + 3)
                    x = xtok[:, bass.ds(i + 2, 1), :, :].rearrange("q g p c -> q (g p) c")
                    nc.vector.tensor_reduce(sums[s][:, :], x, AX_X, ALU.add).then_inc(sum_done, 1)
                    dve.wait_ge(sum_done, i + 3)
                    nc.vector.scalar_tensor_tensor(cen[s][:, :, :], bc(sums[s][:, :], 2, C), -1.0 / C, x,
                                                   ALU.mult, ALU.add).then_inc(cen_done, 1)
                if has(i + 1):
                    dve.wait_ge(k_copied, i + 2)
                    for h in range(NH):
                        last = nc.vector.tensor_scalar(
                            kb[1 - s][ONE:ONE + C, :, h, :], ks[ONE:ONE + C, :].rearrange("q (n m) -> q n m", m=NT),
                            headmask[ONE:ONE + C, h:h + 1], None, ALU.mult)
                    last.then_inc(kb_done, 1)
                if has(i + 2):
                    dve.wait_ge(sq_done, i + 3)
                    nc.vector.tensor_reduce(sq_sums[s][:, :], sq[:, :, :], AX_X, ALU.add).then_inc(var_done, 1)
                if has(i - 3):
                    dve.wait_ge(sq2_done, i - 2)
                    nc.vector.tensor_reduce(sq_sums2[1 - s][:, :], sq2[:, :, :], AX_X, ALU.add).then_inc(var2_done, 1)

            schedule(dve, step)

        @block.scalar
        def _(act):
            nc.scalar.preload_act_table_set("natural_log_exp_and_others")

            def step(i, s):
                if has(i + 1):
                    act.wait_ge(xnT_ready, i + 2)
                    nc.scalar.activation(xnT[1 - s][0:C, :], ps_t[0:C, :], ACT.Copy).then_inc(xnT_copied, 1)
                if has(i - 1):
                    act.wait_ge(pT_ready, i)
                    nc.scalar.activation(probT[:, :, :, :].rearrange("q p h n -> q (p h n)"),
                                         ps_p[:, :, :].rearrange("q b n -> q (b n)"), ACT.Copy).then_inc(pT_copied, 1)
                if has(i):
                    act.wait_ge(v_ready, i + 1)
                    for h in range(2):
                        for w in range(2):
                            dst = vb[s][NT * h:NT * h + NT, 0:2 * PAIRS * VB].rearrange(
                                "q (b w h e) -> q b w h e", w=2, h=2, e=HD + 1)[:, :, w, h, 0:HD]
                            src = ps_v[NT * w:NT * w + NT, 0:PAIRS * C].rearrange("q (b h e) -> q b h e", h=2, e=HD)
                            last = nc.scalar.activation(dst, src[:, :, h, :], ACT.Copy)
                    last.then_inc(v_copied, 1)
                if has(i + 2):
                    if isinstance(i, int) and i == 5:
                        act.wait_ge(mats_stored[0], 16 * LOADS * 2)
                        act.wait_ge(mats_stored[1], 16 * LOADS)
                    act.wait_ge(x_turned, i + 3)
                    x = xtok[:, bass.ds(i + 2, 1), :, :].rearrange("q g p c -> q (g p c)")
                    nc.scalar.activation(x, ps_x[:, 0:PAIRS * C], ACT.Copy).then_inc(x_copied, 1)
                if has(i + 1):
                    act.wait_ge(qk_ready, i + 2)
                    wait(act, kb_done, i + 1)
                    nc.scalar.activation(ks[ONE:ONE + C, :], ps_k[ONE:ONE + C, :], ACT.Copy).then_inc(k_copied, 1)
                    nc.scalar.activation(qa[1 - s][ONE:ONE + C, :], ps_k[0:C, :], ACT.Copy).then_inc(q_copied, 1)
                if has(i - 2):
                    act.wait_ge(oT_ready, i - 1)
                    nc.scalar.activation(oT[0:C, :], ps_t[0:C, :], ACT.Copy).then_inc(oT_copied, 1)
                if has(i):
                    act.wait_ge(sub_done, i + 1)
                    nc.scalar.activation(prob[s][:, :, :], prob[s][:, :, :], ACT.Exp).then_inc(exp_done, 1)
                if has(i + 2):
                    act.wait_ge(var_done, i + 3)
                    nc.scalar.activation(lnv[s][:, :], sq_sums[s][:, :], ACT.Ln, bias=eps[:, :], scale=1.0 / C)\
                        .then_inc(ln_done, 1)
                    act.wait_ge(ln_done, i + 3)
                    nc.scalar.activation(rstd[s][:, :], lnv[s][:, :], ACT.Exp, scale=-0.5).then_inc(rstd_done, 1)
                if has(i - 3):
                    act.wait_ge(var2_done, i - 2)
                    nc.scalar.activation(lnv2[1 - s][:, :], sq_sums2[1 - s][:, :], ACT.Ln, bias=eps[:, :], scale=1.0 / C)\
                        .then_inc(ln2_done, 1)
                    act.wait_ge(ln2_done, i - 2)
                    nc.scalar.activation(rstd2[1 - s][:, :], lnv2[1 - s][:, :], ACT.Exp, scale=-0.5)\
                        .then_inc(rstd2_done, 1)

            schedule(act, step)

        @block.gpsimd
        def _(pool):
            def step(i, s):
                if has(i - 3):
                    pool.wait_ge(cen2_done, i - 2)
                    nc.gpsimd.tensor_tensor(sq2[:, :, :], cen2[1 - s][:, :, :], cen2[1 - s][:, :, :], ALU.mult)\
                        .then_inc(sq2_done, 1)
                if has(i + 2):
                    pool.wait_ge(cen_done, i + 3)
                    nc.gpsimd.tensor_tensor(sq[:, :, :], cen[s][:, :, :], cen[s][:, :, :], ALU.mult).then_inc(sq_done, 1)
                    pool.wait_ge(rstd_done, i + 3)
                    nc.gpsimd.tensor_tensor(xn[s][:, :, :], cen[s][:, :, :], bc(rstd[s][:, :], 2, C), ALU.mult)\
                        .then_inc(xn_done, 1)
                if has(i - 3):
                    pool.wait_ge(rstd2_done, i - 2)
                    nc.gpsimd.tensor_tensor(mid[1 - s][:, :, 0:C], cen2[1 - s][:, :, :], bc(rstd2[1 - s][:, :], 2, C),
                                            ALU.mult).then_inc(mid_done, 1)

            schedule(pool, step)



def mlp(nc, d, block, room, psum, stored, emptied):
    REST = HID0 - P
    with ExitStack() as ctx:
        used = [0]

        def sb(name, shape):
            size = int(np.prod(shape[1:]))
            at, used[0] = used[0], used[0] + size
            t = room[0:shape[0], at:at + size]
            if len(shape) == 2:
                return t
            axes = "abc"[:len(shape) - 1]
            return t.rearrange(f"q ({' '.join(axes)}) -> q {' '.join(axes)}", **dict(zip(axes, shape[1:])))

        sem = lambda n: ctx.enter_context(nc.semaphore(n))
        ident = sb("ident2", [P, P])
        fc1, bias_row = sb("fc1", [C, HID0]), sb("bias_row", [1, HID0])
        g, b = sb("g2", [C, 1]), sb("b2", [C, 1])
        w1 = sb("w1", [P, HID0])
        w2 = sb("w2", [P, NT])
        w2r = [sb(f"w2r{k}", [P, NT]) for k in range(2)]
        b1, b1r = sb("b1", [P, 1]), sb("b1r", [P, 1])
        b2c = sb("b2c", [P, 1])
        mid = [sb(f"midb{s}", [P, 2, PAIRS, MID]) for s in range(2)]
        lnT = [sb(f"lnT{s}", [P, 2, TOK]) for s in range(2)]
        xT = [sb(f"xT{s}", [P, TOK]) for s in range(2)]
        hid = [sb(f"hid{s}", [P, 3, TOK]) for s in range(2)]
        y = [sb(f"y{s}", [P, WS, GW + 2]) for s in range(2)]
        assert used[0] <= PATCHES * CH
        ps_t, ps_h, ps_y = psum[:, 0:2, :], psum[:, 2:5, :], psum[:, 5:7, :]
        fixed, w_loaded, w_bias, w_ready = sem("m_fixed"), sem("m_loaded"), sem("m_bias"), sem("m_ready")
        loaded = [sem(f"mid_loaded{s}") for s in range(2)]
        gelu_done, y_done = emptied
        turned, ln_copied, x_copied, hid_ready, y_ready = (
            sem(n) for n in ("m_turned", "m_ln_copied", "m_x_copied", "m_hid_ready", "m_y_ready"))

        def has(j):
            return not isinstance(j, int) or 0 <= j < STRIPS

        def schedule(eng, step):
            for j in range(-1, 4):
                step(j, j % 2)
            with eng.Fori(4, STRIPS - 5, 2) as j:
                step(j, 0)
                step(j + 1, 1)
            for j in range(STRIPS - 4, STRIPS + 1):
                step(j, j % 2)

        @block.sync
        def _(sp):
            sp.wait_ge(fixed, 1)
            for dst, src in ((ident[:, :], d["ident"]), (fc1[:, :], d["fc1_wT"]), (g[:, :], d["n2_g"]), (b[:, :], d["n2_b"]),
                             (w2[:, 0:C], d["fc2_wT"][0:P, :]), (w2r[0][0:REST, 0:C], d["fc2_wT"][P:HID0, :]),
                             (w2r[1][REST:P, 0:C], d["fc2_wT"][P:HID0, :]), (b1[:, :], d["fc1_b"][0:P, :]),
                             (b1r[0:REST, :], d["fc1_b"][P:HID0, :]), (b1r[REST:P, :], d["fc1_b"][P:HID0, :]),
                             (b2c[0:C, :], d["fc2_b"]), (b2c[ONE:ONE + C, :], d["fc2_b"])):
                sp.dma_start(dst, src).then_inc(w_loaded, 16)

            def load(j, s):
                if has(j):
                    wait(sp, turned, j - 1)
                    sp.dma_start(mid[s][:, :, :, :].rearrange("q k p e -> q k (p e)"),
                                 d["mid_strips"][j]).then_inc(loaded[s], 16)

            def step(j, s):
                load(j + 3, 1 - s)
                if has(j - 1):
                    sp.wait_ge(y_done, j)
                    for k in range(2):
                        x0 = (GW + 1) * k
                        sp.dma_start(d["img_strips"][:, j - 1, :, x0:x0 + GW + 1], y[1 - s][64 * k:64 * k + C, :, k:k + GW + 1])\
                            .then_inc(stored[1 - s], 16)

            load(0, 0)
            load(1, 1)
            schedule(sp, step)

        @block.tensor
        def _(pe):
            pe.wait_ge(w_loaded, 16 * 12)
            nc.tensor.matmul(ps_y[0:1, 0, 0:HID0], b[:, :], fc1[:, :], start=True, stop=True).then_inc(w_bias, 1)
            pe.wait_ge(w_ready, 2)

            def step(j, s):
                if has(j + 1):
                    pe.wait_ge(loaded[1 - s], 8 * (j + 1 - (1 - s)) + 16)
                    wait(pe, ln_copied, j + 1)
                    wait(pe, x_copied, j + 1)
                    for k in range(2):
                        for p in range(PAIRS):
                            mm = nc.tensor.transpose(ps_t[0:MID, k, P * p:P * p + P], mid[1 - s][:, k, p, :], ident[:, :])
                    mm.then_inc(turned, 1)
                if has(j - 1):
                    pe.wait_ge(gelu_done, 3 * j)
                    wait(pe, y_done, j - 2)
                    for half in range(2):
                        for k in range(2):
                            mm = nc.tensor.matmul(ps_y[64 * k:64 * k + 64, 1 - s, :], w2r[k][:, :] if half else w2[:, :],
                                                  hid[1 - s][:, 2 if half else k, :], start=(half == 0), stop=(half == 1))
                    mm.then_inc(y_ready, 1)
                if has(j):
                    pe.wait_ge(ln_copied, j + 1)
                    for k in range(2):
                        wait(pe, gelu_done, 3 * j - 2 + k)
                        nc.tensor.matmul(ps_h[:, k, :], w1[:, 0:P], lnT[s][:, k, :], start=True, stop=True)\
                            .then_inc(hid_ready, 1)
                    wait(pe, gelu_done, 3 * j)
                    for k in range(2):
                        mm = nc.tensor.matmul(ps_h[REST * k:REST * k + REST, 2, :], w1[:, P:HID0], lnT[s][:, k, :],
                                              start=True, stop=True)
                    mm.then_inc(hid_ready, 1)

            schedule(pe, step)

        @block.vector
        def _(dve):
            for t in (w1, w2, w2r[0], w2r[1], lnT[0], lnT[1], xT[0], xT[1], y[0], y[1]):
                nc.vector.memset(t[...], 0.0)
            nc.vector.memset(b2c[:, :], 0.0).then_inc(fixed, 1)
            dve.wait_ge(w_loaded, 16 * 12)
            dve.wait_ge(w_bias, 1)
            nc.vector.tensor_copy(bias_row[:, :], ps_y[0:1, 0, 0:HID0]).then_inc(w_ready, 1)
            nc.vector.tensor_scalar(w1[0:C, :], fc1[:, :], g[:, 0:1], None, ALU.mult)
            dve.wait_ge(w_ready, 1)
            nc.vector.tensor_copy(w1[ONE:ONE + 1, :], bias_row[:, :])
            for s in range(2):
                last = nc.vector.memset(lnT[s][ONE:ONE + 1, :, :], 1.0)
            last.then_inc(w_ready, 1)

            def step(j, s):
                if has(j - 1):
                    dve.wait_ge(x_copied, j)
                    dve.wait_ge(y_ready, j)
                    wait(dve, stored[1 - s], 16 * (j - 1 - (1 - s)))
                    px = lambda ap: ap.rearrange("q (n r c) -> q n r c", r=WS, c=WS)
                    nc.vector.tensor_tensor(y[1 - s][:, :, 1:GW + 1].rearrange("q r (n c) -> q n r c", c=WS),
                                            px(ps_y[:, 1 - s, :]), px(xT[1 - s][:, :]), ALU.add).then_inc(y_done, 1)
                if has(j + 1):
                    wait(dve, y_done, j)
                    dve.wait_ge(turned, j + 2)
                    for k in range(2):
                        r = slice(64 * k, 64 * k + C)
                        last = nc.vector.tensor_scalar(xT[1 - s][r, :], ps_t[ONE:ONE + C, k, :], b2c[r, 0:1], None, ALU.add)
                    last.then_inc(x_copied, 1)

            schedule(dve, step)

        @block.scalar
        def _(act):
            act.wait_ge(w_ready, 2)

            def step(j, s):
                if has(j + 1):
                    act.wait_ge(turned, j + 2)
                    nc.scalar.activation(lnT[1 - s][0:C, :, :].rearrange("q k t -> q (k t)"),
                                         ps_t[0:C, :, :].rearrange("q k t -> q (k t)"), ACT.Copy).then_inc(ln_copied, 1)
                if has(j):
                    for k in range(3):
                        act.wait_ge(hid_ready, 3 * j + k + 1)
                        nc.scalar.activation(hid[s][:, k, :], ps_h[:, k, :], ACT.Gelu,
                                             bias=(b1r if k == 2 else b1)[:, 0:1]).then_inc(gelu_done, 1)

            schedule(act, step)


def conv(nc, d):
    with ExitStack() as ctx:
        sb = lambda n, s: ctx.enter_context(nc.sbuf_tensor(n, s, F32))
        sem = lambda n: ctx.enter_context(nc.semaphore(n))
        ident = sb("ident3", [P, P])
        eps = sb("eps3", [P, 1])
        w1 = sb("ew", [P, CHUNKS, CH])
        w2 = sb("pw", [P, CHUNKS, NT])
        q = {n: sb(f"q_{n}", [CH, C]) for n in "gvt"}
        c2 = {n: sb(f"c_{n}", [P, 1]) for n in "gbmvt"}
        SLOTS = 5
        piece = [sb(f"piece{s}", [C, PH + 2, SC]) for s in range(SLOTS)]
        xp = sb("xp", [P, PATCHES, PIN])
        h1 = sb("h1", [P, CH, PATCHES])
        e = {n: h1[0:C, CHUNKS * j:CHUNKS * (j + 1), 0:CH] for j, n in enumerate("gbmvt")}
        room = sb("room", [P, PATCHES * CH])
        h2 = room[0:POUT, :].rearrange("q (p c) -> q p c", c=CH)
        mats = [sb(f"mats{s}", [PIN + 1, TCH, POUT]) for s in range(LOADS)]
        h2T = [[sb(f"h2T{s}{k}", [P, 5 * POUT]) for k in range(2)] for s in range(2)]
        y = sb("yc", [P, PR * PH, PC // 2 * PW])
        psum = ctx.enter_context(nc.psum_tensor("psum2", [P, 8, 512], F32))
        ring = [psum[:, s, :] for s in range(4)]
        ps_t = [psum[:, 4 + k, :] for k in range(2)]
        ps_y = [psum[:, 6 + s, :] for s in range(2)]
        fixed, w_loaded, root, w_ready = sem("c_fixed"), sem("c_loaded"), sem("c_root"), sem("c_ready")
        piece_loaded, first_loaded, cut, ones_set = [sem(f"piece_loaded{s}") for s in range(SLOTS)], sem("first_loaded"), sem("cut"), sem("ones_set")
        mats_loaded = [sem(f"mats_loaded{s}") for s in range(LOADS)]
        unit_ready, unit_act, unit_dve = sem("unit_ready"), sem("unit_act"), sem("unit_dve")
        turned, copied = sem("c_turned"), sem("c_copied")
        y_ready, y_done, y_stored = sem("c_y_ready"), sem("c_y_done"), sem("c_y_stored")
        img_stored = [sem(f"img_stored{s}") for s in range(2)]
        mlp_gelu, mlp_done = sem("gelu_done"), sem("m_y_done")

        fives = PATCHES - 4 * UNITS
        start = lambda j: 4 * j + min(j, fives)
        PARTS = ((0, 5), (5, 4), (9, 4))
        STEPS = [(pc, a, n) for pc in range(PC // 2) for a, n in PARTS]
        NSTEP = len(STEPS)

        def schedule(eng, first, chunk):
            first()
            with eng.Fori(0, HALVES // 2 - 1, 1) as b:
                for hx in range(2):
                    for c in range(CHUNKS):
                        chunk(b, hx, c, False)
            for hx in range(2):
                for c in range(CHUNKS):
                    chunk(HALVES // 2 - 1, hx, c, hx == 1 and c == CHUNKS - 1)

        def more(b, hx):
            return not (hx == 1 and isinstance(b, int))

        slot_of = [0] + [1 + j % (SLOTS - 2) for j in range(1, PR - 1)] + [SLOTS - 1]
        PER_HALF = [slot_of.count(s) for s in range(SLOTS)]

        def nth_in_slot(j):
            return slot_of[:j].count(slot_of[j])

        def place_of(j):
            s = slot_of[j]
            before = [i for i in range(j) if slot_of[i] == s]
            return s, before[-1] + 1 if before else max(i for i in range(PR) if slot_of[i] == s) + 1 - PR

        def number(b, hx, c):
            return 2 * CHUNKS * b + CHUNKS * hx + c

        def expand_at(j):
            return start(j), start(j + 1) - start(j)

        def evacuate(activation, j, expand):
            bank = ring[j % 4]
            if expand:
                a, n = expand_at(j)
                dst = h1[0:PIN, :, a:a + n].rearrange("q c p -> q p c")
                src = bank[0:PIN, 0:n * CH].rearrange("q (p c) -> q p c", c=CH)
            else:
                dst = h2[:, :, 4 * j:4 * j + 4].rearrange("q p c -> q c p")
                src = bank[0:POUT, 0:4 * PATCHES].rearrange("q (c p) -> q c p", c=4)
            if activation:
                return nc.scalar.activation(dst, src, ACT.Relu)
            return nc.vector.tensor_scalar(dst, src, 0.0, None, ALU.max)

        block = ctx.enter_context(nc.Block(name="mlp_conv"))

        def cut_piece(copy, j):
            slot, _ = place_of(j)
            src = piece[slot][:, :, :]
            src = bass.AP(src.tensor, src.offset, [list(src.ap[0]), [PW, PC], [SC, PH + 2], [1, PW + 2]])
            dst = xp[0:C, :, :].rearrange("k (c j) (r x) -> k j c r x", j=PR, x=PW + 2)[:, j]
            copy(dst, src).then_inc(cut, 1)

        def place_ones(eng, memset, hx, h):
            ones = xp[ONE:ONE + 1, :, :].rearrange("k (c j) (r x) -> k c j r x", j=PR, x=PW + 2)
            for pc, x, out in ((0, 0, hx == 0), (PC - 1, PW + 1, hx == 1)):
                last = memset(ones[:, pc, :, :, x], 0.0 if out else 1.0)
            last.then_inc(ones_set, 1)
            eng.wait_ge(ones_set, 2 * h + 1)
            memset(ones[:, :, 0, 0, :], 0.0)
            memset(ones[:, :, PR - 1, H - PH * (PR - 1) + 1:, :], 0.0).then_inc(ones_set, 1)

        def piece_rows(j):
            lo, hi = max(PH * j - 1, 0), min(PH * j + PH + 1, H)
            return lo, hi, lo - (PH * j - 1)

        @block.gpsimd
        def _(pool):
            constants = [(t[...], 0.0) for t in (w1, w2, *c2.values(), *h2T[0], *h2T[1], *piece, xp)]
            constants += [(h1[96:P, :, :], 1.0), (eps[:, :], EPS), (xp[ONE:ONE + 1, :, :], 1.0)]
            for n, (t, value) in enumerate(constants):
                nc.gpsimd.memset(t, value).then_inc(fixed, 1)
                pool.wait_ge(fixed, n + 1)
            loads = [(ident[:, :], d["ident"]), (w1[0:C, :, :], d["w1T"])]
            loads += [(e[n], d[f"bn1_{n}"].partition_broadcast(C)) for n in "gbmv"]
            loads += [(w2[0:CH, k, 0:C], d["w2T"][CH * k:CH * k + CH, :]) for k in range(CHUNKS)]
            loads += [(q[n][:, :], d[f"bn2_{n}"].partition_broadcast(CH)) for n in "gv"]
            loads += [(c2[n][r:r + C, :], d[f"bn2_{n}"].rearrange("(c a) -> c a", a=1)) for n in "gbmv" for r in (0, ONE)]
            assert len(loads) == 19
            for dst, src in loads:
                pool.dma_start(dst, src).then_inc(w_loaded, 16)
            nc.gpsimd.memset(y[:, :, :], 0.0).then_inc(y_stored, 32)
            pool.wait_ge(y_stored, 32)
            for s in range(2):
                pool.wait_ge(img_stored[s], 32 * (H // WS // 2))
            for j in range(PR):
                slot, nth = place_of(j)
                wait(pool, cut, nth)
                lo, hi, off = piece_rows(j)
                pool.dma_start(piece[slot][:, off:off + hi - lo, :], d["img_images"][:, 0, lo:hi, 0:SC])\
                    .then_inc(first_loaded, 16)
                pool.wait_ge(first_loaded, 16 * (j + 1))
                cut_piece(nc.gpsimd.tensor_copy, j)
            place_ones(pool, nc.gpsimd.memset, 0, 0)

        @block.sync
        def _(sp):
            for s in range(LOADS):
                sp.dma_start(mats[s][:, :, :], d["conv_mats"][s]).then_inc(mats_loaded[s], 16)

        mlp(nc, d, block, room, psum, img_stored, (mlp_gelu, mlp_done))

        @block.sync
        def _(sp):
            for s in range(2):
                sp.wait_ge(img_stored[s], 32 * (STRIPS // 2))

            def load_half(b, hx, h):
                for j in range(PR):
                    slot, nth = place_of(j)
                    wait(sp, cut, PR * h + nth)
                    lo, hi, off = piece_rows(j)
                    sp.dma_start(piece[slot][:, off:off + hi - lo, :],
                                 d["img_images"][:, b, lo:hi, HALF * hx:HALF * hx + SC]).then_inc(piece_loaded[slot], 16)

            def chunk(b, hx, c, last):
                k = number(b, hx, c)
                if c == CHUNKS - 1 and more(b, hx):
                    load_half(b + hx, 1 - hx, 2 * b + hx + 1)
                if not last:
                    for s in range(LOADS):
                        sp.wait_ge(unit_ready, UNITS * (2 * k + 1) + UNITS // LOADS * (s + 1))
                        sp.dma_start(mats[s][:, :, :], d["conv_mats"][LOADS * ((c + 1) % CHUNKS) + s])\
                            .then_inc(mats_loaded[s], 16)
                if c == CHUNKS - 1:
                    sp.wait_ge(y_done, NSTEP * (k + 1))
                    for r in range(2):
                        sp.dma_start(d["out"][4 * b + 2 * hx + r], y[64 * r:64 * r + C, 0:H, :].rearrange("c y x -> c (y x)"))\
                            .then_inc(y_stored, 16)

            schedule(sp, lambda: None, chunk)
            sp.wait_ge(y_stored, 32 * HALVES + 32)

        @block.tensor
        def _(pe):
            pe.wait_ge(w_ready, 5)

            def bank_free(stage, j):
                wait(pe, unit_dve if j % 2 else unit_act, UNITS // 2 * stage + (j - 4) // 2 + 1)

            def emptied(stages):
                wait(pe, unit_act, UNITS // 2 * stages)
                wait(pe, unit_dve, UNITS // 2 * stages)

            def expand(stage, c):
                for j in range(UNITS):
                    bank_free(stage, j)
                    a, n = expand_at(j)
                    for p in range(a, a + n):
                        mm = nc.tensor.matmul(ring[j % 4][0:PIN, CH * (p - a):CH * (p - a) + CH],
                                              xp[:, p, :], w1[:, c, :], start=True, stop=True)
                    mm.then_inc(unit_ready, 1)

            def first():
                pe.wait_ge(mlp_gelu, 3 * STRIPS)
                pe.wait_ge(mlp_done, STRIPS)
                pe.wait_ge(ones_set, 2)
                expand(0, 0)

            def chunk(b, hx, c, last):
                k = number(b, hx, c)
                emptied(2 * k + 1)
                for j in range(UNITS):
                    if j % (UNITS // LOADS) == 0:
                        pe.wait_ge(mats_loaded[j // (UNITS // LOADS)], 16 * (k + 1))
                    bank_free(2 * k + 1, j)
                    for n in range(4):
                        ch = 4 * j + n
                        mm = nc.tensor.matmul(ring[j % 4][0:POUT, PATCHES * n:PATCHES * (n + 1)],
                                              mats[ch // TCH][:, ch % TCH, :], h1[0:PIN + 1, ch, :], start=True, stop=True)
                    mm.then_inc(unit_ready, 1)
                if not last:
                    if c == CHUNKS - 1:
                        pe.wait_ge(ones_set, 2 * (2 * b + hx + 2))
                    expand(2 * k + 2, (c + 1) % CHUNKS)
                emptied(2 * k + 2)
                for n in range(NSTEP + 1):
                    if n < NSTEP:
                        pc, a, m = STEPS[n]
                        for r in range(2):
                            if n >= 1:
                                pe.wait_ge(copied, 2 * (NSTEP * k + n) + r - 1)
                            for p in range(m):
                                patch = PR * (pc + PC // 2 * r) + a + p
                                mm = nc.tensor.transpose(ps_t[r][0:CH, POUT * p:POUT * (p + 1)], h2[:, patch, :],
                                                         ident[0:POUT, 0:POUT])
                            mm.then_inc(turned, 1)
                    if n >= 1:
                        m = STEPS[n - 1][2]
                        pe.wait_ge(copied, 2 * (NSTEP * k + n))
                        if n >= 3:
                            pe.wait_ge(y_done, NSTEP * k + n - 2)
                        for r in range(2):
                            mm = nc.tensor.matmul(ps_y[(n - 1) % 2][64 * r:64 * r + 64, 0:POUT * m], w2[:, c, :],
                                                  h2T[(n - 1) % 2][r][:, 0:POUT * m], start=True, stop=True)
                        mm.then_inc(y_ready, 1)

            schedule(pe, first, chunk)

        @block.scalar
        def _(act):
            act.wait_ge(w_loaded, 16 * 19)
            nc.scalar.activation(e["t"], e["v"], ACT.Sqrt, bias=eps[0:C, :]).then_inc(root, 1)
            nc.scalar.activation(q["t"][:, :], q["v"][:, :], ACT.Sqrt, bias=eps[0:CH, :]).then_inc(root, 1)
            nc.scalar.activation(c2["t"][:, :], c2["v"][:, :], ACT.Sqrt, bias=eps[:, :]).then_inc(root, 1)

            def units(k2, expand):
                for j in range(0, UNITS, 2):
                    act.wait_ge(unit_ready, UNITS * k2 + j + 1)
                    evacuate(True, j, expand).then_inc(unit_act, 1)

            def chunk(b, hx, c, last):
                k = number(b, hx, c)
                units(2 * k + 1, False)
                if not last:
                    units(2 * k + 2, True)
                for n in range(NSTEP):
                    m = STEPS[n][2]
                    for r in range(2):
                        act.wait_ge(turned, 2 * (NSTEP * k + n) + r + 1)
                        nc.scalar.activation(h2T[n % 2][r][0:CH, 0:POUT * m], ps_t[r][0:CH, 0:POUT * m], ACT.Copy)\
                            .then_inc(copied, 1)

            def first():
                units(0, True)
                for s in range(2):
                    act.wait_ge(img_stored[s], 32 * (STRIPS // 2))

            schedule(act, first, chunk)

        @block.vector
        def _(dve):
            dve.wait_ge(root, 3)
            for t, v in ((e, 1), (q, 1), (c2, 1)):
                last = nc.vector.reciprocal(t["v"][...], t["t"][...])
            last.then_inc(w_ready, 1)
            dve.wait_ge(w_ready, 1)
            for t in (e, q, c2):
                last = nc.vector.tensor_tensor(t["t"][...], t["v"][...], t["g"][...], ALU.mult)
            last.then_inc(w_ready, 1)
            dve.wait_ge(w_ready, 2)
            for t in (e, c2):
                nc.vector.tensor_tensor(t["m"][...], t["m"][...], t["t"][...], ALU.mult)
            nc.vector.tensor_tensor(w1[0:C, :, :], w1[0:C, :, :], e["t"], ALU.mult)
            nc.vector.tensor_tensor(w2[0:CH, :, 0:C], w2[0:CH, :, 0:C], bc(q["t"][:, :], 1, CHUNKS), ALU.mult)\
                .then_inc(w_ready, 1)
            dve.wait_ge(w_ready, 3)
            for t in (e, c2):
                last = nc.vector.tensor_tensor(t["b"][...], t["b"][...], t["m"][...], ALU.subtract)
            last.then_inc(w_ready, 1)
            dve.wait_ge(w_ready, 4)
            nc.vector.tensor_copy(w1[ONE:ONE + 1, :, :], h1[0:1, CHUNKS:2 * CHUNKS, 0:CH]).then_inc(w_ready, 1)

            def next_piece(j, h):
                slot, _ = place_of(j)
                dve.wait_ge(piece_loaded[slot], 16 * (PER_HALF[slot] * (h - 1) + nth_in_slot(j) + 1))
                cut_piece(nc.vector.tensor_copy, j)

            def units(k2, expand, between=None):
                for j in range(1, UNITS, 2):
                    dve.wait_ge(unit_ready, UNITS * k2 + j + 1)
                    evacuate(False, j, expand).then_inc(unit_dve, 1)
                    if between:
                        between(j // 2)

            def add(n, b, hx, c, k):
                pc, a, m = STEPS[n]
                dve.wait_ge(y_ready, NSTEP * k + n + 1)
                rows = slice(PH * a, PH * (a + m))
                cols = slice(PW * pc, PW * pc + PW)
                dst = y[:, rows, cols]
                src = ps_y[n % 2][:, 0:POUT * m].rearrange("q (r x) -> q r x", x=PW)
                if c == 0:
                    if n == 0:
                        dve.wait_ge(y_stored, 32 * (2 * b + hx) + 32)
                    for r in range(2):
                        t = slice(64 * r, 64 * r + C)
                        p0 = PR * (pc + PC // 2 * r) + a
                        x = xp[0:C, p0:p0 + m, :].rearrange("k j (r x) -> k j r x", x=PW + 2)[:, :, 1:PH + 1, 1:PW + 1]
                        last = nc.vector.tensor_tensor(
                            y[t, rows, cols].rearrange("q (j r) x -> q j r x", j=m),
                            ps_y[n % 2][t, 0:POUT * m].rearrange("q (j r x) -> q j r x", j=m, x=PW), x, ALU.add)
                    last.then_inc(y_done, 1)
                elif c == CHUNKS - 1:
                    nc.vector.scalar_tensor_tensor(dst, src, c2["b"][:, 0:1], dst, ALU.add, ALU.add).then_inc(y_done, 1)
                else:
                    nc.vector.tensor_tensor(dst, src, dst, ALU.add).then_inc(y_done, 1)

            def chunk(b, hx, c, last):
                k = number(b, hx, c)
                cutting = c == CHUNKS - 1 and more(b, hx)
                units(2 * k + 1, False, (lambda j: next_piece(j, 2 * b + hx + 1)) if cutting else None)
                if cutting:
                    next_piece(PR - 1, 2 * b + hx + 1)
                    place_ones(dve, nc.vector.memset, 1 - hx, 2 * b + hx + 1)
                if not last:
                    units(2 * k + 2, True)
                for n in range(NSTEP + 1):
                    if n >= 1:
                        add(n - 1, b, hx, c, k)

            def first():
                units(0, True)
                for s in range(2):
                    dve.wait_ge(img_stored[s], 32 * (STRIPS // 2))

            assert UNITS // 2 + 1 == PR
            schedule(dve, first, chunk)


def block_program(nc, d):
    d["mid_strips"] = d["tok_mid"].rearrange("(j k) q e -> j q k e", k=2)
    d["tok_mid"] = d["tok_mid"].rearrange("g q (p e) -> g q p e", e=MID)
    d["img_strips"] = d["img_mid"].rearrange("c (j r) x -> c j r x", r=WS)
    d["img_images"] = d["img_mid"].rearrange("c (b y) x -> c b y x", b=B)
    attention(nc, d)
    conv(nc, d)


def tap_places():
    places = np.zeros((TAPROW + 1, POUT, P), np.float32)
    for r in range(PH):
        for c in range(PW):
            for t in range(9):
                places[t, r * PW + c, (r + t // 3) * (PW + 2) + c + t % 3] = 1
    places[TAPROW, :, PIN] = 1
    return places


def head_mask():
    mask = np.zeros((P, NH), np.float32)
    for h in range(NH):
        mask[ONE + HD * h:ONE + HD * (h + 1), h] = 1
    return mask


def kernel(**inputs):
    from concourse.bacc import Bacc
    from concourse.bass_utils import run_bass_kernel_spmd

    L0 = lambda n: np.asarray(inputs["L0_conv_" + n])
    L1 = lambda n: np.asarray(inputs["L1_conv_" + n])
    x = np.asarray(inputs["x"])
    groups = x.reshape(B, C, H // WS, WS, W // GW, GW // WS, WS).transpose(0, 2, 4, 1, 5, 3, 6)
    arrays = {
        "x_groups": groups.reshape(GROUPS, C, TOK),
        "n1_g": L0("norm1_g").reshape(C, 1), "n1_b": L0("norm1_b").reshape(C, 1),
        "qkv_wT": L0("qkv_w").T, "qkv_b": L0("qkv_b").reshape(1, 3 * C),
        "table": L0("rpb_table"), "rel_idx": L0("rel_idx").reshape(NT * NT),
        "proj_wT": L0("proj_w").T, "proj_b": L0("proj_b").reshape(1, C),
        "n2_g": L0("norm2_g").reshape(C, 1), "n2_b": L0("norm2_b").reshape(C, 1),
        "fc1_wT": L0("fc1_w").T, "fc1_b": L0("fc1_b").reshape(HID0, 1),
        "fc2_wT": L0("fc2_w").T, "fc2_b": L0("fc2_b").reshape(C, 1),
        "w1T": L1("w1").T, "wd": L1("wd").reshape(HID1, 9).T, "w2T": L1("w2").T,
        "ident": np.eye(P, dtype=np.float32), "headmask": head_mask(), "places": tap_places(),
        "number": np.arange(2 * P, dtype=np.float32).reshape(2, P).T,
    }
    for k, bn in (("1", "bn1"), ("2", "bn2")):
        for n in "gbmv":
            arrays[f"{bn}_{n}"] = L1(n + k)
    for n in ("gd", "bd", "md", "vd"):
        arrays[n] = L1(n)
    arrays = {f"in_{n}": np.ascontiguousarray(a) for n, a in arrays.items()}

    nc = Bacc("TRN2", target_bir_lowering=False, num_devices=1)
    d = {n[3:]: nc.dram_tensor(n, a.shape, mybir.dt.from_np(a.dtype), kind="ExternalInput").ap() for n, a in arrays.items()}
    halves = (B, W // HALF, 2, C, H, HALF // 2)
    for n, shape in (("conv_mats", (HID1 // TCH, PIN + 1, TCH, POUT)), ("rel_bias", (NH, NT * NT)),
                     ("tok_mid", (GROUPS, P, PAIRS * MID)), ("img_mid", (C, B * H, W + 2))):
        d[n] = nc.dram_tensor(n, shape, F32, kind="Internal").ap()
    d["out"] = nc.dram_tensor("out", (B * 4, C, H * HALF // 2), F32, kind="ExternalOutput").ap()
    block_program(nc, d)
    got = run_bass_kernel_spmd(nc, [arrays], core_ids=[0]).results[0]["out"]
    return got.reshape(halves).transpose(0, 3, 4, 1, 2, 5).reshape(B, C, H, W)
```

```python
from contextlib import ExitStack

import numpy as np

import concourse.bass as bass
from concourse import mybir

F32 = mybir.dt.float32
I32 = mybir.dt.int32
ALU = mybir.AluOpType
ACT = mybir.ActivationFunctionType
AX_X = mybir.AxisListType.X

P = 128
B, C, H, W = 4, 48, 128, 128
WS, NH = 8, 4
HD = C // NH
NT = WS * WS
EPS = 1e-5
ONE = 64

GW = 64
PAIRS = GW // (2 * WS)
TOK = PAIRS * 2 * NT
GROUPS = B * (H // WS) * (W // GW)
VB = 2 * 2 * HD
NB = 96
MID = 112
HID0 = 4 * C

HID1 = 288
PH, PW = 8, 8
PIN, POUT = (PH + 2) * (PW + 2), PH * PW
PC, PR = 8, 16
PATCHES = PC * PR
HALF = PC * PW
SC = HALF + 2
CH = 96
CHUNKS = HID1 // CH
TCH = 32
LOADS = CH // TCH
TAPROW = 32
HALVES = B * 2
STRIPS = GROUPS // 2
EXPANDS = PATCHES // 4
DEPTHS = CH // 4


def wait(eng, sem, n):
    if not isinstance(n, int) or n >= 1:
        eng.wait_ge(sem, n)


def bc(ap, axis, n):
    a = ap.unsqueeze(axis)
    shape = list(a.shape)
    shape[axis] = n
    return a.broadcast_to(shape)


def prepare_tables(nc, d, block, scratch, psum, kb, kb_set):
    ctx = ExitStack()
    sb = lambda n, s, t=F32: ctx.enter_context(nc.sbuf_tensor(n, s, t))
    sem = lambda n: ctx.enter_context(nc.semaphore(n))
    ids = sb("ids", [P, NT * NT], I32)
    table, number = sb("table", [P, 2, NH]), sb("number", [P, 2])
    taps = sb("taps", [P, HID1])
    gd, vd, md, bd = (sb(n, [TAPROW + 1, HID1]) for n in ("gd", "vd", "md", "bd"))
    sd, shift = sb("sd", [TAPROW + 1, HID1]), sb("shift", [TAPROW + 1, HID1])
    eps = sb("eps_d", [P, 1])
    size = [POUT * P, CH * POUT]
    places = scratch[:, 0:size[0]].rearrange("q (o i) -> q o i", o=POUT)
    onehot = scratch[:, size[0]:size[0] + 2 * NT * NT].rearrange("q (t n) -> q t n", t=2)
    idsf = scratch[:, size[0] + 2 * NT * NT:size[0] + 3 * NT * NT]
    bias = idsf[0:NH, :]
    mats = [scratch[:, size[0] + size[1] * k:size[0] + size[1] * (k + 1)].rearrange("q (c o) -> q c o", o=POUT)
            for k in range(2)]
    cleared, loaded, ids_loaded, cast = sem("t_cleared"), sem("t_loaded"), sem("ids_loaded"), sem("ids_cast")
    hot, looked_up, copied, stored, kb_loaded = (
        sem(n) for n in ("hot", "looked_up", "b_copied", "b_stored", "kb_loaded"))
    bn_loaded, table_loaded = sem("bn_loaded"), sem("table_loaded")
    root, scaled = sem("d_root"), sem("d_scaled")
    mat_ready, copied_v, copied_a = sem("mat_ready"), sem("mat_cv"), sem("mat_ca")
    mats_stored = [sem(f"mat_stored{k}") for k in range(2)]
    K = TAPROW + 1
    UNIT = 4
    NU = POUT // UNIT
    BLOCKS = NT * NT // 512

    @block.gpsimd
    def _(pool):
        for n, (t, value) in enumerate(((eps[:, :], EPS), (table[:, :, :], 0.0), (taps[:, :], 0.0),
                                       (places, 0.0))):
            nc.gpsimd.memset(t, value).then_inc(cleared, 1)
            pool.wait_ge(cleared, n + 1)

    @block.sync
    def _(sp):
        for dst, src in ((ids[:, :], d["rel_idx"].partition_broadcast(P)), (number[:, :], d["number"])):
            sp.dma_start(dst, src).then_inc(ids_loaded, 16)
        for t, n in ((vd, "vd"), (gd, "gd"), (md, "md"), (bd, "bd")):
            sp.dma_start(t[:, :], d[n].partition_broadcast(K)).then_inc(bn_loaded, 16)
        sp.wait_ge(cleared, 2)
        for t, rows in ((0, slice(0, P)), (1, slice(P, d["table"].shape[0]))):
            sp.dma_start(table[0:rows.stop - rows.start, t, :], d["table"][rows, :]).then_inc(table_loaded, 16)
        sp.wait_ge(cleared, 4)
        sp.dma_start(taps[0:9, :], d["wd"]).then_inc(loaded, 16)
        sp.dma_start(places[0:K, :, :], d["places"]).then_inc(loaded, 16)
        sp.wait_ge(copied, BLOCKS)
        sp.dma_start(d["rel_bias"], bias).then_inc(stored, 16)
        sp.wait_ge(stored, 16)
        sp.wait_ge(*kb_set)
        for s in range(2):
            for h in range(NH):
                src = d["rel_bias"][h].rearrange("(n m) -> n m", m=NT)
                sp.dma_start(kb[s][0:NT, :, h, :], bc(src, 1, 2 * PAIRS)).then_inc(kb_loaded, 16)
        for c in range(CHUNKS):
            sp.wait_ge(copied_v, NU // 2 * (c + 1))
            sp.wait_ge(copied_a, NU // 2 * (c + 1))
            for u in range(LOADS):
                sp.dma_start(d["conv_mats"][LOADS * c + u], mats[c % 2][0:PIN + 1, TCH * u:TCH * u + TCH, :])\
                    .then_inc(mats_stored[c % 2], 16)

    def mats_free(eng, c):
        if c == 1:
            eng.wait_ge(stored, 16)
        if c >= 2:
            eng.wait_ge(mats_stored[c % 2], 16 * LOADS * (c // 2))

    @block.vector
    def _(dve):
        dve.wait_ge(ids_loaded, 32)
        nc.vector.tensor_copy(idsf, ids[:, :]).then_inc(cast, 1)
        dve.wait_ge(cast, 1)
        for t in range(2):
            nc.vector.tensor_scalar(onehot[:, t, :], idsf, number[:, t:t + 1], None, ALU.is_equal).then_inc(hot, 1)
        dve.wait_ge(root, 1)
        nc.vector.reciprocal(vd[:, :], sd[:, :]).then_inc(scaled, 1)
        dve.wait_ge(scaled, 1)
        nc.vector.tensor_tensor(sd[:, :], vd[:, :], gd[:, :], ALU.mult).then_inc(scaled, 1)
        dve.wait_ge(scaled, 2)
        nc.vector.tensor_tensor(md[:, :], md[:, :], sd[:, :], ALU.mult).then_inc(scaled, 1)
        dve.wait_ge(loaded, 32)
        nc.vector.tensor_tensor(taps[0:9, :], taps[0:9, :], sd[0:9, :], ALU.mult).then_inc(scaled, 1)
        dve.wait_ge(scaled, 4)
        nc.vector.tensor_tensor(shift[:, :], bd[:, :], md[:, :], ALU.subtract).then_inc(scaled, 1)
        dve.wait_ge(scaled, 5)
        nc.vector.tensor_copy(taps[TAPROW:K, :], shift[0:1, :]).then_inc(scaled, 1)
        for j in range(0, BLOCKS, 2):
            dve.wait_ge(looked_up, j + 1)
            nc.vector.tensor_copy(bias[:, 512 * j:512 * j + 512], psum[0:NH, j, :]).then_inc(copied, 1)
        for c in range(CHUNKS):
            mats_free(dve, c)
            for u in range(NU * c, NU * (c + 1), 2):
                dve.wait_ge(mat_ready, u + 1)
                j = UNIT * (u % NU)
                nc.vector.tensor_copy(mats[c % 2][0:PIN + 1, :, j:j + UNIT].rearrange("q c o -> q o c"),
                                      psum[0:PIN + 1, u % 8, 0:UNIT * CH].rearrange("q (o c) -> q o c", c=CH)).then_inc(copied_v, 1)

    @block.scalar
    def _(act):
        act.wait_ge(bn_loaded, 64)
        act.wait_ge(cleared, 1)
        nc.scalar.activation(sd[:, :], vd[:, :], ACT.Sqrt, bias=eps[0:K, :]).then_inc(root, 1)
        for j in range(1, BLOCKS, 2):
            act.wait_ge(looked_up, j + 1)
            nc.scalar.activation(bias[:, 512 * j:512 * j + 512], psum[0:NH, j, :], ACT.Copy).then_inc(copied, 1)
        for c in range(CHUNKS):
            mats_free(act, c)
            for u in range(NU * c + 1, NU * (c + 1), 2):
                act.wait_ge(mat_ready, u + 1)
                j = UNIT * (u % NU)
                nc.scalar.activation(mats[c % 2][0:PIN + 1, :, j:j + UNIT].rearrange("q c o -> q o c"),
                                     psum[0:PIN + 1, u % 8, 0:UNIT * CH].rearrange("q (o c) -> q o c", c=CH), ACT.Copy)\
                    .then_inc(copied_a, 1)

    @block.tensor
    def _(pe):
        pe.wait_ge(table_loaded, 32)
        pe.wait_ge(hot, 2)
        for j in range(BLOCKS):
            for t in range(2):
                mm = nc.tensor.matmul(psum[0:NH, j, :], table[:, t, :], onehot[:, t, 512 * j:512 * j + 512],
                                      start=(t == 0), stop=(t == 1))
            mm.then_inc(looked_up, 1)
        pe.wait_ge(loaded, 32)
        pe.wait_ge(scaled, 6)
        pe.wait_ge(copied, BLOCKS)
        for u in range(CHUNKS * NU):
            if u >= 8:
                pe.wait_ge(copied_a if u % 2 else copied_v, (u - 8) // 2 + 1)
            c, j = u // NU, UNIT * (u % NU)
            for k in range(UNIT):
                mm = nc.tensor.matmul(psum[0:PIN + 1, u % 8, CH * k:CH * k + CH], places[:, j + k, 0:PIN + 1],
                                      taps[:, CH * c:CH * c + CH], start=True, stop=True)
            mm.then_inc(mat_ready, 1)
        pe.wait_ge(copied_a, NU // 2 * CHUNKS)
        pe.wait_ge(copied_v, NU // 2 * CHUNKS)

    return ctx, kb_loaded, mats_stored


def attention(nc, d):
    with ExitStack() as ctx:
        sb = lambda n, s, t=F32: ctx.enter_context(nc.sbuf_tensor(n, s, t))
        sem = lambda n: ctx.enter_context(nc.semaphore(n))
        ident = sb("ident", [P, P])
        headmask = sb("headmask", [P, NH])
        eps = sb("eps", [P, 1])
        w_qk = sb("w_qk", [P, 112])
        w_v, w_o = sb("w_v", [P, NB]), sb("w_o", [P, NB])
        qkv_w, qkv_b = sb("qkv_w", [C, 3 * C]), sb("qkv_b", [1, 3 * C])
        lnrow = sb("lnrow", [1, 3 * C])
        ln_g, ln_b = sb("ln_g", [C, 1]), sb("ln_b", [C, 1])
        xs = [sb(f"xs{s}", [C, TOK]) for s in range(2)]
        scratch = sb("scratch", [P, max(GROUPS * PAIRS * C, POUT * P + 2 * CH * POUT)])
        xtok = scratch[:, 0:GROUPS * PAIRS * C].rearrange("q (g p c) -> q g p c", g=GROUPS, p=PAIRS)
        sums, sq_sums, lnv, rstd = ([sb(f"{n}{s}", [P, PAIRS]) for s in range(2)] for n in ("sum", "sqs", "lnv", "rstd"))
        sums2, sq_sums2, lnv2, rstd2 = ([sb(f"{n}{s}", [P, PAIRS]) for s in range(2)] for n in ("sumb", "sqsb", "lnvb", "rstdb"))
        cen = [sb(f"cen{s}", [P, PAIRS, C]) for s in range(2)]
        cen2 = [sb(f"cenb{s}", [P, PAIRS, C]) for s in range(2)]
        sq, sq2 = sb("sq", [P, PAIRS, C]), sb("sqb", [P, PAIRS, C])
        xn = [sb(f"xn{s}", [P, PAIRS, C]) for s in range(2)]
        xnT = [sb(f"xnT{s}", [P, TOK]) for s in range(2)]
        qa = [sb(f"qa{s}", [P, TOK]) for s in range(2)]
        kb = [sb(f"kb{s}", [P, 2 * PAIRS, NH, NT]) for s in range(2)]
        vb = [sb(f"vb{s}", [P, 2 * PAIRS * VB]) for s in range(2)]
        top = [sb(f"top{s}", [P, PAIRS * NH]) for s in range(2)]
        prob = [sb(f"prob{s}", [P, PAIRS * NH, NT]) for s in range(2)]
        probT = sb("probT", [P, PAIRS, 2, P])
        den = [sb(f"den{s}", [P, PAIRS * NH]) for s in range(2)]
        rden = [sb(f"rden{s}", [P, PAIRS * NH]) for s in range(2)]
        oT = sb("oT", [P, TOK])
        mid = [sb(f"mid{s}", [P, PAIRS, MID]) for s in range(2)]

        psum = ctx.enter_context(nc.psum_tensor("psum1", [P, 8, 512], F32))
        ps_s = psum[:, 0:2, :]
        ps_p = psum[:, 2:4, :]
        ps_x = psum[:, 4, :]
        ps_t = psum[0:64, 5, :]
        ps_o = psum[64:P, 5, :]
        ps_k = psum[:, 6, :]
        ps_y = psum[:, 7, :]

        w_loaded, fixed, w_bias, w_ready = sem("w_loaded"), sem("fixed"), sem("w_bias"), sem("w_ready")
        ident_put, lnrow_put = sem("ident_put"), sem("lnrow_put")
        x_loaded = [sem(f"x_loaded{s}") for s in range(2)]
        stored = [sem(f"mid_stored{s}") for s in range(2)]
        x_turned, x_copied, sum_done, cen_done, sq_done, var_done, ln_done, rstd_done, xn_done = (
            sem(n) for n in ("x_turned", "x_copied", "sum_done", "cen_done", "sq_done", "var_done", "ln_done",
                             "rstd_done", "xn_done"))
        xnT_ready, xnT_copied, qk_ready, q_copied, kb_done = (
            sem(n) for n in ("xnT_ready", "xnT_copied", "qk_ready", "q_copied", "kb_done"))
        v_ready, v_copied, s_ready, top_done, sub_done, exp_done = (
            sem(n) for n in ("v_ready", "v_copied", "s_ready", "top_done", "sub_done", "exp_done"))
        pT_ready, pT_copied, o_ready, den_done, rden_done, prob_done, oT_copied, y_ready, res_done = (
            sem(n) for n in ("pT_ready", "pT_copied", "o_ready", "den_done", "rden_done", "prob_done", "oT_copied",
                             "y_ready", "res_done"))
        sum2_done, cen2_done, sq2_done, var2_done, ln2_done, rstd2_done, mid_done = (
            sem(n) for n in ("sum2_done", "cen2_done", "sq2_done", "var2_done", "ln2_done", "rstd2_done", "mid_done"))

        HALF_G = PAIRS * NH // 2
        W_LOADS = 9
        W_FIXED, FIXED = 3, 18
        def has(g):
            return not isinstance(g, int) or 0 <= g < GROUPS

        def schedule(eng, step):
            for i in range(-4, 6):
                step(i, i % 2)
            with eng.Fori(6, GROUPS - 7, 2) as i:
                step(i, 0)
                step(i + 1, 1)
            for i in range(GROUPS - 6, GROUPS + 4):
                step(i, i % 2)

        block = ctx.enter_context(nc.Block(name="attention"))

        @block.gpsimd
        def _(pool):
            constants = [(t[...], 0.0) for t in (w_qk, w_v, w_o)]
            LOADED_INTO = len(constants)
            constants += [(t[...], 0.0) for t in (qa[0], qa[1], xnT[0], xnT[1], oT, vb[0], vb[1], kb[0], kb[1], mid[0], mid[1])]
            constants += [(eps[:, :], EPS)] + [(t[ONE:ONE + 1, :], 1.0) for t in (xnT[0], xnT[1], oT)]
            for n, (t, value) in enumerate(constants):
                nc.gpsimd.memset(t, value).then_inc(fixed, 1)
                pool.wait_ge(fixed, n + 1)
            assert (LOADED_INTO, len(constants)) == (W_FIXED, FIXED)

        @block.scalar
        def _(act):
            act.wait_ge(fixed, W_FIXED)
            for dst, src in ((ident[:, :], d["ident"]), (headmask[:, :], d["headmask"]), (qkv_w[:, :], d["qkv_wT"]),
                             (qkv_b[:, :], d["qkv_b"]), (ln_g[:, :], d["n1_g"]), (ln_b[:, :], d["n1_b"]),
                             (w_o[0:C // 2, 0:C], d["proj_wT"][0:C // 2, :]),
                             (w_o[32:32 + C // 2, 0:C], d["proj_wT"][C // 2:C, :]), (w_o[ONE:ONE + 1, 0:C], d["proj_b"])):
                act.dma_start(dst, src).then_inc(w_loaded, 16)
            for s in range(2):
                act.dma_start(xs[s][:, :], d["x_groups"][s]).then_inc(x_loaded[s], 16)

        @block.vector
        def _(dve):
            nc.vector.memset(ps_o, 0.0)
            dve.wait_ge(fixed, W_FIXED + 2)
            dve.wait_ge(w_loaded, 16 * W_LOADS)
            for s in range(2):
                last = nc.vector.tensor_copy(qa[s][0:NT, :].rearrange("q (n t) -> q n t", n=2 * PAIRS),
                                             bc(ident[0:NT, 0:NT], 1, 2 * PAIRS))
            last.then_inc(ident_put, 1)
            nc.vector.tensor_scalar(w_qk[0:C, 0:C], qkv_w[:, 0:C], ln_g[:, 0:1], HD ** -0.5, ALU.mult, ALU.mult)\
                .then_inc(w_ready, 1)
            nc.vector.tensor_scalar(w_qk[0:C, ONE:ONE + C], qkv_w[:, C:2 * C], ln_g[:, 0:1], None, ALU.mult)\
                .then_inc(w_ready, 1)
            nc.vector.tensor_scalar(w_v[0:C, 0:C], qkv_w[:, 2 * C:3 * C], ln_g[:, 0:1], None, ALU.mult)\
                .then_inc(w_ready, 1)
            dve.wait_ge(w_bias, 1)
            nc.vector.tensor_tensor(lnrow[:, :], ps_x[0:1, 0:3 * C], qkv_b[:, :], ALU.add).then_inc(lnrow_put, 1)
            dve.wait_ge(lnrow_put, 1)
            one = slice(ONE, ONE + 1)
            nc.vector.tensor_scalar(w_qk[one, 0:C], lnrow[:, 0:C], HD ** -0.5, None, ALU.mult).then_inc(w_ready, 1)
            nc.vector.tensor_copy(w_qk[one, ONE:ONE + C], lnrow[:, C:2 * C]).then_inc(w_ready, 1)
            nc.vector.tensor_copy(w_v[one, 0:C], lnrow[:, 2 * C:3 * C]).then_inc(w_ready, 1)

        @block.tensor
        def _(pe):
            pe.wait_ge(w_loaded, 16 * W_LOADS)
            nc.tensor.matmul(ps_x[0:1, 0:3 * C], ln_b[:, :], qkv_w[:, :], start=True, stop=True).then_inc(w_bias, 1)

        tables, kb_loaded, mats_stored = prepare_tables(nc, d, block, scratch, psum, kb, (fixed, FIXED))
        ctx.enter_context(tables)

        @block.sync
        def _(sp):
            def load(g, s):
                if has(g):
                    wait(sp, x_turned, g - 1)
                    sp.dma_start(xs[s][:, :], d["x_groups"][g]).then_inc(x_loaded[s], 16)

            def step(i, s):
                load(i + 6, s)
                if has(i - 4):
                    sp.wait_ge(mid_done, i - 3)
                    sp.dma_start(d["tok_mid"][i - 4], mid[s][:, :, :]).then_inc(stored[s], 16)

            schedule(sp, step)
            for s in range(2):
                sp.wait_ge(stored[s], 16 * (GROUPS // 2))

        @block.tensor
        def _(pe):
            pe.wait_ge(w_ready, 6)
            pe.wait_ge(ident_put, 1)
            pe.wait_ge(fixed, FIXED)
            pe.wait_ge(kb_loaded, 16 * 2 * NH)

            def step(i, s):
                if isinstance(i, int):
                    for sem, g in ((v_copied, i), (x_copied, i + 3), (res_done, i - 3), (oT_copied, i - 2)):
                        if has(g):
                            pe.wait_ge(sem, g + 1)
                if has(i):
                    pe.wait_ge(q_copied, i + 1)
                    pe.wait_ge(kb_done, i + 1)
                    wait(pe, sub_done, i)
                    for n in range(2 * PAIRS):
                        p, w = divmod(n, 2)
                        mm = nc.tensor.matmul(ps_s[NT * w:NT * w + NT, p // 2, 256 * (p % 2):256 * (p % 2) + 256],
                                              qa[s][:, NT * n:NT * n + NT], kb[s][:, n, :, :], start=True, stop=True)
                    mm.then_inc(s_ready, 1)
                if has(i + 1):
                    pe.wait_ge(xnT_copied, i + 2)
                if has(i + 2):
                    pe.wait_ge(xn_done, i + 3)
                if has(i + 1):
                    nc.tensor.matmul(ps_k[0:112, :], w_qk[:, :], xnT[1 - s][:, :], start=True, stop=True)\
                        .then_inc(qk_ready, 1)
                if has(i + 2):
                    for p in range(PAIRS):
                        mm = nc.tensor.transpose(ps_t[0:C, P * p:P * p + P], xn[s][:, p, :], ident[:, :])
                    mm.then_inc(xnT_ready, 1)
                if has(i + 4):
                    pe.wait_ge(x_loaded[s], 8 * (i + 4 - s) + 16)
                    if has(i):
                        pe.wait_ge(v_copied, i + 1)
                if has(i - 1):
                    wait(pe, pT_copied, 2 * i - 2)
                    for p in range(PAIRS):
                        if p % (PAIRS // 2) == 0:
                            pe.wait_ge(prob_done, 2 * i - 1 + p // (PAIRS // 2))
                        for h in range(2):
                            src = prob[1 - s][:, NH * p + 2 * h:NH * p + 2 * h + 2, :]
                            at = 256 * (p % 2) + P * h
                            mm = nc.tensor.transpose(ps_p[:, p // 2, at:at + P], src, ident[:, :])
                        if p % (PAIRS // 2) == 1:
                            mm.then_inc(pT_ready, 1)
                if has(i + 4):
                    for p in range(PAIRS):
                        mm = nc.tensor.transpose(ps_x[:, C * p:C * p + C], xs[s][:, P * p:P * p + P], ident[0:C, 0:C])
                    mm.then_inc(x_turned, 1)
                if has(i - 2):
                    pe.wait_ge(oT_copied, i - 1)
                    wait(pe, res_done, i - 2)
                    for p in range(PAIRS):
                        mm = nc.tensor.matmul(ps_y[:, C * p:C * p + NB], oT[:, P * p:P * p + P], w_o[:, :],
                                              start=True, stop=True)
                    mm.then_inc(y_ready, 1)
                if has(i - 1):
                    pe.wait_ge(pT_copied, 2 * i)
                    for p in range(PAIRS):
                        for w in range(2):
                            for h in range(2):
                                at = VB * (2 * p + h) + 2 * HD * w
                                tok = P * p + NT * w
                                mm = nc.tensor.matmul(ps_o[32 * h:32 * h + 2 * HD, tok:tok + NT], vb[1 - s][:, at:at + 2 * HD],
                                                      probT[:, p, h, NT * w:NT * w + NT], start=True, stop=True)
                    mm.then_inc(o_ready, 1)
                if has(i + 1):
                    if has(i + 4):
                        pe.wait_ge(x_copied, i + 5)
                    for p in range(PAIRS):
                        mm = nc.tensor.matmul(ps_x[:, C * p:C * p + NB], xnT[1 - s][:, P * p:P * p + P], w_v[:, :],
                                              start=True, stop=True)
                    mm.then_inc(v_ready, 1)

            schedule(pe, step)

        @block.vector
        def _(dve):
            def step(i, s):
                def total(k):
                    r = slice(HALF_G * k, HALF_G * (k + 1))
                    nc.vector.tensor_reduce(den[1 - s][:, r], prob[1 - s][:, r, :], AX_X, ALU.add).then_inc(den_done, 1)

                def inverse(k):
                    r = slice(HALF_G * k, HALF_G * (k + 1))
                    dve.wait_ge(den_done, 2 * i - 1 + k)
                    nc.vector.reciprocal(rden[1 - s][:, r], den[1 - s][:, r]).then_inc(rden_done, 1)

                if has(i - 1):
                    dve.wait_ge(exp_done, i)
                    total(0)
                m = mid[1 - s][:, :, ONE:ONE + C]
                if has(i - 3):
                    dve.wait_ge(y_ready, i - 2)
                    wait(dve, stored[1 - s], 8 * (i - 3 - (1 - s)))
                    x = xtok[:, bass.ds(i - 3, 1), :, :].rearrange("q g p c -> q (g p) c")
                    nc.vector.tensor_tensor(m, ps_y[:, 0:PAIRS * C].rearrange("q (p c) -> q p c", c=C), x, ALU.add)\
                        .then_inc(res_done, 1)
                if has(i - 1):
                    inverse(0)
                    total(1)
                if has(i - 3):
                    dve.wait_ge(res_done, i - 2)
                    nc.vector.tensor_reduce(sums2[1 - s][:, :], m, AX_X, ALU.add).then_inc(sum2_done, 1)
                if has(i - 1):
                    inverse(1)
                if has(i + 3):
                    dve.wait_ge(x_copied, i + 4)
                    x = xtok[:, bass.ds(i + 3, 1), :, :].rearrange("q g p c -> q (g p) c")
                    nc.vector.tensor_reduce(sums[1 - s][:, :], x, AX_X, ALU.add).then_inc(sum_done, 1)
                if has(i - 3):
                    dve.wait_ge(sum2_done, i - 2)
                    nc.vector.scalar_tensor_tensor(cen2[1 - s][:, :, :], bc(sums2[1 - s][:, :], 2, C), -1.0 / C, m,
                                                   ALU.mult, ALU.add).then_inc(cen2_done, 1)
                sc = ps_s[:, :, :].rearrange("q b (h m) -> q (b h) m", m=NT)
                if has(i):
                    dve.wait_ge(s_ready, i + 1)
                    nc.vector.tensor_reduce(top[s][:, :], sc, AX_X, ALU.max).then_inc(top_done, 1)
                if has(i + 3):
                    dve.wait_ge(sum_done, i + 4)
                    x = xtok[:, bass.ds(i + 3, 1), :, :].rearrange("q g p c -> q (g p) c")
                    nc.vector.scalar_tensor_tensor(cen[1 - s][:, :, :], bc(sums[1 - s][:, :], 2, C), -1.0 / C, x,
                                                   ALU.mult, ALU.add).then_inc(cen_done, 1)
                if has(i):
                    dve.wait_ge(top_done, i + 1)
                    nc.vector.tensor_tensor(prob[s][:, :, :], sc, bc(top[s][:, :], 2, NT), ALU.subtract)\
                        .then_inc(sub_done, 1)
                if has(i + 1):
                    dve.wait_ge(qk_ready, i + 2)
                    nc.vector.tensor_copy(qa[1 - s][ONE:ONE + C, :], ps_k[0:C, :]).then_inc(q_copied, 1)
                if has(i + 3):
                    dve.wait_ge(sq_done, i + 4)
                    nc.vector.tensor_reduce(sq_sums[1 - s][:, :], sq[:, :, :], AX_X, ALU.add).then_inc(var_done, 1)
                if has(i - 3):
                    dve.wait_ge(sq2_done, i - 2)
                    nc.vector.tensor_reduce(sq_sums2[1 - s][:, :], sq2[:, :, :], AX_X, ALU.add).then_inc(var2_done, 1)

            schedule(dve, step)

        @block.scalar
        def _(act):
            nc.scalar.preload_act_table_set("natural_log_exp_and_others")

            def keys(i, s, heads):
                for h in heads:
                    last = nc.scalar.activation(
                        kb[1 - s][ONE:ONE + C, :, h, :], ps_k[ONE:ONE + C, :].rearrange("q (n m) -> q n m", m=NT),
                        ACT.Copy, scale=headmask[ONE:ONE + C, h:h + 1])
                return last

            def step(i, s):
                if has(i + 1):
                    act.wait_ge(xnT_ready, i + 2)
                    nc.scalar.activation(xnT[1 - s][0:C, :], ps_t[0:C, :], ACT.Copy).then_inc(xnT_copied, 1)
                if has(i - 4):
                    act.wait_ge(var2_done, i - 3)
                    nc.scalar.activation(lnv2[s][:, :], sq_sums2[s][:, :], ACT.Ln, bias=eps[:, :], scale=1.0 / C)\
                        .then_inc(ln2_done, 1)
                if has(i):
                    act.wait_ge(v_ready, i + 1)
                    for h in range(2):
                        for w in range(2):
                            dst = vb[s][NT * h:NT * h + NT, :].rearrange(
                                "q (b w h e) -> q b w h e", w=2, h=2, e=HD)[:, :, w, h, :]
                            src = ps_x[NT * w:NT * w + NT, 0:PAIRS * C].rearrange("q (b h e) -> q b h e", h=2, e=HD)
                            last = nc.scalar.activation(dst, src[:, :, h, :], ACT.Copy)
                    last.then_inc(v_copied, 1)
                if has(i - 4):
                    act.wait_ge(ln2_done, i - 3)
                    nc.scalar.activation(rstd2[s][:, :], lnv2[s][:, :], ACT.Exp, scale=-0.5).then_inc(rstd2_done, 1)
                if has(i - 2):
                    act.wait_ge(o_ready, i - 1)
                    nc.scalar.activation(oT[0:32 + 2 * HD, :], ps_o[0:32 + 2 * HD, :], ACT.Copy).then_inc(oT_copied, 1)
                if has(i + 1):
                    act.wait_ge(qk_ready, i + 2)
                    keys(i, s, range(0, 3))
                if has(i - 1):
                    for k in range(2):
                        act.wait_ge(pT_ready, 2 * i - 1 + k)
                        nc.scalar.activation(probT[:, 2 * k:2 * k + 2, :, :].rearrange("q p h n -> q (p h n)"),
                                             ps_p[:, k, :], ACT.Copy).then_inc(pT_copied, 1)
                if has(i + 4):
                    if isinstance(i, int) and i == 5:
                        act.wait_ge(mats_stored[0], 16 * LOADS * 2)
                        act.wait_ge(mats_stored[1], 16 * LOADS)
                    act.wait_ge(x_turned, i + 5)
                    x = xtok[:, bass.ds(i + 4, 1), :, :].rearrange("q g p c -> q (g p c)")
                    nc.scalar.activation(x, ps_x[:, 0:PAIRS * C], ACT.Copy).then_inc(x_copied, 1)
                if has(i + 1):
                    keys(i, s, range(3, NH)).then_inc(kb_done, 1)
                if has(i):
                    act.wait_ge(sub_done, i + 1)
                    nc.scalar.activation(prob[s][:, :, :], prob[s][:, :, :], ACT.Exp).then_inc(exp_done, 1)
                if has(i + 3):
                    act.wait_ge(var_done, i + 4)
                    nc.scalar.activation(lnv[1 - s][:, :], sq_sums[1 - s][:, :], ACT.Ln, bias=eps[:, :], scale=1.0 / C)\
                        .then_inc(ln_done, 1)
                    act.wait_ge(ln_done, i + 4)
                    nc.scalar.activation(rstd[1 - s][:, :], lnv[1 - s][:, :], ACT.Exp, scale=-0.5).then_inc(rstd_done, 1)

            schedule(act, step)

        @block.gpsimd
        def _(pool):
            def step(i, s):
                if has(i - 1):
                    for k in range(2):
                        r = slice(HALF_G * k, HALF_G * (k + 1))
                        pool.wait_ge(rden_done, 2 * i - 1 + k)
                        nc.gpsimd.tensor_tensor(prob[1 - s][:, r, :], prob[1 - s][:, r, :], bc(rden[1 - s][:, r], 2, NT),
                                                ALU.mult).then_inc(prob_done, 1)
                if has(i - 4):
                    pool.wait_ge(rstd2_done, i - 3)
                    nc.gpsimd.tensor_tensor(mid[s][:, :, 0:C], cen2[s][:, :, :], bc(rstd2[s][:, :], 2, C),
                                            ALU.mult).then_inc(mid_done, 1)
                if has(i - 3):
                    pool.wait_ge(cen2_done, i - 2)
                    nc.gpsimd.tensor_tensor(sq2[:, :, :], cen2[1 - s][:, :, :], cen2[1 - s][:, :, :], ALU.mult)\
                        .then_inc(sq2_done, 1)
                if has(i + 3):
                    pool.wait_ge(cen_done, i + 4)
                    nc.gpsimd.tensor_tensor(sq[:, :, :], cen[1 - s][:, :, :], cen[1 - s][:, :, :], ALU.mult).then_inc(sq_done, 1)
                    pool.wait_ge(rstd_done, i + 4)
                    nc.gpsimd.tensor_tensor(xn[1 - s][:, :, :], cen[1 - s][:, :, :], bc(rstd[1 - s][:, :], 2, C), ALU.mult)\
                        .then_inc(xn_done, 1)

            schedule(pool, step)



def mlp(nc, d, block, room, psum, stored, emptied):
    REST = HID0 - P
    with ExitStack() as ctx:
        used = [0]

        def sb(name, shape):
            size = int(np.prod(shape[1:]))
            at, used[0] = used[0], used[0] + size
            t = room[0:shape[0], at:at + size]
            if len(shape) == 2:
                return t
            axes = "abc"[:len(shape) - 1]
            return t.rearrange(f"q ({' '.join(axes)}) -> q {' '.join(axes)}", **dict(zip(axes, shape[1:])))

        sem = lambda n: ctx.enter_context(nc.semaphore(n))
        ident = sb("ident2", [P, P])
        fc1, bias_row = sb("fc1", [C, HID0]), sb("bias_row", [1, HID0])
        g, b = sb("g2", [C, 1]), sb("b2", [C, 1])
        w1 = sb("w1", [P, HID0])
        w2 = sb("w2", [P, NT])
        w2r = [sb(f"w2r{k}", [P, NT]) for k in range(2)]
        b1, b1r = sb("b1", [P, 1]), sb("b1r", [P, 1])
        b2c = sb("b2c", [P, 1])
        mid = [sb(f"midb{s}", [P, 2, PAIRS, MID]) for s in range(2)]
        lnT = [sb(f"lnT{s}", [P, 2, TOK]) for s in range(2)]
        xT = [sb(f"xT{s}", [P, TOK]) for s in range(2)]
        hid = [sb(f"hid{s}", [P, 3, TOK]) for s in range(2)]
        y = [sb(f"y{s}", [P, WS, GW + 2]) for s in range(2)]
        assert used[0] <= PATCHES * CH
        ps_t, ps_h, ps_y = psum[:, 0:2, :], psum[:, 2:5, :], psum[:, 5:7, :]
        fixed, w_loaded, w_bias, w_ready = sem("m_fixed"), sem("m_loaded"), sem("m_bias"), sem("m_ready")
        loaded = [sem(f"mid_loaded{s}") for s in range(2)]
        gelu_done, y_done = emptied
        turned, ln_copied, x_copied, hid_ready, y_ready = (
            sem(n) for n in ("m_turned", "m_ln_copied", "m_x_copied", "m_hid_ready", "m_y_ready"))

        def has(j):
            return not isinstance(j, int) or 0 <= j < STRIPS

        def schedule(eng, step):
            for j in range(-1, 4):
                step(j, j % 2)
            with eng.Fori(4, STRIPS - 5, 2) as j:
                step(j, 0)
                step(j + 1, 1)
            for j in range(STRIPS - 4, STRIPS + 1):
                step(j, j % 2)

        @block.sync
        def _(sp):
            for s in range(2):
                sp.dma_start(mid[s][:, :, :, :].rearrange("q k p e -> q k (p e)"), d["mid_strips"][s])\
                    .then_inc(loaded[s], 16)
            sp.wait_ge(fixed, 1)
            for dst, src in ((ident[:, :], d["ident"]), (fc1[:, :], d["fc1_wT"]), (g[:, :], d["n2_g"]), (b[:, :], d["n2_b"]),
                             (w2[:, 0:C], d["fc2_wT"][0:P, :]), (w2r[0][0:REST, 0:C], d["fc2_wT"][P:HID0, :]),
                             (w2r[1][REST:P, 0:C], d["fc2_wT"][P:HID0, :]), (b1[:, :], d["fc1_b"][0:P, :]),
                             (b1r[0:REST, :], d["fc1_b"][P:HID0, :]), (b1r[REST:P, :], d["fc1_b"][P:HID0, :]),
                             (b2c[0:C, :], d["fc2_b"]), (b2c[ONE:ONE + C, :], d["fc2_b"])):
                sp.dma_start(dst, src).then_inc(w_loaded, 16)

            def load(j, s):
                if has(j):
                    wait(sp, turned, j - 1)
                    sp.dma_start(mid[s][:, :, :, :].rearrange("q k p e -> q k (p e)"),
                                 d["mid_strips"][j]).then_inc(loaded[s], 16)

            def step(j, s):
                load(j + 3, 1 - s)
                if has(j - 1):
                    sp.wait_ge(y_done, j)
                    for k in range(2):
                        x0 = (GW + 1) * k
                        sp.dma_start(d["img_strips"][:, j - 1, :, x0:x0 + GW + 1], y[1 - s][64 * k:64 * k + C, :, k:k + GW + 1])\
                            .then_inc(stored[1 - s], 16)

            schedule(sp, step)

        @block.tensor
        def _(pe):
            pe.wait_ge(w_loaded, 16 * 12)
            nc.tensor.matmul(ps_y[0:1, 0, 0:HID0], b[:, :], fc1[:, :], start=True, stop=True).then_inc(w_bias, 1)
            pe.wait_ge(w_ready, 3)

            def step(j, s):
                if has(j + 1):
                    pe.wait_ge(loaded[1 - s], 8 * (j + 1 - (1 - s)) + 16)
                    wait(pe, ln_copied, j + 1)
                    wait(pe, x_copied, j + 1)
                    for k in range(2):
                        for p in range(PAIRS):
                            mm = nc.tensor.transpose(ps_t[0:MID, k, P * p:P * p + P], mid[1 - s][:, k, p, :], ident[:, :])
                    mm.then_inc(turned, 1)
                if has(j - 1):
                    pe.wait_ge(gelu_done, 3 * j)
                    wait(pe, y_done, j - 2)
                    for half in range(2):
                        for k in range(2):
                            mm = nc.tensor.matmul(ps_y[64 * k:64 * k + 64, 1 - s, :], w2r[k][:, :] if half else w2[:, :],
                                                  hid[1 - s][:, 2 if half else k, :], start=(half == 0), stop=(half == 1))
                    mm.then_inc(y_ready, 1)
                if has(j):
                    pe.wait_ge(ln_copied, j + 1)
                    for k in range(2):
                        wait(pe, gelu_done, 3 * j - 2 + k)
                        nc.tensor.matmul(ps_h[:, k, :], w1[:, 0:P], lnT[s][:, k, :], start=True, stop=True)\
                            .then_inc(hid_ready, 1)
                    wait(pe, gelu_done, 3 * j)
                    for k in range(2):
                        mm = nc.tensor.matmul(ps_h[REST * k:REST * k + REST, 2, :], w1[:, P:HID0], lnT[s][:, k, :],
                                              start=True, stop=True)
                    mm.then_inc(hid_ready, 1)

            schedule(pe, step)

        @block.vector
        def _(dve):
            for t in (w1, w2, w2r[0], w2r[1]):
                nc.vector.memset(t[...], 0.0)
            nc.vector.memset(b2c[:, :], 0.0).then_inc(fixed, 1)
            for t in (lnT[0], lnT[1], xT[0], xT[1], y[0], y[1]):
                last = nc.vector.memset(t[...], 0.0)
            last.then_inc(w_ready, 1)
            dve.wait_ge(w_ready, 1)
            for s in range(2):
                nc.vector.memset(lnT[s][ONE:ONE + 1, :, :], 1.0)
            dve.wait_ge(w_loaded, 16 * 12)
            dve.wait_ge(w_bias, 1)
            nc.vector.tensor_copy(bias_row[:, :], ps_y[0:1, 0, 0:HID0]).then_inc(w_ready, 1)
            nc.vector.tensor_scalar(w1[0:C, :], fc1[:, :], g[:, 0:1], None, ALU.mult)
            dve.wait_ge(w_ready, 2)
            nc.vector.tensor_copy(w1[ONE:ONE + 1, :], bias_row[:, :]).then_inc(w_ready, 1)

            def step(j, s):
                if has(j - 1):
                    dve.wait_ge(x_copied, j)
                    dve.wait_ge(y_ready, j)
                    wait(dve, stored[1 - s], 16 * (j - 1 - (1 - s)))
                    px = lambda ap: ap.rearrange("q (n r c) -> q n r c", r=WS, c=WS)
                    nc.vector.tensor_tensor(y[1 - s][:, :, 1:GW + 1].rearrange("q r (n c) -> q n r c", c=WS),
                                            px(ps_y[:, 1 - s, :]), px(xT[1 - s][:, :]), ALU.add).then_inc(y_done, 1)
                if has(j + 1):
                    wait(dve, y_done, j)
                    dve.wait_ge(turned, j + 2)
                    for k in range(2):
                        r = slice(64 * k, 64 * k + C)
                        last = nc.vector.tensor_scalar(xT[1 - s][r, :], ps_t[ONE:ONE + C, k, :], b2c[r, 0:1], None, ALU.add)
                    last.then_inc(x_copied, 1)

            schedule(dve, step)

        @block.scalar
        def _(act):
            act.wait_ge(w_ready, 3)

            def step(j, s):
                if has(j + 1):
                    act.wait_ge(turned, j + 2)
                    nc.scalar.activation(lnT[1 - s][0:C, :, :].rearrange("q k t -> q (k t)"),
                                         ps_t[0:C, :, :].rearrange("q k t -> q (k t)"), ACT.Copy).then_inc(ln_copied, 1)
                if has(j):
                    for k in range(3):
                        act.wait_ge(hid_ready, 3 * j + k + 1)
                        nc.scalar.activation(hid[s][:, k, :], ps_h[:, k, :], ACT.Gelu,
                                             bias=(b1r if k == 2 else b1)[:, 0:1]).then_inc(gelu_done, 1)

            schedule(act, step)


def conv(nc, d):
    with ExitStack() as ctx:
        sb = lambda n, s: ctx.enter_context(nc.sbuf_tensor(n, s, F32))
        sem = lambda n: ctx.enter_context(nc.semaphore(n))
        ident = sb("ident3", [P, P])
        eps = sb("eps3", [P, 1])
        w1 = sb("ew", [P, CHUNKS, CH])
        w2 = sb("pw", [P, CHUNKS, NT])
        q = {n: sb(f"q_{n}", [CH, C]) for n in "gvt"}
        c2 = {n: sb(f"c_{n}", [P, 1]) for n in "gbmvt"}
        SLOTS = 5
        PART = 4
        piece = [sb(f"piece{s}", [C, PH + 2, SC]) for s in range(SLOTS)]
        xp = sb("xp", [P, PATCHES, PIN])
        h1 = sb("h1", [P, CH, PATCHES])
        e = {n: h1[0:C, CHUNKS * j:CHUNKS * (j + 1), 0:CH] for j, n in enumerate("gbmvt")}
        room = sb("room", [P, PATCHES * CH])
        h2 = room[0:POUT, :].rearrange("q (p c) -> q p c", c=CH)
        mats = [sb(f"mats{s}", [P, TCH, POUT]) for s in range(LOADS)]
        h2T = [sb(f"h2T{s}", [P, 2, PART * POUT]) for s in range(2)]
        y = sb("yc", [P, PR * PH, PC // 2 * PW])
        psum = ctx.enter_context(nc.psum_tensor("psum2", [P, 8, 512], F32))
        ring = [psum[:, s, :] for s in range(4)]
        ps_t = [psum[:, 4 + k, :] for k in range(2)]
        ps_y = [psum[:, 6 + s, :] for s in range(2)]
        fixed, w_loaded, root, w_ready = sem("c_fixed"), sem("c_loaded"), sem("c_root"), sem("c_ready")
        piece_loaded, first_loaded = [sem(f"piece_loaded{s}") for s in range(SLOTS)], sem("first_loaded")
        cut, ones_set = sem("cut"), sem("ones_set")
        mats_loaded = [sem(f"mats_loaded{s}") for s in range(LOADS)]
        unit_ready, unit_act, unit_dve = sem("unit_ready"), sem("unit_act"), sem("unit_dve")
        turned, copied = sem("c_turned"), sem("c_copied")
        y_ready, y_done, y_stored = sem("c_y_ready"), sem("c_y_done"), sem("c_y_stored")
        img_stored = [sem(f"img_stored{s}") for s in range(2)]
        mlp_gelu, mlp_done = sem("gelu_done"), sem("m_y_done")

        STEPS = [(pc, a, PART) for pc in range(PC // 2) for a in range(0, PR, PART)]
        NSTEP = len(STEPS)

        def schedule(eng, first, chunk):
            first()
            with eng.Fori(0, HALVES // 2 - 1, 1) as b:
                for hx in range(2):
                    for c in range(CHUNKS):
                        chunk(b, hx, c, False)
            for hx in range(2):
                for c in range(CHUNKS):
                    chunk(HALVES // 2 - 1, hx, c, hx == 1 and c == CHUNKS - 1)

        CUT = CHUNKS - 2

        def more(b, hx):
            return not (hx == 1 and isinstance(b, int))

        FIXED = 2 + 5 + 2 + SLOTS + 1 + LOADS + 3

        slot_of = [0] + [1 + j % (SLOTS - 2) for j in range(1, PR - 1)] + [SLOTS - 1]
        PER_HALF = [slot_of.count(s) for s in range(SLOTS)]

        def nth_in_slot(j):
            return slot_of[:j].count(slot_of[j])

        def place_of(j):
            s = slot_of[j]
            before = [i for i in range(j) if slot_of[i] == s]
            return s, before[-1] + 1 if before else max(i for i in range(PR) if slot_of[i] == s) + 1 - PR

        def number(b, hx, c):
            return 2 * CHUNKS * b + CHUNKS * hx + c

        def before_expand(k):
            return (EXPANDS + DEPTHS) // 2 * k

        def before_depthwise(k):
            return (EXPANDS + DEPTHS) // 2 * k + EXPANDS // 2

        def evacuate(activation, j, expand):
            bank = ring[j % 4]
            if expand:
                dst = h1[0:PIN, :, 4 * j:4 * j + 4].rearrange("q c p -> q p c")
                src = bank[0:PIN, 0:4 * CH].rearrange("q (p c) -> q p c", c=CH)
            else:
                dst = h2[:, :, 4 * j:4 * j + 4].rearrange("q p c -> q c p")
                src = bank[POUT * (j % 2):POUT * (j % 2) + POUT, 0:4 * PATCHES].rearrange("q (c p) -> q c p", c=4)
            if activation:
                return nc.scalar.activation(dst, src, ACT.Relu)
            return nc.vector.tensor_scalar(dst, src, 0.0, None, ALU.max)

        block = ctx.enter_context(nc.Block(name="mlp_conv"))

        def cut_piece(copy, j):
            slot, _ = place_of(j)
            src = piece[slot][:, :, :]
            src = bass.AP(src.tensor, src.offset, [list(src.ap[0]), [PW, PC], [SC, PH + 2], [1, PW + 2]])
            dst = xp[0:C, :, :].rearrange("k (c j) (r x) -> k j c r x", j=PR, x=PW + 2)[:, j]
            copy(dst, src).then_inc(cut, 1)

        def place_ones(eng, memset, hx, h):
            ones = xp[ONE:ONE + 1, :, :].rearrange("k (c j) (r x) -> k c j r x", j=PR, x=PW + 2)
            for pc, x, out in ((0, 0, hx == 0), (PC - 1, PW + 1, hx == 1)):
                last = memset(ones[:, pc, :, :, x], 0.0 if out else 1.0)
            last.then_inc(ones_set, 1)
            eng.wait_ge(ones_set, 2 * h + 1)
            memset(ones[:, :, 0, 0, :], 0.0)
            memset(ones[:, :, PR - 1, H - PH * (PR - 1) + 1:, :], 0.0).then_inc(ones_set, 1)

        def piece_rows(j):
            lo, hi = max(PH * j - 1, 0), min(PH * j + PH + 1, H)
            return lo, hi, lo - (PH * j - 1)

        @block.gpsimd
        def _(pool):
            constants = [(t[...], 0.0) for t in (w1, w2, *c2.values(), *h2T, *piece, xp)]
            constants += [(t[96:P, :, :], 0.0) for t in mats]
            constants += [(h1[96:P, :, :], 1.0), (eps[:, :], EPS), (xp[ONE:ONE + 1, :, :], 1.0)]
            assert len(constants) == FIXED
            for n, (t, value) in enumerate(constants):
                nc.gpsimd.memset(t, value).then_inc(fixed, 1)
                pool.wait_ge(fixed, n + 1)
            loads = [(ident[:, :], d["ident"]), (w1[0:C, :, :], d["w1T"])]
            loads += [(e[n], d[f"bn1_{n}"].partition_broadcast(C)) for n in "gbmv"]
            loads += [(w2[0:CH, k, 0:C], d["w2T"][CH * k:CH * k + CH, :]) for k in range(CHUNKS)]
            loads += [(q[n][:, :], d[f"bn2_{n}"].partition_broadcast(CH)) for n in "gv"]
            loads += [(c2[n][r:r + C, :], d[f"bn2_{n}"].rearrange("(c a) -> c a", a=1)) for n in "gbmv" for r in (0, ONE)]
            assert len(loads) == 19
            for dst, src in loads:
                pool.dma_start(dst, src).then_inc(w_loaded, 16)
            nc.gpsimd.memset(y[:, :, :], 0.0).then_inc(y_stored, 32)
            pool.wait_ge(y_stored, 32)
            for s in range(2):
                pool.wait_ge(img_stored[s], 32 * (H // WS // 2))
            for j in range(PR):
                slot, nth = place_of(j)
                wait(pool, cut, nth)
                lo, hi, off = piece_rows(j)
                pool.dma_start(piece[slot][:, off:off + hi - lo, :], d["img_images"][:, 0, lo:hi, 0:SC])\
                    .then_inc(first_loaded, 16)
                pool.wait_ge(first_loaded, 16 * (j + 1))
                cut_piece(nc.gpsimd.tensor_copy, j)
            place_ones(pool, nc.gpsimd.memset, 0, 0)

        mlp(nc, d, block, room, psum, img_stored, (mlp_gelu, mlp_done))

        @block.sync
        def _(sp):
            sp.wait_ge(fixed, FIXED)
            for s in range(LOADS):
                sp.dma_start(mats[s][0:PIN + 1, :, :], d["conv_mats"][s]).then_inc(mats_loaded[s], 16)
            for s in range(2):
                sp.wait_ge(img_stored[s], 32 * (STRIPS // 2))

            def load_half(b, hx, h):
                for j in range(PR):
                    slot, nth = place_of(j)
                    wait(sp, cut, PR * h + nth)
                    lo, hi, off = piece_rows(j)
                    sp.dma_start(piece[slot][:, off:off + hi - lo, :],
                                 d["img_images"][:, b, lo:hi, HALF * hx:HALF * hx + SC]).then_inc(piece_loaded[slot], 16)

            def chunk(b, hx, c, last):
                k = number(b, hx, c)
                if not last:
                    for s in range(LOADS):
                        sp.wait_ge(unit_ready, 2 * before_depthwise(k) + DEPTHS // LOADS * (s + 1))
                        sp.dma_start(mats[s][0:PIN + 1, :, :], d["conv_mats"][LOADS * ((c + 1) % CHUNKS) + s])\
                            .then_inc(mats_loaded[s], 16)
                if c == CUT and more(b, hx):
                    load_half(b + hx, 1 - hx, 2 * b + hx + 1)
                if c == CHUNKS - 1:
                    sp.wait_ge(y_done, NSTEP * (k + 1))
                    for r in range(2):
                        sp.dma_start(d["out"][4 * b + 2 * hx + r], y[64 * r:64 * r + C, 0:H, :].rearrange("c y x -> c (y x)"))\
                            .then_inc(y_stored, 16)

            schedule(sp, lambda: None, chunk)
            sp.wait_ge(y_stored, 32 * HALVES + 32)

        @block.tensor
        def _(pe):
            pe.wait_ge(w_ready, 5)

            def bank_free(before, j):
                wait(pe, unit_dve if j % 2 else unit_act, before + (j - 4) // 2 + 1)

            def emptied(before):
                pe.wait_ge(unit_act, before)
                pe.wait_ge(unit_dve, before)

            def expand(k, c):
                for j in range(EXPANDS):
                    bank_free(before_expand(k), j)
                    for p in range(4):
                        mm = nc.tensor.matmul(ring[j % 4][0:PIN, CH * p:CH * p + CH], xp[:, 4 * j + p, :], w1[:, c, :],
                                              start=True, stop=True)
                    mm.then_inc(unit_ready, 1)

            def depthwise(k):
                for j in range(0, DEPTHS, 2):
                    if j % (DEPTHS // LOADS) == 0:
                        pe.wait_ge(mats_loaded[j // (DEPTHS // LOADS)], 16 * (k + 1))
                    for u in range(2):
                        bank_free(before_depthwise(k), j + u)
                    for n in range(4):
                        for u in range(2):
                            ch = 4 * (j + u) + n
                            mm = nc.tensor.matmul(ring[(j + u) % 4][POUT * u:POUT * u + POUT, PATCHES * n:PATCHES * (n + 1)],
                                                  mats[ch // TCH][:, ch % TCH, :], h1[:, ch, :], start=True, stop=True)
                            if n == 3:
                                mm.then_inc(unit_ready, 1)

            def first():
                pe.wait_ge(mlp_gelu, 3 * STRIPS)
                pe.wait_ge(mlp_done, STRIPS)
                pe.wait_ge(ones_set, 2)
                expand(0, 0)

            def chunk(b, hx, c, last):
                k = number(b, hx, c)
                emptied(before_depthwise(k))
                depthwise(k)
                if not last:
                    if c == CHUNKS - 1:
                        pe.wait_ge(ones_set, 2 * (2 * b + hx + 2))
                    expand(k + 1, (c + 1) % CHUNKS)
                if last:
                    emptied(before_expand(k + 1))
                for n in range(NSTEP + 1):
                    if n < NSTEP:
                        pc, a, m = STEPS[n]
                        for r in range(2):
                            for p in range(m):
                                patch = PR * (pc + PC // 2 * r) + a + p
                                at = POUT * (m * r + p)
                                mm = nc.tensor.transpose(ps_t[n % 2][0:CH, at:at + POUT], h2[:, patch, :],
                                                         ident[0:POUT, 0:POUT])
                        mm.then_inc(turned, 1)
                    if n >= 1:
                        m = STEPS[n - 1][2]
                        pe.wait_ge(copied, NSTEP * k + n)
                        if n >= 3:
                            pe.wait_ge(y_done, NSTEP * k + n - 2)
                        for r in range(2):
                            mm = nc.tensor.matmul(ps_y[(n - 1) % 2][64 * r:64 * r + 64, 0:POUT * m], w2[:, c, :],
                                                  h2T[(n - 1) % 2][:, r, :], start=True, stop=True)
                        mm.then_inc(y_ready, 1)

            schedule(pe, first, chunk)

        @block.scalar
        def _(act):
            act.wait_ge(w_loaded, 16 * 19)
            nc.scalar.activation(e["t"], e["v"], ACT.Sqrt, bias=eps[0:C, :]).then_inc(root, 1)
            nc.scalar.activation(q["t"][:, :], q["v"][:, :], ACT.Sqrt, bias=eps[0:CH, :]).then_inc(root, 1)
            nc.scalar.activation(c2["t"][:, :], c2["v"][:, :], ACT.Sqrt, bias=eps[:, :]).then_inc(root, 1)

            def units(before, expand):
                for j in range(0, EXPANDS if expand else DEPTHS, 2):
                    act.wait_ge(unit_ready, 2 * before + j + 1)
                    evacuate(True, j, expand).then_inc(unit_act, 1)

            def chunk(b, hx, c, last):
                k = number(b, hx, c)
                units(before_depthwise(k), False)
                if not last:
                    units(before_expand(k + 1), True)
                for n in range(NSTEP):
                    m = STEPS[n][2]
                    act.wait_ge(turned, NSTEP * k + n + 1)
                    nc.scalar.activation(h2T[n % 2][0:CH, :, :].rearrange("q r t -> q (r t)"), ps_t[n % 2][0:CH, :],
                                         ACT.Copy).then_inc(copied, 1)

            def first():
                units(0, True)
                for s in range(2):
                    act.wait_ge(img_stored[s], 32 * (STRIPS // 2))

            schedule(act, first, chunk)

        @block.vector
        def _(dve):
            dve.wait_ge(root, 3)
            for t in (e, q, c2):
                last = nc.vector.reciprocal(t["v"][...], t["t"][...])
            last.then_inc(w_ready, 1)
            dve.wait_ge(w_ready, 1)
            for t in (e, q, c2):
                last = nc.vector.tensor_tensor(t["t"][...], t["v"][...], t["g"][...], ALU.mult)
            last.then_inc(w_ready, 1)
            dve.wait_ge(w_ready, 2)
            for t in (e, c2):
                nc.vector.tensor_tensor(t["m"][...], t["m"][...], t["t"][...], ALU.mult)
            nc.vector.tensor_tensor(w1[0:C, :, :], w1[0:C, :, :], e["t"], ALU.mult)
            nc.vector.tensor_tensor(w2[0:CH, :, 0:C], w2[0:CH, :, 0:C], bc(q["t"][:, :], 1, CHUNKS), ALU.mult)\
                .then_inc(w_ready, 1)
            dve.wait_ge(w_ready, 3)
            for t in (e, c2):
                last = nc.vector.tensor_tensor(t["b"][...], t["b"][...], t["m"][...], ALU.subtract)
            last.then_inc(w_ready, 1)
            dve.wait_ge(w_ready, 4)
            nc.vector.tensor_copy(w1[ONE:ONE + 1, :, :], h1[0:1, CHUNKS:2 * CHUNKS, 0:CH]).then_inc(w_ready, 1)

            def next_piece(j, h):
                slot, _ = place_of(j)
                dve.wait_ge(piece_loaded[slot], 16 * (PER_HALF[slot] * (h - 1) + nth_in_slot(j) + 1))
                cut_piece(nc.vector.tensor_copy, j)

            def units(before, expand):
                for j in range(1, EXPANDS if expand else DEPTHS, 2):
                    dve.wait_ge(unit_ready, 2 * before + j + 1)
                    evacuate(False, j, expand).then_inc(unit_dve, 1)

            def add(n, b, hx, c, k):
                pc, a, m = STEPS[n]
                dve.wait_ge(y_ready, NSTEP * k + n + 1)
                rows = slice(PH * a, PH * (a + m))
                cols = slice(PW * pc, PW * pc + PW)
                dst = y[:, rows, cols]
                src = ps_y[n % 2][:, 0:POUT * m].rearrange("q (r x) -> q r x", x=PW)
                if c == 0:
                    if n == 0:
                        dve.wait_ge(y_stored, 32 * (2 * b + hx) + 32)
                    for r in range(2):
                        t = slice(64 * r, 64 * r + C)
                        p0 = PR * (pc + PC // 2 * r) + a
                        x = xp[0:C, p0:p0 + m, :].rearrange("k j (r x) -> k j r x", x=PW + 2)[:, :, 1:PH + 1, 1:PW + 1]
                        last = nc.vector.tensor_tensor(
                            y[t, rows, cols].rearrange("q (j r) x -> q j r x", j=m),
                            ps_y[n % 2][t, 0:POUT * m].rearrange("q (j r x) -> q j r x", j=m, x=PW), x, ALU.add)
                    last.then_inc(y_done, 1)
                elif c == CHUNKS - 1:
                    nc.vector.scalar_tensor_tensor(dst, src, c2["b"][:, 0:1], dst, ALU.add, ALU.add).then_inc(y_done, 1)
                else:
                    nc.vector.tensor_tensor(dst, src, dst, ALU.add).then_inc(y_done, 1)

            def chunk(b, hx, c, last):
                k = number(b, hx, c)
                units(before_depthwise(k), False)
                if not last:
                    units(before_expand(k + 1), True)
                cutting = c == CUT and more(b, hx)
                for n in range(NSTEP + 1):
                    if n >= 1:
                        add(n - 1, b, hx, c, k)
                    if cutting and n < PR:
                        next_piece(n, 2 * b + hx + 1)
                if cutting:
                    place_ones(dve, nc.vector.memset, 1 - hx, 2 * b + hx + 1)

            def first():
                units(0, True)
                for s in range(2):
                    dve.wait_ge(img_stored[s], 32 * (STRIPS // 2))

            assert NSTEP >= PR
            schedule(dve, first, chunk)


def block_program(nc, d):
    d["mid_strips"] = d["tok_mid"].rearrange("(j k) q e -> j q k e", k=2)
    d["tok_mid"] = d["tok_mid"].rearrange("g q (p e) -> g q p e", e=MID)
    d["img_strips"] = d["img_mid"].rearrange("c (j r) x -> c j r x", r=WS)
    d["img_images"] = d["img_mid"].rearrange("c (b y) x -> c b y x", b=B)
    attention(nc, d)
    conv(nc, d)


def tap_places():
    places = np.zeros((TAPROW + 1, POUT, P), np.float32)
    for r in range(PH):
        for c in range(PW):
            for t in range(9):
                places[t, r * PW + c, (r + t // 3) * (PW + 2) + c + t % 3] = 1
    places[TAPROW, :, PIN] = 1
    return places


def head_mask():
    mask = np.zeros((P, NH), np.float32)
    for h in range(NH):
        mask[ONE + HD * h:ONE + HD * (h + 1), h] = 1
    return mask


def kernel(**inputs):
    from concourse.bacc import Bacc
    from concourse.bass_utils import run_bass_kernel_spmd

    L0 = lambda n: np.asarray(inputs["L0_conv_" + n])
    L1 = lambda n: np.asarray(inputs["L1_conv_" + n])
    x = np.asarray(inputs["x"])
    groups = x.reshape(B, C, H // WS, WS, W // GW, GW // WS, WS).transpose(0, 2, 4, 1, 5, 3, 6)
    arrays = {
        "x_groups": groups.reshape(GROUPS, C, TOK),
        "n1_g": L0("norm1_g").reshape(C, 1), "n1_b": L0("norm1_b").reshape(C, 1),
        "qkv_wT": L0("qkv_w").T, "qkv_b": L0("qkv_b").reshape(1, 3 * C),
        "table": L0("rpb_table"), "rel_idx": L0("rel_idx").reshape(NT * NT),
        "proj_wT": L0("proj_w").T, "proj_b": L0("proj_b").reshape(1, C),
        "n2_g": L0("norm2_g").reshape(C, 1), "n2_b": L0("norm2_b").reshape(C, 1),
        "fc1_wT": L0("fc1_w").T, "fc1_b": L0("fc1_b").reshape(HID0, 1),
        "fc2_wT": L0("fc2_w").T, "fc2_b": L0("fc2_b").reshape(C, 1),
        "w1T": L1("w1").T, "wd": L1("wd").reshape(HID1, 9).T, "w2T": L1("w2").T,
        "ident": np.eye(P, dtype=np.float32), "headmask": head_mask(), "places": tap_places(),
        "number": np.arange(2 * P, dtype=np.float32).reshape(2, P).T,
    }
    for k, bn in (("1", "bn1"), ("2", "bn2")):
        for n in "gbmv":
            arrays[f"{bn}_{n}"] = L1(n + k)
    for n in ("gd", "bd", "md", "vd"):
        arrays[n] = L1(n)
    arrays = {f"in_{n}": np.ascontiguousarray(a) for n, a in arrays.items()}

    nc = Bacc("TRN2", target_bir_lowering=False, num_devices=1)
    d = {n[3:]: nc.dram_tensor(n, a.shape, mybir.dt.from_np(a.dtype), kind="ExternalInput").ap() for n, a in arrays.items()}
    halves = (B, W // HALF, 2, C, H, HALF // 2)
    for n, shape in (("conv_mats", (HID1 // TCH, PIN + 1, TCH, POUT)), ("rel_bias", (NH, NT * NT)),
                     ("tok_mid", (GROUPS, P, PAIRS * MID)), ("img_mid", (C, B * H, W + 2))):
        d[n] = nc.dram_tensor(n, shape, F32, kind="Internal").ap()
    d["out"] = nc.dram_tensor("out", (B * 4, C, H * HALF // 2), F32, kind="ExternalOutput").ap()
    block_program(nc, d)
    got = run_bass_kernel_spmd(nc, [arrays], core_ids=[0]).results[0]["out"]
    return got.reshape(halves).transpose(0, 3, 4, 1, 2, 5).reshape(B, C, H, W)
```
